# Optimizing a Trainium2 kernel written in Bass

```python
import numpy as np
import jax
import jax.numpy as jnp

def _softmax(x, axis=-1):
    return jax.nn.softmax(x, axis=axis)

def _gelu(x):
    return jax.nn.gelu(x, approximate=True)

def _silu(x):
    return jax.nn.silu(x)

def _sigmoid(x):
    return jax.nn.sigmoid(x)

def _layernorm(x, axis=-1, eps=1e-05):
    m = jnp.mean(x, axis=axis, keepdims=True)
    v = jnp.var(x, axis=axis, keepdims=True)
    return (x - m) / jnp.sqrt(v + eps)

def _scatter_add(tgt, idx, src, axis=0):
    return tgt.at[idx].add(src)

def _segment_sum(src, seg, n):
    return jax.ops.segment_sum(src, seg, n)
kernel_name = 'mk_prb_d1_jaxref_r8_18aa20'

def setup_inputs(seed: int=0):
    np.random.seed(seed)
    _w = jnp.asarray

    def _L0_attn_setup():
        import jax, jax.numpy as jnp
        import numpy as np
        B, T, C = (4, 128, 256)
        H, DN, DR = (16, 128, 64)
        D = DN + DR
        Q_RANK, KV_RANK = (192, 64)
        ROPE_BASE = 10000.0

        def rope_cos_sin(seq_len, dim, dtype=jnp.float32):
            inv_freq = 1.0 / ROPE_BASE ** (jnp.arange(0, dim, 2, dtype=jnp.float32) / dim)
            t = jnp.arange(seq_len, dtype=jnp.float32)
            freqs = jnp.outer(t, inv_freq)
            return (jnp.cos(freqs).astype(dtype), jnp.sin(freqs).astype(dtype))

        def apply_rope(x, cos, sin):
            x1 = x[..., 0::2]
            x2 = x[..., 1::2]
            c = cos[None, :, None, :]
            s = sin[None, :, None, :]
            o1 = x1 * c - x2 * s
            o2 = x1 * s + x2 * c
            return jnp.stack([o1, o2], axis=-1).reshape(x.shape)
        key = jax.random.key(seed)
        ks = jax.random.split(key, 9)

        def g(k, shape, scale):
            return jax.random.normal(k, shape, dtype=jnp.float32) * scale
        return {'x': g(ks[0], (B, T, C), 1.0), 'wq_down': g(ks[1], (C, Q_RANK), C ** (-0.5)), 'wq_nope': g(ks[2], (Q_RANK, H * DN), Q_RANK ** (-0.5)), 'wq_rope': g(ks[3], (Q_RANK, H * DR), Q_RANK ** (-0.5)), 'wkv_down': g(ks[4], (C, KV_RANK), C ** (-0.5)), 'wv_up': g(ks[5], (KV_RANK, H * D), KV_RANK ** (-0.5)), 'wk_nope': g(ks[6], (KV_RANK, H * DN), KV_RANK ** (-0.5)), 'wk_rope': g(ks[7], (KV_RANK, H * DR), KV_RANK ** (-0.5)), 'wo': g(ks[8], (H * D, C), (H * D) ** (-0.5))}
    _L0_attn_in = _L0_attn_setup()

    def _L0_ffn_setup():
        import jax, jax.numpy as jnp
        import numpy as np
        TOP_K = 8

        def _masked_routing(router_logits):
            T, E = router_logits.shape
            sel_w, sel_e = jax.lax.top_k(router_logits, TOP_K)
            sel_w = jax.nn.softmax(sel_w.astype(jnp.float32), axis=1)
            rows = jnp.arange(T)[:, None]
            masked = jnp.zeros((T, E), dtype=jnp.float32).at[rows, sel_e].set(sel_w)
            count = jnp.zeros((E,), dtype=jnp.int32).at[sel_e.reshape(-1)].add(1)
            return (masked, count)
        key = jax.random.key(seed)
        k1, k2, k3, k4, k5 = jax.random.split(key, 5)
        B, S, H, E, I = (1, 256, 256, 32, 96)
        return {'hidden_states': jax.random.normal(k1, (B, S, H), dtype=jnp.float32), 'gate_w': jax.random.normal(k2, (E, H), dtype=jnp.float32) * H ** (-0.5), 'w_gate_proj': jax.random.normal(k3, (E, I, H), dtype=jnp.float32) * H ** (-0.5), 'w_up_proj': jax.random.normal(k4, (E, I, H), dtype=jnp.float32) * H ** (-0.5), 'w_down_proj': jax.random.normal(k5, (E, H, I), dtype=jnp.float32) * I ** (-0.5)}
    _L0_ffn_in = _L0_ffn_setup()
    _d = {'L0_attn_x': _L0_attn_in['x'], 'L0_attn_wq_down': _L0_attn_in['wq_down'], 'L0_attn_wq_nope': _L0_attn_in['wq_nope'], 'L0_attn_wq_rope': _L0_attn_in['wq_rope'], 'L0_attn_wkv_down': _L0_attn_in['wkv_down'], 'L0_attn_wv_up': _L0_attn_in['wv_up'], 'L0_attn_wk_nope': _L0_attn_in['wk_nope'], 'L0_attn_wk_rope': _L0_attn_in['wk_rope'], 'L0_attn_wo': _L0_attn_in['wo'], 'L0_ffn_gate_w': _L0_ffn_in['gate_w'], 'L0_ffn_w_gate_proj': _L0_ffn_in['w_gate_proj'], 'L0_ffn_w_up_proj': _L0_ffn_in['w_up_proj'], 'L0_ffn_w_down_proj': _L0_ffn_in['w_down_proj']}
    _x0 = _d['L0_attn_x']
    _d['L0_attn_x'] = jax.random.normal(jax.random.fold_in(jax.random.key(seed), 1), (2, 1024, 256), dtype=_x0.dtype)
    del _x0
    return _d

def reference(L0_attn_x, L0_attn_wq_down, L0_attn_wq_nope, L0_attn_wq_rope, L0_attn_wkv_down, L0_attn_wv_up, L0_attn_wk_nope, L0_attn_wk_rope, L0_attn_wo, L0_ffn_gate_w, L0_ffn_w_gate_proj, L0_ffn_w_up_proj, L0_ffn_w_down_proj):

    def _L0_attn_ref(x, wq_down, wq_nope, wq_rope, wkv_down, wv_up, wk_nope, wk_rope, wo):
        import jax, jax.numpy as jnp
        import numpy as np
        B, T, C = (4, 128, 256)
        H, DN, DR = (16, 128, 64)
        D = DN + DR
        Q_RANK, KV_RANK = (192, 64)
        ROPE_BASE = 10000.0

        def rope_cos_sin(seq_len, dim, dtype=jnp.float32):
            inv_freq = 1.0 / ROPE_BASE ** (jnp.arange(0, dim, 2, dtype=jnp.float32) / dim)
            t = jnp.arange(seq_len, dtype=jnp.float32)
            freqs = jnp.outer(t, inv_freq)
            return (jnp.cos(freqs).astype(dtype), jnp.sin(freqs).astype(dtype))

        def apply_rope(x, cos, sin):
            x1 = x[..., 0::2]
            x2 = x[..., 1::2]
            c = cos[None, :, None, :]
            s = sin[None, :, None, :]
            o1 = x1 * c - x2 * s
            o2 = x1 * s + x2 * c
            return jnp.stack([o1, o2], axis=-1).reshape(x.shape)
        b, t, c = x.shape
        q_latent = x @ wq_down
        kv_latent = x @ wkv_down
        q_c = (q_latent @ wq_nope).reshape(b, t, H, DN)
        q_r = (q_latent @ wq_rope).reshape(b, t, H, DR)
        v = (kv_latent @ wv_up).reshape(b, t, H, D)
        k_c = (kv_latent @ wk_nope).reshape(b, t, H, DN)
        k_r = (kv_latent @ wk_rope).reshape(b, t, H, DR)
        cos, sin = rope_cos_sin(t, DR, x.dtype)
        q_r = apply_rope(q_r, cos, sin)
        k_r = apply_rope(k_r, cos, sin)
        q = jnp.concatenate([q_c, q_r], axis=-1)
        k = jnp.concatenate([k_c, k_r], axis=-1)
        scale = 1.0 / D ** 0.5
        scores = jnp.einsum('bthd,bshd->bhts', q, k) * scale
        causal = jnp.tril(jnp.ones((t, t), dtype=bool))
        scores = jnp.where(causal[None, None], scores, jnp.finfo(scores.dtype).min)
        probs = jax.nn.softmax(scores, axis=-1)
        out = jnp.einsum('bhts,bshd->bthd', probs, v).reshape(b, t, H * D)
        return out @ wo

    def _L0_ffn_ref(hidden_states, gate_w, w_gate_proj, w_up_proj, w_down_proj):
        import jax, jax.numpy as jnp
        import numpy as np
        TOP_K = 8

        def _masked_routing(router_logits):
            T, E = router_logits.shape
            sel_w, sel_e = jax.lax.top_k(router_logits, TOP_K)
            sel_w = jax.nn.softmax(sel_w.astype(jnp.float32), axis=1)
            rows = jnp.arange(T)[:, None]
            masked = jnp.zeros((T, E), dtype=jnp.float32).at[rows, sel_e].set(sel_w)
            count = jnp.zeros((E,), dtype=jnp.int32).at[sel_e.reshape(-1)].add(1)
            return (masked, count)
        B, S, H = hidden_states.shape
        x = hidden_states.reshape(-1, H)
        router_logits = x @ gate_w.T
        masked_w, _count = _masked_routing(router_logits)
        g = jnp.einsum('th,eih->tei', x, w_gate_proj)
        u = jnp.einsum('th,eih->tei', x, w_up_proj)
        h = jax.nn.silu(g) * u
        h = h * masked_w[:, :, None]
        out = jnp.einsum('tei,ehi->th', h, w_down_proj)
        return out.reshape(B, S, H)
    x = L0_attn_x
    xn = _layernorm(x, axis=-1)
    x = x + _L0_attn_ref(xn, L0_attn_wq_down, L0_attn_wq_nope, L0_attn_wq_rope, L0_attn_wkv_down, L0_attn_wv_up, L0_attn_wk_nope, L0_attn_wk_rope, L0_attn_wo) + _L0_ffn_ref(xn, L0_ffn_gate_w, L0_ffn_w_gate_proj, L0_ffn_w_up_proj, L0_ffn_w_down_proj)
    return x

_drawn_inputs = setup_inputs


def setup_inputs(seed=0):
    import zlib

    import numpy as np

    out = dict(_drawn_inputs(seed))
    spreads = {}
    factors = {}
    for name, (base, spread) in spreads.items():
        noise = np.random.default_rng([zlib.crc32(name.encode()), seed]).standard_normal(out[name].shape)
        drawn = base * np.exp(spread * noise) if base else spread * noise
        out[name] = jnp.asarray(drawn.astype(out[name].dtype))
    for name, factor in factors.items():
        out[name] = (out[name] * factor).astype(out[name].dtype)
    return out
```

```python
import numpy as np
import concourse.bass as bass
import concourse.mybir as mybir
from contextlib import ExitStack

F32 = mybir.dt.float32
F32R = mybir.dt.float32r
BF16 = mybir.dt.bfloat16
ALU = mybir.AluOpType
ACT = mybir.ActivationFunctionType
AXX = mybir.AxisListType.X

B, T, C = 2, 1024, 256
N = B * T
H, DN, DR = 16, 128, 64
D = DN + DR
QR, KVR = 192, 64
E, I, TOPK = 32, 96, 8
P = 128
NT = N // P
CH = 512
NCH = N // CH
TPC = CH // P
PAIRS = H // 2
SCALE = 1.0 / D ** 0.5
EPS = 1e-5
MASKED = -float(2 ** 120)
IT = E * I // P
PAIRSWAP = [x ^ 1 for x in range(32)]


def ge(engine, semaphore, value):
    if not isinstance(value, int) or value > 0:
        engine.wait_ge(semaphore, value)


def tensors(nc, ctx, specs):
    return [ctx.enter_context(nc.sbuf_tensor(name, shape, dt)) for name, shape, dt in specs]


def prepare(nc, d, keep):
    ctx = ExitStack()
    with ctx:
        x, xn, ident, wl, wkg, stats, mv, var, std, rinv, tmp = tensors(nc, ctx, [
            ("x", [P, NT, C], F32), ("xn", [P, NT, C], F32), ("p_ident", [P, P], F32),
            ("wl", [P, 2, 3 * P], F32), ("wkg", [P, 2, KVR + E], F32),
            ("stats", [P, NT, 6], F32), ("mv", [P, NT, 2], F32), ("var", [P, NT], F32), ("std", [P, NT], F32),
            ("rinv", [P, NT], F32), ("rtmp", [P, NT], F32)])
        xT, = tensors(nc, ctx, [("xT", [P, 2, N], F32)])
        ps_t = [ctx.enter_context(nc.psum_tensor(f"ps_t{k}", [P, CH], F32)) for k in range(2)]
        ps_l = [ctx.enter_context(nc.psum_tensor(f"ps_l{k}", [P, CH], F32)) for k in range(3)]
        ps_n = ctx.enter_context(nc.psum_tensor("ps_n", [P, CH], F32))
        sem = lambda name: ctx.enter_context(nc.semaphore(name))
        x_loaded = [sem(f"x_loaded{g}") for g in range(NCH)]
        weights_loaded, stats_done, aggregated, norm_step = sem("weights_loaded"), sem("stats_done"), sem("aggregated"), sem("norm_step")
        std_done, normed, transposed, xT_ready = sem("std_done"), sem("normed"), sem("transposed"), sem("xT_ready")
        latent_ready, natural_ready = sem("latent_ready"), sem("natural_ready")
        hi_copied, lo_done, natural_copied, xT_stored = sem("hi_copied"), sem("lo_done"), sem("natural_copied"), sem("xT_stored")
        block = ctx.enter_context(nc.Block())
        xv = d["x"].rearrange("(n p) c -> p n c", p=P)

        @block.sync
        def _(sp):
            for g in range(NCH):
                sp.dma_start(x[:, g * TPC:(g + 1) * TPC, :], xv[:, g * TPC:(g + 1) * TPC, :]).then_inc(x_loaded[g], 16)
            for g in range(NCH):
                sp.wait_ge(xT_ready, 2 * (g + 1))
                sp.dma_start(d["xT"][:, :, g * CH:(g + 1) * CH], xT[:, :, g * CH:(g + 1) * CH]).then_inc(xT_stored, 16)
            sp.wait_ge(xT_stored, 16 * NCH)

        @block.vector
        def _(dve):
            steps = 0
            for g in range(NCH):
                tiles = range(g * TPC, (g + 1) * TPC)
                q = slice(g * TPC, (g + 1) * TPC)
                dve.wait_ge(x_loaded[g], 16)
                for t in tiles:
                    nc.vector.bn_stats(stats[:, t, :], x[:, t, :]).then_inc(stats_done, 1)
                dve.wait_ge(stats_done, TPC * (g + 1))
                for t in tiles:
                    nc.vector.bn_aggr(mv[:, t, :], stats[:, t, :]).then_inc(aggregated, 1)
                dve.wait_ge(aggregated, TPC * (g + 1))
                nc.vector.tensor_scalar(var[:, q], mv[:, q, 1], EPS, None, ALU.add).then_inc(norm_step, 1)
                steps += 1
                dve.wait_ge(std_done, g + 1)
                nc.vector.reciprocal(rinv[:, q], std[:, q]).then_inc(norm_step, 1)
                steps += 1
                dve.wait_ge(norm_step, steps)
                nc.vector.tensor_tensor(tmp[:, q], rinv[:, q], rinv[:, q], ALU.mult).then_inc(norm_step, 1)
                steps += 1
                dve.wait_ge(norm_step, steps)
                nc.vector.tensor_tensor(tmp[:, q], tmp[:, q], var[:, q], ALU.mult).then_inc(norm_step, 1)
                steps += 1
                dve.wait_ge(norm_step, steps)
                nc.vector.tensor_scalar(tmp[:, q], tmp[:, q], -0.5, 1.5, ALU.mult, ALU.add).then_inc(norm_step, 1)
                steps += 1
                dve.wait_ge(norm_step, steps)
                nc.vector.tensor_tensor(rinv[:, q], rinv[:, q], tmp[:, q], ALU.mult).then_inc(norm_step, 1)
                steps += 1
                dve.wait_ge(norm_step, steps)
                for t in tiles:
                    nc.vector.tensor_scalar(xn[:, t, :], x[:, t, :], mv[:, t, 0:1], rinv[:, t:t + 1],
                                            ALU.subtract, ALU.mult).then_inc(normed, 1)
            for g in range(NCH):
                s = slice(g * CH, (g + 1) * CH)
                dve.wait_ge(hi_copied, 7 * g + 3)
                nc.vector.tensor_tensor(keep["q1lo"][:, s], ps_l[0][:, :], keep["q1hi"][:, s].bitcast(F32), ALU.subtract).then_inc(lo_done, 1)
                nc.vector.tensor_tensor(keep["q2"][64:P, s], ps_l[1][64:P, :], keep["q2"][64:P, s].bitcast(F32), ALU.subtract).then_inc(lo_done, 1)
                b, c = g // 2, g % 2
                cs = slice(c * CH, (c + 1) * CH)
                dve.wait_ge(hi_copied, 7 * g + 6)
                nc.vector.tensor_tensor(keep["klo"][b][0][64:P, cs], ps_l[2][64:P, :], keep["khi"][b][0][64:P, cs].bitcast(F32), ALU.subtract).then_inc(lo_done, 1)
                nc.vector.tensor_tensor(keep["klo"][b][1][0:64, cs], ps_l[2][0:64, :], keep["khi"][b][1][0:64, cs].bitcast(F32), ALU.subtract).then_inc(lo_done, 1)
                nc.vector.tensor_tensor(keep["kv"][64:P, s], ps_l[2][64:P, :], keep["kv"][64:P, s].bitcast(F32), ALU.subtract).then_inc(lo_done, 1)

        @block.scalar
        def _(act):
            act.dma_start(ident[:, :], d["ident"]).then_inc(weights_loaded, 16)
            act.dma_start(wl[:, :, :], d["wl"]).then_inc(weights_loaded, 16)
            act.dma_start(wkg[:, :, :], d["wkg"]).then_inc(weights_loaded, 16)
            for g in range(NCH):
                act.wait_ge(norm_step, 6 * g + 1)
                nc.scalar.activation(std[:, g * TPC:(g + 1) * TPC], var[:, g * TPC:(g + 1) * TPC], ACT.Sqrt).then_inc(std_done, 1)
            for g in range(NCH):
                s = slice(g * CH, (g + 1) * CH)
                act.wait_ge(transposed, 2 * TPC * (g + 1))
                for k in range(2):
                    nc.scalar.activation(xT[:, k, s], ps_t[k][:, :], ACT.Copy).then_inc(xT_ready, 1)
                b, c = g // 2, g % 2
                cs = slice(c * CH, (c + 1) * CH)
                act.wait_ge(latent_ready, 3 * (g + 1))
                nc.scalar.activation(keep["q1hi"][:, s], ps_l[0][:, :], ACT.Copy).then_inc(hi_copied, 1)
                nc.scalar.activation(keep["q2"][:, s], ps_l[1][:, :], ACT.Copy).then_inc(hi_copied, 1)
                nc.scalar.activation(keep["kv"][:, s], ps_l[2][:, :], ACT.Copy).then_inc(hi_copied, 1)
                nc.scalar.activation(keep["khi"][b][0][64:P, cs], ps_l[2][64:P, :], ACT.Copy).then_inc(hi_copied, 1)
                nc.scalar.activation(keep["khi"][b][1][0:64, cs], ps_l[2][0:64, :], ACT.Copy).then_inc(hi_copied, 1)
                act.wait_ge(natural_ready, g + 1)
                nat = ps_n[:, 0:TPC * (KVR + E)].rearrange("p (t n) -> p t n", t=TPC)
                nc.scalar.activation(keep["kvn"][:, g * TPC:(g + 1) * TPC, :], nat[:, :, 0:KVR], ACT.Copy).then_inc(hi_copied, 1)
                nc.scalar.activation(keep["logits"][:, g * TPC:(g + 1) * TPC, :], nat[:, :, KVR:KVR + E], ACT.Copy).then_inc(hi_copied, 1)

        @block.tensor
        def _(pe):
            pe.wait_ge(weights_loaded, 48)
            for g in range(NCH):
                s = slice(g * CH, (g + 1) * CH)
                ge(pe, xT_ready, 2 * g)
                for j in range(TPC):
                    t = g * TPC + j
                    pe.wait_ge(normed, t + 1)
                    for k in range(2):
                        nc.tensor.transpose(ps_t[k][:, j * P:(j + 1) * P], xn[:, t, k * P:(k + 1) * P], ident[:, :]).then_inc(transposed, 1)
                pe.wait_ge(xT_ready, 2 * (g + 1))
                ge(pe, lo_done, 5 * g)
                ge(pe, hi_copied, 7 * g)
                for m in range(3):
                    for k in range(2):
                        mm = nc.tensor.matmul(ps_l[m][:, :], wl[:, k, m * P:(m + 1) * P], xT[:, k, s], start=k == 0, stop=k == 1)
                    mm.then_inc(latent_ready, 1)
                for j in range(TPC):
                    for k in range(2):
                        mm = nc.tensor.matmul(ps_n[:, j * (KVR + E):(j + 1) * (KVR + E)], xT[:, k, (g * TPC + j) * P:(g * TPC + j + 1) * P],
                                              wkg[:, k, :], start=k == 0, stop=k == 1)
                mm.then_inc(natural_ready, 1)


STEPS = 12
PROLOGUE = ["WA", "QR0", "KR0", "QR1", "KR1", "QL0", "QL1"]
STAGE = ["QR0", "KR0", "QR1", "KR1", "Lp", "QL0", "QL1", "Yp0", "Yp1", "B", "WA", "L0", "Y0", "Y1"]


def misc_order(first):
    got = []
    for b in range(B):
        for name in STAGE:
            if (name in ("B", "WA") and b) or (first and b == 0 and name in ("Lp", "Yp0", "Yp1")):
                continue
            got.append((b, name))
    return got


FIRST, LATER = misc_order(True), misc_order(False)
AFTER_FIRST = len(PROLOGUE) + len(FIRST)


def misc(i, b, name):
    if b is None:
        n = PROLOGUE.index(name)
        return n, n % 2
    if isinstance(i, int) and i == 0:
        n = len(PROLOGUE) + FIRST.index((b, name))
        return n, n % 2
    pos = LATER.index((b, name))
    if isinstance(i, int):
        n = AFTER_FIRST + len(LATER) * (i - 1) + pos
        return n, n % 2
    return i * len(LATER) + (AFTER_FIRST - len(LATER) + pos), (AFTER_FIRST + pos) % 2


def misc_before(i, b, name):
    n, _ = misc(i, b, name)
    if isinstance(n, int):
        return n // 2
    pos = LATER.index((b, name))
    return i * (len(LATER) // 2) + (AFTER_FIRST - len(LATER) + pos) // 2


assert len(LATER) % 2 == 0 and (AFTER_FIRST - len(LATER)) % 2 == 0


def step_of(k):
    c, j = (0, k) if k < TPC else (1, k - TPC)
    return c, j, max(0, j * P - c * CH), j * P >= c * CH


RING = 3


def ring_of(k):
    r = k - 1 if k < TPC else k - 2
    steps = [s for s in range(STEPS) if s not in (0, TPC)]
    if r >= RING:
        return r % RING, steps[r - RING]
    last = max(q for q in range(len(steps)) if q % RING == r % RING)
    return r % RING, steps[last] - STEPS


def pieces():
    got = [(e, t, 0, (t + 1) * P) for e in range(2) for t in range(TPC)]
    for t in range(TPC, 2 * TPC):
        for e in range(2):
            got += [(e, t, 0, CH), (e, t, CH, (t + 1) * P - CH)]
    return got


PIECES = pieces()
NP = len(PIECES)
U = 2 * STEPS


def attend(nc, d, keep):
    ctx = ExitStack()
    with ctx:
        khi, klo, kvn = keep["khi"], keep["klo"], keep["kvn"]
        qhi, qlo = ([[ctx.enter_context(nc.sbuf_tensor(f"q{w}{b}{e}", [P, T], F32R)) for e in range(2)] for b in range(B)]
                    for w in ("hi", "lo"))
        cosv, sinv, ident, ident16, ones, ones16, mask16 = tensors(nc, ctx, [
            ("cosv", [P, T], F32), ("sinv", [P, T], F32), ("ident", [P, P], F32), ("ident16", [P, P], BF16),
            ("ones", [P, P], F32), ("ones16", [P, P], BF16), ("mask16", [P, P], BF16)])
        raw_a, raw_b, rhi, rlo, lhi, llo, bhi, blo = tensors(nc, ctx, [
            ("raw_a", [P, 1024], F32), ("raw_b", [96, 1280], F32),
            ("rhi", [P, 384], F32R), ("rlo", [P, 384], F32R), ("lhi", [P, 256], F32R), ("llo", [P, 256], F32R),
            ("bhi", [P, 256], F32R), ("blo", [P, 256], F32R)])
        t1, sh, first, ring, shift, oe, rec, on, ohi, olo = tensors(nc, ctx, [
            ("t1", [P, 4, CH], F32), ("sh", [P, 4, CH], F32), ("first", [P, 2, 2, CH], F32), ("ring", [P, RING, 2, CH], F32),
            ("shift", [P, 2, 2, CH], BF16), ("oe", [P, CH], F32), ("rec", [P, CH], F32), ("on", [P, CH], F32),
            ("ohi", [P, CH], F32R), ("olo", [P, CH], F32R)])
        raw_mask = sh[:, 0, 0:P]
        nm0, nm1, nm1c = tensors(nc, ctx, [("nm0", [P, 8], F32), ("nm1", [P, 2, 8], F32), ("nm1c", [P, 8], F32)])
        yacc = keep["yacc"]
        bank = lambda name: ctx.enter_context(nc.psum_tensor(name, [P, CH], F32))
        ps_s = [bank(f"ps_s{k}") for k in range(3)]
        ps_m = [bank(f"ps_m{k}") for k in range(2)]
        ps_o = bank("ps_o")
        ps_x = [bank(f"ps_x{k}") for k in range(2)]
        sem = lambda name: ctx.enter_context(nc.semaphore(name))
        consts_loaded, a_loaded, b_loaded = sem("consts_loaded"), sem("a_loaded"), sem("b_loaded")
        scores_ready, exp_done, pv_done = sem("scores_ready"), sem("exp_done"), sem("pv_done")
        misc_ready, misc_free = sem("misc_ready"), [sem("misc_free0"), sem("misc_free1")]
        piece_ready, piece_max, halves_joined = sem("piece_ready"), sem("piece_max"), sem("halves_joined")
        shift0_done, shift1_done = sem("shift0_done"), sem("shift1_done")
        a_split, b_split = sem("a_split"), sem("b_split")
        rope_in, rope_sin, rope_sum = sem("rope_in"), sem("rope_sin"), sem("rope_sum")
        hi_done, latent_lo, rope_lo = sem("hi_done"), sem("latent_lo"), sem("rope_lo")
        sum_pool, sum_dve = sem("sum_pool"), sem("sum_dve")
        o_copied, rec_done, on_done, ohi_done, olo_done, y_added = (sem("o_copied"), sem("rec_done"), sem("on_done"),
                                                                    sem("ohi_done"), sem("olo_done"), sem("y_added"))
        y_zeroed, consts16_done = sem("y_zeroed"), sem("consts16_done")
        block = ctx.enter_context(nc.Block())

        def pairs_loop(engine, body):
            body(0)
            with engine.Fori(1, PAIRS) as i:
                body(i)

        def probs(k, e):
            c, j, off, _ = step_of(k)
            if j == 0:
                return first[:, c, e, off:]
            return ring[:, ring_of(k)[0], e, off:]

        @block.sync
        def _(sp):
            for name, to in (("ident", ident[:, :]), ("cos", cosv[:, :]), ("sin", sinv[:, :]), ("ones", ones[:, :]), ("mask", raw_mask)):
                sp.dma_start(to, d[name]).then_inc(consts_loaded, 16)
            sp.dma_start(raw_a[:, :], d["a"][0]).then_inc(a_loaded, 16)
            sp.dma_start(raw_b[:, :], d["b"][0]).then_inc(b_loaded, 16)
            with sp.Fori(0, PAIRS) as i:
                sp.wait_ge(a_split, i * 4 + 4)
                sp.dma_start(raw_a[:, :], d["a"][i + 1]).then_inc(a_loaded, 16)
                sp.wait_ge(b_split, i * 2 + 2)
                sp.dma_start(raw_b[:, :], d["b"][i + 1]).then_inc(b_loaded, 16)
            sp.wait_ge(a_loaded, 16 * (PAIRS + 1))
            sp.wait_ge(b_loaded, 16 * (PAIRS + 1))

        @block.tensor
        def _(pe):
            def side(i, b, name, products):
                _, x = misc(i, b, name)
                ge(pe, misc_free[x], misc_before(i, b, name))
                products(ps_x[x]).then_inc(misc_ready, 1)

            def fold_a(i, b, p):
                ge(pe, a_loaded, p * 16 + 16)
                qn = raw_a[:, 0:512].rearrange("p (e n) -> p e n", e=2)
                kn = raw_a[:, 512:640].rearrange("p (e n) -> p e n", e=2)

                def products(out):
                    for part in range(2):
                        for at, e in ((0, 1), (64, 0)):
                            mm = nc.tensor.matmul(out[:, part * P + at:part * P + at + 64], qn[:, e, part * P:(part + 1) * P],
                                                  kn[:, e, :], start=True, stop=True)
                    return mm
                side(i, b, "WA", products)

            def fold_b(i, b):
                ge(pe, b_loaded, i * 16 + 16)
                vt = raw_b[:, 0:256].rearrange("p (e h n) -> p e h n", e=2, h=2)
                wo = raw_b[:, 256:1280].rearrange("p (e h n) -> p e h n", e=2, h=2)

                def products(out):
                    for e in range(2):
                        for h in range(2):
                            mm = nc.tensor.matmul(out[64 * e:64 * e + 64, 0:C], vt[:, e, h, :], wo[:, e, h, :], start=h == 0, stop=h == 1)
                    return mm
                side(i, b, "B", products)

            def project(i, b, name, p, to_b):
                c = int(name[2])
                s = slice((2 * to_b + c) * CH, (2 * to_b + c + 1) * CH)
                q1h, q1l, q2, kv = (keep[n][:, s] for n in ("q1hi", "q1lo", "q2", "kv"))
                hi, lo = (lhi, llo) if name[:2] == "QL" else (rhi, rlo)
                if name[:2] == "KR":
                    passes = [(rhi[:, 256:384], kv), (rlo[:, 256:384], kv)]
                else:
                    passes = [(hi[:, 0:P], q1h), (hi[:, 0:P], q1l), (hi[:, P:2 * P], q2), (lo[:, P:2 * P], q2), (lo[:, 0:P], q1h)]
                ge(pe, a_split, p * 4 + 4)

                def products(out):
                    for n, (w, x) in enumerate(passes):
                        mm = nc.tensor.matmul(out[:, :], w, x, start=n == 0, stop=n == len(passes) - 1)
                    return mm
                side(i, b, name, products)

            def piece(s, n, b):
                e, t, k0, keys = PIECES[n]
                ge(pe, piece_max, s * NP + n - 1)
                if n == 0:
                    pe.wait_ge(hi_done, s * 12 + 8)
                if n == 8:
                    pe.wait_ge(hi_done, s * 12 + 12)
                out = ps_m[n % 2]
                diagonal = k0 + keys == (t + 1) * P
                mm = nc.tensor.matmul(out[:, 0:keys], qhi[b][e][:, t * P:(t + 1) * P], khi[b][e][:, k0:k0 + keys],
                                      start=True, stop=not diagonal)
                if diagonal:
                    mm = nc.tensor.matmul(out[:, keys - P:keys], mask16[:, :], ident16[:, :], start=False, stop=True)
                mm.then_inc(piece_ready, 1)

            def scores(s, b, k, e):
                c, j, off, diagonal = step_of(k)
                u = s * U + 2 * k + e
                if k == 0 and e == 0:
                    pe.wait_ge(hi_done, s * 12 + 12)
                    pe.wait_ge(latent_lo, s * 4 + 4)
                    pe.wait_ge(rope_lo, s * 8 + 8)
                if k == 0:
                    pe.wait_ge(shift0_done, s * 8 + 8)
                if k == TPC:
                    pe.wait_ge(shift1_done, s * 8 + 8)
                ge(pe, exp_done, u - 2)
                out = ps_s[(2 * k + e) % 3]
                q = slice(c * CH + off, (c + 1) * CH)
                kk = slice(j * P, (j + 1) * P)
                nc.tensor.matmul(out[:, off:], ones16[:, :], shift[:, c, e, off:], start=True, stop=False)
                if diagonal:
                    nc.tensor.matmul(out[:, off:off + P], ident16[:, :], mask16[:, :], start=False, stop=False)
                nc.tensor.matmul(out[:, off:], khi[b][e][:, kk], qhi[b][e][:, q], start=False, stop=False)
                nc.tensor.matmul(out[:, off:], khi[b][e][:, kk], qlo[b][e][:, q], start=False, stop=False)
                nc.tensor.matmul(out[:, off:], klo[b][e][:, kk], qhi[b][e][:, q], start=False, stop=True).then_inc(scores_ready, 1)

            def values(s, b, k):
                c, j, off, _ = step_of(k)
                last = k in (TPC - 1, STEPS - 1)
                if j == 0:
                    ge(pe, o_copied, s * 2 + c)
                for e in range(2):
                    pe.wait_ge(exp_done, s * U + 2 * k + e + 1)
                    nc.tensor.matmul(ps_o[64 * e:64 * e + 64, off:], kvn[:, b * 8 + j, :], probs(k, e),
                                     start=j == 0, stop=last).then_inc(pv_done, 1)

            def row_sums(i, b, name, s, c):
                pe.wait_ge(*((sum_dve, s * 14 + 14) if c else (sum_pool, s * 6 + 6)))

                def products(out):
                    for e in range(2):
                        mm = nc.tensor.matmul(out[64 * e:64 * e + 64, :], ones[:, 0:64], first[:, c, e, :], start=True, stop=True)
                    return mm
                side(i, b, name, products)

            def project_out(i, b, name, s, c, m):
                pe.wait_ge(b_split, i * 2 + 2 if name[1] != "p" or b else i * 2)
                pe.wait_ge(olo_done, s * 2 + c + 1)

                def products(out):
                    cols = slice(m * P, (m + 1) * P)
                    nc.tensor.matmul(out[:, :], bhi[:, cols], ohi[:, :], start=True, stop=False)
                    nc.tensor.matmul(out[:, :], bhi[:, cols], olo[:, :], start=False, stop=False)
                    return nc.tensor.matmul(out[:, :], blo[:, cols], ohi[:, :], start=False, stop=True)
                side(i, b, name, products)

            def body(i):
                for b in range(B):
                    s = i * 2 + b
                    earlier = b == 1 or not isinstance(i, int)
                    p = i + 1 if b else i
                    for k in range(STEPS):
                        take = [4 * (k - 6) + n for n in range(4)] if k >= 6 else [None] * 4

                        def maxima(n):
                            if take[n] is not None:
                                piece(s + 1, take[n], 1 - b)
                        maxima(0)
                        scores(s, b, k, 0)
                        maxima(1)
                        scores(s, b, k, 1)
                        maxima(2)
                        if k:
                            values(s, b, k - 1)
                        elif earlier:
                            values(s - 1, 1 - b, STEPS - 1)
                        maxima(3)
                        if k < 2:
                            project(i, b, f"QR{k}", p, 1 - b)
                            project(i, b, f"KR{k}", p, 1 - b)
                        if k == 1 and earlier:
                            row_sums(i, b, "Lp", s - 1, 1)
                        if k == 2:
                            project(i, b, "QL0", p, 1 - b)
                            project(i, b, "QL1", p, 1 - b)
                        if k == 3 and earlier:
                            for m in range(2):
                                project_out(i, b, f"Yp{m}", s - 1, 1, m)
                        if k == 5 and b == 0:
                            fold_b(i, b)
                            fold_a(i, b, i + 1)
                        if k == 6:
                            row_sums(i, b, "L0", s, 0)
                        if k == 8:
                            for m in range(2):
                                project_out(i, b, f"Y{m}", s, 0, m)

            pe.wait_ge(consts_loaded, 16 * 5)
            pe.wait_ge(consts16_done, 3)
            fold_a(0, None, 0)
            for name in PROLOGUE[1:]:
                project(0, None, name, 0, 0)
            for n in range(NP):
                piece(0, n, 0)
            pairs_loop(pe, body)
            s = 2 * PAIRS - 1
            values(s, 1, STEPS - 1)
            n = AFTER_FIRST + len(LATER) * (PAIRS - 1)
            pe.wait_ge(sum_dve, s * 14 + 14)
            pe.wait_ge(misc_free[0], n // 2)
            pe.wait_ge(misc_free[1], n // 2)
            for e in range(2):
                mm = nc.tensor.matmul(ps_x[0][64 * e:64 * e + 64, :], ones[:, 0:64], first[:, 1, e, :], start=True, stop=True)
            mm.then_inc(misc_ready, 1)
            pe.wait_ge(olo_done, 2 * s + 2)
            pe.wait_ge(misc_free[0], n // 2 + 1)
            for m in range(2):
                out, cols = ps_x[1 - m], slice(m * P, (m + 1) * P)
                nc.tensor.matmul(out[:, :], bhi[:, cols], ohi[:, :], start=True, stop=False)
                nc.tensor.matmul(out[:, :], bhi[:, cols], olo[:, :], start=False, stop=False)
                nc.tensor.matmul(out[:, :], blo[:, cols], ohi[:, :], start=False, stop=True).then_inc(misc_ready, 1)

        @block.scalar
        def _(act):
            def exponent(s, k, e):
                c, j, off, _ = step_of(k)
                u = s * U + 2 * k + e
                act.wait_ge(scores_ready, u + 1)
                if j:
                    _, before = ring_of(k)
                    ge(act, pv_done, s * U + 2 * before + e + 1)
                    if before >= 0:
                        cb, jb, _, _ = step_of(before)
                        sb = s
                    else:
                        cb, jb, _, _ = step_of(before + STEPS)
                        sb = s - 1
                    if cb:
                        ge(act, sum_dve, sb * 14 + 2 * (jb - 1) + e + 1)
                    else:
                        ge(act, sum_pool, sb * 6 + 2 * (jb - 1) + e + 1)
                nc.scalar.activation(probs(k, e), ps_s[(2 * k + e) % 3][:, off:], ACT.Exp, scale=SCALE).then_inc(exp_done, 1)

            def first_free(i, b, c):
                if c == 0:
                    if b == 1:
                        act.wait_ge(misc_ready, misc(i, 0, "L0")[0] + 1)
                    elif not isinstance(i, int):
                        act.wait_ge(misc_ready, misc(i, 0, "QR0")[0] - 2)
                elif b == 1 or not isinstance(i, int):
                    act.wait_ge(misc_ready, misc(i, b, "Lp")[0] + 1)

            def latent_hi(i, b, to_b):
                for c in range(2):
                    n, x = misc(i, b, f"QL{c}")
                    act.wait_ge(misc_ready, n + 1)
                    cs = slice(c * CH, (c + 1) * CH)
                    nc.scalar.activation(qhi[to_b][1][0:64, cs], ps_x[x][0:64, :], ACT.Copy).then_inc(hi_done, 1)
                    nc.scalar.activation(qhi[to_b][0][64:P, cs], ps_x[x][64:P, :], ACT.Copy).then_inc(hi_done, 1)

            def rope_hi(s, c, to_b):
                cs = slice(c * CH, (c + 1) * CH)
                for g, to in ((2 * c, qhi), (2 * c + 1, khi)):
                    act.wait_ge(rope_sum, s * 4 + g + 1)
                    nc.scalar.activation(to[to_b][0][0:64, cs], t1[0:64, g, :], ACT.Copy).then_inc(hi_done, 1)
                    nc.scalar.activation(to[to_b][1][64:P, cs], t1[64:P, g, :], ACT.Copy).then_inc(hi_done, 1)

            def shift_matrix(s, c):
                if c == 0:
                    act.wait_ge(piece_max, s * NP + 8)
                    ge(act, scores_ready, (s - 1) * U + 8)
                else:
                    act.wait_ge(halves_joined, s + 1)
                    ge(act, scores_ready, s * U)
                for e in range(2):
                    for t in range(TPC):
                        m = (nm1c if c else nm0)[:, e * TPC + t:e * TPC + t + 1]
                        nc.scalar.activation(shift[:, c, e, t * P:(t + 1) * P], ident[:, :], ACT.Copy, scale=m).then_inc(
                            shift1_done if c else shift0_done, 1)

            def copy_out(s, c):
                act.wait_ge(pv_done, s * U + (U if c else 8))
                ge(act, on_done, s * 2 + c)
                nc.scalar.activation(oe[:, :], ps_o[:, :], ACT.Copy).then_inc(o_copied, 1)

            def out_hi(s, c, last_y):
                act.wait_ge(on_done, s * 2 + c + 1)
                if last_y is not None:
                    act.wait_ge(misc_ready, last_y + 1)
                nc.scalar.activation(ohi[:, :], on[:, :], ACT.Copy).then_inc(ohi_done, 1)

            def body(i):
                for b in range(B):
                    s = i * 2 + b
                    earlier = b == 1 or not isinstance(i, int)
                    for k in range(STEPS):
                        if k in (0, TPC):
                            first_free(i, b, k // TPC)
                        exponent(s, k, 0)
                        exponent(s, k, 1)
                        if k == 0 and earlier:
                            copy_out(s - 1, 1)
                        if k == 1:
                            shift_matrix(s, 1)
                        if k == 2:
                            latent_hi(i, b, 1 - b)
                            if earlier:
                                last = misc(i, 0, "Y1")[0] if b else misc(i, 0, "QR0")[0] - 1
                                out_hi(s - 1, 1, last)
                        if k == 3:
                            rope_hi(s + 1, 0, 1 - b)
                        if k == 4:
                            copy_out(s, 0)
                            rope_hi(s + 1, 1, 1 - b)
                        if k == 7:
                            out_hi(s, 0, misc(i, b, "Yp1")[0] if earlier else None)
                        if k == 8:
                            shift_matrix(s + 1, 0)

            act.wait_ge(consts_loaded, 16 * 5)
            for to, of in ((ident16, ident[:, :]), (ones16, ones[:, :]), (mask16, raw_mask)):
                nc.scalar.activation(to[:, :], of, ACT.Copy).then_inc(consts16_done, 1)
            rope_hi_first = PROLOGUE.index("QL0")
            assert rope_hi_first == 5
            latent_hi(0, None, 0)
            for c in range(2):
                rope_hi(0, c, 0)
            shift_matrix(0, 0)
            pairs_loop(act, body)
            s = 2 * PAIRS - 1
            copy_out(s, 1)
            out_hi(s, 1, AFTER_FIRST + len(LATER) * (PAIRS - 1) - 1)

        @block.vector
        def _(dve):
            def rope_products(i, b, name, g, s):
                n, x = misc(i, b, name)
                c = g // 2
                ge(dve, rope_lo, (s - 1) * 8 + 2 * g + 2)
                dve.wait_ge(misc_ready, n + 1)
                nc.vector.tensor_tensor(t1[:, g, :], ps_x[x][:, :], cosv[:, c * CH:(c + 1) * CH], ALU.mult).then_inc(rope_in, 1)
                nc.vector.stream_shuffle(sh[:, g, :], ps_x[x][:, :], PAIRSWAP).then_inc(rope_in, 1)

            def latent_low(i, b, s, to_b):
                for c in range(2):
                    _, x = misc(i, b, f"QL{c}")
                    cs = slice(c * CH, (c + 1) * CH)
                    dve.wait_ge(hi_done, s * 12 + 2 * c + 2)
                    nc.vector.tensor_tensor(qlo[to_b][1][0:64, cs], ps_x[x][0:64, :], qhi[to_b][1][0:64, cs].bitcast(F32),
                                            ALU.subtract).then_inc(latent_lo, 1)
                    nc.vector.tensor_tensor(qlo[to_b][0][64:P, cs], ps_x[x][64:P, :], qhi[to_b][0][64:P, cs].bitcast(F32),
                                            ALU.subtract).then_inc(latent_lo, 1)
                    dve.wait_ge(latent_lo, s * 4 + 2 * c + 2)
                    dve.sem_inc(misc_free[x], 1)

            def split_a(i, b, p):
                n, x = misc(i, b, "WA")
                dve.wait_ge(a_loaded, p * 16 + 16)
                nc.vector.tensor_copy(rhi[:, :], raw_a[:, 640:1024]).then_inc(a_split, 1)
                dve.wait_ge(misc_ready, n + 1)
                nc.vector.tensor_copy(lhi[:, :], ps_x[x][:, 0:256]).then_inc(a_split, 1)
                dve.wait_ge(a_split, p * 4 + 2)
                nc.vector.tensor_tensor(rlo[:, :], raw_a[:, 640:1024], rhi[:, :].bitcast(F32), ALU.subtract).then_inc(a_split, 1)
                nc.vector.tensor_tensor(llo[:, :], ps_x[x][:, 0:256], lhi[:, :].bitcast(F32), ALU.subtract).then_inc(a_split, 1)
                dve.wait_ge(a_split, p * 4 + 4)
                dve.sem_inc(misc_free[x], 1)

            def split_b(i, b):
                n, x = misc(i, b, "B")
                dve.wait_ge(misc_ready, n + 1)
                nc.vector.tensor_copy(bhi[:, :], ps_x[x][:, 0:256]).then_inc(b_split, 1)
                dve.wait_ge(b_split, i * 2 + 1)
                nc.vector.tensor_tensor(blo[:, :], ps_x[x][:, 0:256], bhi[:, :].bitcast(F32), ALU.subtract).then_inc(b_split, 1)
                dve.wait_ge(b_split, i * 2 + 2)
                dve.sem_inc(misc_free[x], 1)

            def join_halves(s):
                dve.wait_ge(piece_max, s * NP + NP)
                ge(dve, shift1_done, s * 8)
                nc.vector.tensor_tensor(nm1c[:, :], nm1[:, 0, :], nm1[:, 1, :], ALU.min).then_inc(halves_joined, 1)

            def maximum(s, n):
                e, t, k0, keys = PIECES[n]
                dve.wait_ge(piece_ready, s * NP + n + 1)
                if n == 0:
                    ge(dve, shift0_done, s * 8)
                if n == 8:
                    ge(dve, halves_joined, s)
                col = e * TPC + t % TPC
                to = nm0[:, col:col + 1] if t < TPC else nm1[:, int(k0 > 0), col:col + 1]
                nc.vector.tensor_reduce(out=to, in_=ps_m[n % 2][:, 0:keys], axis=AXX, op=ALU.max, negate=True).then_inc(piece_max, 1)

            def add_probs(s, k):
                c, j, off, _ = step_of(k)
                for e in range(2):
                    dve.wait_ge(exp_done, s * U + 2 * k + e + 1)
                    if j == 1:
                        dve.wait_ge(pv_done, s * U + 2 * (k - 1) + e + 1)
                    else:
                        dve.wait_ge(sum_dve, s * 14 + 2 * (j - 2) + e + 1)
                    nc.vector.tensor_tensor(first[:, c, e, off:], first[:, c, e, off:], probs(k, e), ALU.add).then_inc(sum_dve, 1)

            def normalise(n, x, s, c):
                dve.wait_ge(misc_ready, n + 1)
                ge(dve, on_done, s * 2 + c)
                nc.vector.reciprocal(rec[:, :], ps_x[x][:, :]).then_inc(rec_done, 1)
                dve.wait_ge(rec_done, s * 2 + c + 1)
                dve.sem_inc(misc_free[x], 1)
                dve.wait_ge(o_copied, s * 2 + c + 1)
                ge(dve, olo_done, s * 2 + c)
                nc.vector.tensor_tensor(on[:, :], oe[:, :], rec[:, :], ALU.mult).then_inc(on_done, 1)

            def add_out(n, x, s, b, c, m):
                dve.wait_ge(misc_ready, n + 1)
                ge(dve, y_added, s * 4 + 2 * c + m - 4)
                at = slice(b * T + c * CH, b * T + (c + 1) * CH)
                nc.vector.tensor_tensor(yacc[:, m, at], yacc[:, m, at], ps_x[x][:, :], ALU.add).then_inc(y_added, 1)
                dve.wait_ge(y_added, s * 4 + 2 * c + m + 1)
                dve.sem_inc(misc_free[x], 1)

            def rope(i, b, c, s):
                for g, name in ((2 * c, f"QR{c}"), (2 * c + 1, f"KR{c}")):
                    rope_products(i, b, name, g, s)
                    dve.wait_ge(rope_in, s * 8 + 2 * g + 2)
                    dve.sem_inc(misc_free[misc(i, b, name)[1]], 1)

            def body(i):
                for b in range(B):
                    s = i * 2 + b
                    earlier = b == 1 or not isinstance(i, int)
                    for k in range(STEPS):
                        if k == 0:
                            join_halves(s)
                        if k < 2:
                            rope(i, b, k, s + 1)
                        if k == 1 and earlier:
                            normalise(*misc(i, b, "Lp"), s - 1, 1)
                        if k == 2:
                            latent_low(i, b, s + 1, 1 - b)
                        if k == 3 and earlier:
                            for m in range(2):
                                add_out(*misc(i, b, f"Yp{m}"), s - 1, 1 - b, 1, m)
                        if k == 5 and b == 0:
                            split_b(i, b)
                            split_a(i, b, i + 1)
                        if k >= 6:
                            for n in range(3):
                                maximum(s + 1, 4 * (k - 6) + n)
                        if k == 6:
                            normalise(*misc(i, b, "L0"), s, 0)
                        if k >= 6:
                            maximum(s + 1, 4 * (k - 6) + 3)
                        if k == 8:
                            for m in range(2):
                                add_out(*misc(i, b, f"Y{m}"), s, b, 0, m)
                        if k > TPC:
                            add_probs(s, k)

            nc.vector.memset(yacc[:, :, :], 0.0).then_inc(y_zeroed, 1)
            dve.wait_ge(y_zeroed, 1)
            dve.wait_ge(consts_loaded, 16 * 5)
            dve.wait_ge(consts16_done, 3)
            split_a(0, None, 0)
            for c in range(2):
                rope(0, None, c, 0)
            latent_low(0, None, 0, 0)
            for n in range(NP):
                maximum(0, n)
            pairs_loop(dve, body)
            s = 2 * PAIRS - 1
            n = AFTER_FIRST + len(LATER) * (PAIRS - 1)
            normalise(n, 0, s, 1)
            for m in range(2):
                add_out(n + 1 + m, 1 - m, s, 1, 1, m)

        @block.gpsimd
        def _(pool):
            def rope_sums(s, c):
                for g in (2 * c, 2 * c + 1):
                    pool.wait_ge(rope_in, s * 8 + 2 * g + 2)
                    nc.gpsimd.tensor_tensor(sh[:, g, :], sh[:, g, :], sinv[:, c * CH:(c + 1) * CH], ALU.mult).then_inc(rope_sin, 1)
                    pool.wait_ge(rope_sin, s * 4 + g + 1)
                    nc.gpsimd.tensor_tensor(t1[:, g, :], t1[:, g, :], sh[:, g, :], ALU.add).then_inc(rope_sum, 1)

            def rope_low(s, c, to_b):
                cs = slice(c * CH, (c + 1) * CH)
                for g, hi, lo in ((2 * c, qhi, qlo), (2 * c + 1, khi, klo)):
                    pool.wait_ge(rope_sum, s * 4 + g + 1)
                    pool.wait_ge(hi_done, s * 12 + 4 + 2 * g + 2)
                    for e, rows in ((0, slice(0, 64)), (1, slice(64, P))):
                        ge(pool, rope_lo, s * 8 + 2 * g + e)
                        nc.gpsimd.tensor_tensor(lo[to_b][e][rows, cs], t1[rows, g, :], hi[to_b][e][rows, cs].bitcast(F32),
                                                ALU.subtract).then_inc(rope_lo, 1)

            def add_probs(s, k):
                _, j, off, _ = step_of(k)
                for e in range(2):
                    pool.wait_ge(exp_done, s * U + 2 * k + e + 1)
                    if j == 1:
                        pool.wait_ge(pv_done, s * U + e + 1)
                    else:
                        pool.wait_ge(sum_pool, s * 6 + 2 * (j - 2) + e + 1)
                    nc.gpsimd.tensor_tensor(first[:, 0, e, off:], first[:, 0, e, off:], probs(k, e), ALU.add).then_inc(sum_pool, 1)

            def out_low(s, c):
                pool.wait_ge(ohi_done, s * 2 + c + 1)
                nc.gpsimd.tensor_tensor(olo[:, :], on[:, :], ohi[:, :].bitcast(F32), ALU.subtract).then_inc(olo_done, 1)

            def body(i):
                for b in range(B):
                    s = i * 2 + b
                    earlier = b == 1 or not isinstance(i, int)
                    rope_sums(s + 1, 0)
                    add_probs(s, 1)
                    rope_sums(s + 1, 1)
                    add_probs(s, 2)
                    if earlier:
                        out_low(s - 1, 1)
                    add_probs(s, 3)
                    pool.wait_ge(sum_pool, s * 6 + 6)
                    rope_low(s + 1, 0, 1 - b)
                    rope_low(s + 1, 1, 1 - b)
                    pool.wait_ge(rope_lo, s * 8 + 16)
                    out_low(s, 0)

            pool.wait_ge(consts_loaded, 16 * 5)
            for c in range(2):
                rope_sums(0, c)
            pool.wait_ge(rope_sum, 4)
            for c in range(2):
                rope_low(0, c, 0)
            pool.wait_ge(rope_lo, 8)
            pairs_loop(pool, body)
            out_low(2 * PAIRS - 1, 1)


ROUND = 1024
UNITS = ROUND // CH


def mix(nc, d, keep, out):
    ctx = ExitStack()
    with ctx:
        yacc, logits = keep["yacc"], keep["logits"]
        ident, sel, xtf, xhi, xlo = tensors(nc, ctx, [
            ("m_ident", [P, P], F32), ("sel", [P, 2, P], F32R), ("xtf", [P, 2, ROUND], F32),
            ("xhi", [P, 2, ROUND], F32R), ("xlo", [P, 2, ROUND], F32R)])
        raw, whi, wlo, gs, hf, hh, hl = tensors(nc, ctx, [
            ("raw", [P, 2, 768], F32), ("whi", [P, 2, 768], F32R), ("wlo", [P, 2, 768], F32R),
            ("gs", [P, 2, CH], F32), ("hf", [P, 2, CH], F32), ("hh", [P, 2, CH], F32R), ("hl", [P, 2, CH], F32R)])
        wst, top, rest, shifted, w2, total, selraw, xres, yout = tensors(nc, ctx, [
            ("wst", [P, N], F32R), ("top", [P, NT, 8], F32), ("rest", [P, NT, E], F32), ("shifted", [P, NT, E], F32),
            ("w2", [P, NT, 2 * E], F32), ("total", [P, NT], F32), ("selraw", [P, IT * P], F32),
            ("xres", [P, NT, C], F32), ("yout", [P, NT, C], F32)])
        bank = lambda name: ctx.enter_context(nc.psum_tensor(name, [P, CH], F32))
        ps_y = [[bank(f"ps_y{m}{c}") for c in range(UNITS)] for m in range(2)]
        ps_g, ps_u, ps_w, ps_t = bank("ps_g"), bank("ps_u"), bank("ps_w"), bank("ps_tr")
        sem = lambda name: ctx.enter_context(nc.semaphore(name))
        consts_loaded, x_loaded, res_loaded, w_loaded = sem("m_consts_loaded"), sem("m_x_loaded"), sem("res_loaded"), [sem("w_loaded0"), sem("w_loaded1")]
        step, exp_done, w_transposed, w_hi, w_lo, sel_ready = sem("route_step"), sem("route_exp"), sem("w_transposed"), sem("w_hi"), sem("w_lo"), sem("sel_ready")
        x_hi, x_lo, w_hi_done, w_lo_done = sem("x_hi"), sem("x_lo"), sem("expert_hi"), sem("expert_lo")
        weights_bcast, gate_ready, up_ready, silu_done, gated, h_done, h_hi, h_lo, down_done = (
            sem("weights_bcast"), sem("gate_ready"), sem("up_ready"), sem("silu_done"), sem("gated"), sem("h_done"),
            sem("h_hi"), sem("h_lo"), sem("down_done"))
        y_summed, y_transposed, y_final, stored = sem("y_summed"), sem("y_transposed"), sem("y_final"), sem("stored")
        block = ctx.enter_context(nc.Block())
        UR = IT * UNITS
        ROUNDS = N // ROUND
        TR = ROUND // P
        xv = d["x"].rearrange("(n p) c -> p n c", p=P)
        ov = out.rearrange("(n p) c -> p n c", p=P)

        def tiles_loop(engine, body):
            body(0)
            with engine.Fori(1, IT // 2) as i:
                body(i)

        @block.sync
        def _(sp):
            sp.dma_start(ident[:, :], d["ident"]).then_inc(consts_loaded, 16)
            sp.dma_start(selraw[:, :], d["sel"]).then_inc(consts_loaded, 16)
            for r in range(ROUNDS):
                ge(sp, x_lo, 2 * r)
                sp.dma_start(xtf[:, :, :], d["xT"][:, :, r * ROUND:(r + 1) * ROUND]).then_inc(x_loaded, 16)
                if r == 0:
                    sp.dma_start(xres[:, :, :], xv).then_inc(res_loaded, 16)

                def body(i):
                    for q in range(2):
                        ge(sp, w_lo_done, r * IT + 2 * i + q - 1)
                        sp.dma_start(raw[:, q, :], d["e"][2 * i + q]).then_inc(w_loaded[q], 16)
                tiles_loop(sp, body)
            for r in range(ROUNDS):
                sp.wait_ge(y_final, (r + 1) * TR)
                sp.dma_start(ov[:, r * TR:(r + 1) * TR, :], yout[:, r * TR:(r + 1) * TR, :]).then_inc(stored, 16)
            sp.wait_ge(stored, 16 * ROUNDS)

        @block.tensor
        def _(pe):
            pe.wait_ge(consts_loaded, 32)
            pe.wait_ge(step, 8 * 1 + 2 * NT)
            for g in range(NCH):
                for j in range(TPC):
                    t = g * TPC + j
                    if g:
                        pe.wait_ge(w_lo, g)
                    mm = nc.tensor.transpose(ps_t[0:2 * E, j * P:(j + 1) * P], w2[:, t, :], ident[:, :])
                mm.then_inc(w_transposed, 1)
            pe.wait_ge(w_lo, NCH)

            def down(r, i, q, c, first):
                n = r * UR + i * 4 + 2 * q + c
                pe.wait_ge(h_lo, n + 1)
                if first:
                    ge(pe, y_summed, r * 4)
                for m in range(2):
                    cols = slice(512 + m * P, 512 + (m + 1) * P)
                    nc.tensor.matmul(ps_y[m][c][:, :], whi[:, q, cols], hh[:, c, :], start=first, stop=False, skip_group_check=True)
                    nc.tensor.matmul(ps_y[m][c][:, :], whi[:, q, cols], hl[:, c, :], start=False, stop=False, skip_group_check=True)
                    mm = nc.tensor.matmul(ps_y[m][c][:, :], wlo[:, q, cols], hh[:, c, :], start=False, stop=True, skip_group_check=True)
                mm.then_inc(down_done, 1)

            for r in range(ROUNDS):
                pe.wait_ge(x_lo, 2 * r + 2)

                def body(i):
                    for q in range(2):
                        for c in range(UNITS):
                            n = r * UR + i * 4 + 2 * q + c
                            xs = slice(c * CH, (c + 1) * CH)
                            if c == 0:
                                pe.wait_ge(sel_ready, r * IT + 2 * i + q + 1)
                                pe.wait_ge(w_lo_done, r * IT + 2 * i + q + 1)
                            ge(pe, gated, n)
                            nc.tensor.matmul(ps_w[:, :], sel[:, q, :], wst_rows(r, c), start=True, stop=True).then_inc(weights_bcast, 1)
                            for out_ps, w0, done in ((ps_g, 0, gate_ready), (ps_u, 256, up_ready)):
                                if done is up_ready:
                                    ge(pe, h_done, n)
                                for k in range(2):
                                    cols = slice(w0 + k * P, w0 + (k + 1) * P)
                                    nc.tensor.matmul(out_ps[:, :], whi[:, q, cols], xhi[:, k, xs], start=k == 0, stop=False)
                                    nc.tensor.matmul(out_ps[:, :], whi[:, q, cols], xlo[:, k, xs], start=False, stop=False)
                                    mm = nc.tensor.matmul(out_ps[:, :], wlo[:, q, cols], xhi[:, k, xs], start=False, stop=k == 1)
                                mm.then_inc(done, 1)
                            if c == 1:
                                down(r, i, q, 0, isinstance(i, int) and q == 0)
                            elif q == 1:
                                down(r, i, 0, 1, isinstance(i, int))
                            elif not isinstance(i, int):
                                down(r, i - 1, 1, 1, False)

                def wst_rows(r, c):
                    return wst[:, (r * UNITS + c) * CH:(r * UNITS + c + 1) * CH]
                tiles_loop(pe, body)
                down(r, IT // 2 - 1, 1, 1, False)
                for t in range(TR):
                    c, j = t // TPC, t % TPC
                    if t % 2 == 0:
                        pe.wait_ge(y_summed, r * 4 + 4)
                        ge(pe, y_final, r * TR + t)
                    for m in range(2):
                        mm = nc.tensor.transpose(ps_t[:, (t % 2) * C + m * P:(t % 2) * C + (m + 1) * P],
                                                 yacc[:, m, r * ROUND + t * P:r * ROUND + (t + 1) * P], ident[:, :])
                    mm.then_inc(y_transposed, 1)

        @block.scalar
        def _(act):
            act.wait_ge(step, NT + 1)
            nc.scalar.activation(shifted[:, :, :], shifted[:, :, :], ACT.Exp).then_inc(exp_done, 1)
            for g in range(NCH):
                act.wait_ge(w_transposed, g + 1)
                nc.scalar.activation(wst[0:64, g * CH:(g + 1) * CH], ps_t[0:64, :], ACT.Copy).then_inc(w_hi, 1)
            for r in range(ROUNDS):
                act.wait_ge(x_loaded, 16 * (r + 1))
                ge(act, up_ready, r * UR)
                for k in range(2):
                    nc.scalar.activation(xhi[:, k, :], xtf[:, k, :], ACT.Copy).then_inc(x_hi, 1)

                def body(i):
                    for q in range(2):
                        act.wait_ge(w_loaded[q], (r * (IT // 2) + i) * 16 + 16)
                        ge(act, down_done, r * UR + i * 4 + 2 * q - 2)
                        nc.scalar.activation(whi[:, q, :], raw[:, q, :], ACT.Copy).then_inc(w_hi_done, 1)
                        for c in range(UNITS):
                            n = r * UR + i * 4 + 2 * q + c
                            act.wait_ge(gate_ready, n + 1)
                            ge(act, h_done, n - 1)
                            nc.scalar.activation(gs[:, c, :], ps_g[:, :], ACT.Silu).then_inc(silu_done, 1)
                            act.wait_ge(h_done, n + 1)
                            nc.scalar.activation(hh[:, c, :], hf[:, c, :], ACT.Copy).then_inc(h_hi, 1)
                tiles_loop(act, body)

        @block.vector
        def _(dve):
            for t in range(NT):
                nc.vector.max(top[:, t, :], logits[:, t, :]).then_inc(step, 1)
            dve.wait_ge(step, NT)
            nc.vector.tensor_tensor(shifted[:, :, :], logits[:, :, :], top[:, :, 0:1].broadcast_to([P, NT, E]), ALU.subtract).then_inc(step, 1)
            for t in range(NT):
                nc.vector.match_replace(rest[:, t, :], top[:, t, :], logits[:, t, :], MASKED * 64).then_inc(step, 1)
            dve.wait_ge(step, 2 * NT + 1)
            nc.vector.tensor_tensor(rest[:, :, :], rest[:, :, :], logits[:, :, :], ALU.not_equal).then_inc(step, 1)
            dve.wait_ge(step, 2 * NT + 2)
            dve.wait_ge(exp_done, 1)
            nc.vector.tensor_tensor(rest[:, :, :], rest[:, :, :], shifted[:, :, :], ALU.mult).then_inc(step, 1)
            dve.wait_ge(step, 2 * NT + 3)
            nc.vector.tensor_reduce(out=total[:, :], in_=rest[:, :, :], axis=AXX, op=ALU.add).then_inc(step, 1)
            dve.wait_ge(step, 2 * NT + 4)
            nc.vector.reciprocal(total[:, :], total[:, :]).then_inc(step, 1)
            dve.wait_ge(step, 2 * NT + 5)
            for half in range(2):
                nc.vector.tensor_tensor(w2[:, :, half * E:(half + 1) * E], rest[:, :, :],
                                        total[:, :].rearrange("p (n o) -> p n o", o=1).broadcast_to([P, NT, E]), ALU.mult).then_inc(step, 1)
            nc.vector.memset(wst[64:P, :].bitcast(F32), 0.0).then_inc(step, 1)
            dve.wait_ge(consts_loaded, 32)
            for g in range(NCH):
                dve.wait_ge(w_hi, g + 1)
                nc.vector.tensor_tensor(wst[32:64, g * CH:(g + 1) * CH], ps_t[32:64, :], wst[32:64, g * CH:(g + 1) * CH].bitcast(F32),
                                        ALU.subtract).then_inc(w_lo, 1)
            for r in range(ROUNDS):
                dve.wait_ge(x_loaded, 16 * (r + 1))
                for k in range(2):
                    dve.wait_ge(x_hi, 2 * r + k + 1)
                    nc.vector.tensor_tensor(xlo[:, k, :], xtf[:, k, :], xhi[:, k, :].bitcast(F32), ALU.subtract).then_inc(x_lo, 1)

                def body(i):
                    for q in range(2):
                        ge(dve, weights_bcast, r * UR + i * 4 + 2 * q - 2)
                        nc.vector.tensor_copy(sel[:, q, :], selraw[:, bass.ts(2 * i + q, P)]).then_inc(sel_ready, 1)
                        dve.wait_ge(w_hi_done, r * IT + 2 * i + q + 1)
                        nc.vector.tensor_tensor(wlo[:, q, :], raw[:, q, :], whi[:, q, :].bitcast(F32), ALU.subtract).then_inc(w_lo_done, 1)
                        for c in range(UNITS):
                            n = r * UR + i * 4 + 2 * q + c
                            dve.wait_ge(silu_done, n + 1)
                            dve.wait_ge(weights_bcast, n + 1)
                            nc.vector.tensor_tensor(gs[:, c, :], gs[:, c, :], ps_w[:, :], ALU.mult).then_inc(gated, 1)
                            dve.wait_ge(gated, n + 1)
                            dve.wait_ge(up_ready, n + 1)
                            ge(dve, h_lo, n - 1)
                            nc.vector.tensor_tensor(hf[:, c, :], gs[:, c, :], ps_u[:, :], ALU.mult).then_inc(h_done, 1)
                tiles_loop(dve, body)
                dve.wait_ge(down_done, (r + 1) * UR)
                for m in range(2):
                    for c in range(UNITS):
                        at = slice(r * ROUND + c * CH, r * ROUND + (c + 1) * CH)
                        nc.vector.tensor_tensor(yacc[:, m, at], yacc[:, m, at], ps_y[m][c][:, :], ALU.add).then_inc(y_summed, 1)
                dve.wait_ge(res_loaded, 16)
                for t in range(0, TR, 2):
                    g = r * TR + t
                    dve.wait_ge(y_transposed, g + 2)
                    for h in range(2):
                        nc.vector.tensor_tensor(yout[:, g + h, :], xres[:, g + h, :], ps_t[:, h * C:(h + 1) * C], ALU.add).then_inc(y_final, 1)

        @block.gpsimd
        def _(pool):
            for r in range(ROUNDS):
                def body(i):
                    for q in range(2):
                        for c in range(UNITS):
                            n = r * UR + i * 4 + 2 * q + c
                            pool.wait_ge(h_hi, n + 1)
                            ge(pool, down_done, n - 1)
                            nc.gpsimd.tensor_tensor(hl[:, c, :], hf[:, c, :], hh[:, c, :].bitcast(F32), ALU.subtract).then_inc(h_lo, 1)
                tiles_loop(pool, body)


def build(nc, d, out):
    ctx = ExitStack()
    with ctx:
        keep = {}
        for name, shape, dt in (("logits", [P, NT, E], F32), ("yacc", [P, 2, N], F32)):
            keep[name] = ctx.enter_context(nc.sbuf_tensor(name, shape, dt))
        with ExitStack() as inner:
            for name, shape, dt in (("q1hi", [P, N], F32R), ("q1lo", [P, N], F32R), ("q2", [P, N], F32R), ("kv", [P, N], F32R),
                                    ("kvn", [P, NT, KVR], F32)):
                keep[name] = inner.enter_context(nc.sbuf_tensor(name, shape, dt))
            for w in ("khi", "klo"):
                keep[w] = [[inner.enter_context(nc.sbuf_tensor(f"{w}{b}{e}", [P, T], F32R)) for e in range(2)] for b in range(B)]
            prepare(nc, d, keep)
            attend(nc, d, keep)
        mix(nc, d, keep, out)


def laid_out(inputs):
    g = {k: np.asarray(v) for k, v in inputs.items()}
    wqd, wkvd = g["L0_attn_wq_down"], g["L0_attn_wkv_down"]
    wl = np.concatenate([wqd, wqd[:, P:], wkvd, wkvd], axis=1)
    wkg = np.concatenate([wkvd, g["L0_ffn_gate_w"].T], axis=1)
    rows = lambda w: np.ascontiguousarray(w.reshape(2, P, -1).transpose(1, 0, 2))
    wqn, wkn = g["L0_attn_wq_nope"], g["L0_attn_wk_nope"]
    wqr, wkr = g["L0_attn_wq_rope"], g["L0_attn_wk_rope"]
    wvu, wo = g["L0_attn_wv_up"], g["L0_attn_wo"]
    a = np.zeros((PAIRS + 1, P, 1024), np.float32)
    b = np.zeros((PAIRS + 1, 96, 1280), np.float32)
    for p in range(PAIRS):
        for e in range(2):
            h = 2 * p + e
            q = wqn[:, h * DN:(h + 1) * DN].T
            a[p, :, 256 * e:256 * e + 192] = q
            a[p, :, 256 * e + 192:256 * e + 256] = q[:, P:]
            a[p, :, 512 + 64 * e:576 + 64 * e] = wkn[:, h * DN:(h + 1) * DN].T
            for half in range(2):
                r = slice(h * D + 96 * half, h * D + 96 * half + 96)
                b[p, :, 128 * e + 64 * half:128 * e + 64 * half + 64] = wvu[:, r].T
                b[p, :, 256 + 512 * e + 256 * half:512 + 512 * e + 256 * half] = wo[r, :]
        r = slice(p * P, (p + 1) * P)
        a[p, :, 640:768] = wqr[0:P, r]
        for k in range(2):
            a[p, 64 * k:64 * k + 64, 768:896] = wqr[P:, r]
            a[p, 64 * k:64 * k + 64, 896:1024] = wkr[:, r]
    turned = lambda w: w.reshape(IT, P, 2, P).transpose(0, 3, 2, 1).reshape(IT, P, 2 * P)
    wd = g["L0_ffn_w_down_proj"].transpose(0, 2, 1).reshape(IT, P, C)
    e = np.concatenate([turned(g["L0_ffn_w_gate_proj"]), turned(g["L0_ffn_w_up_proj"]), wd], axis=2)
    expert = np.arange(IT * P) // I
    sel = (np.arange(P)[:, None] % E == expert[None, :]) & (np.arange(P)[:, None] < 2 * E)
    inv_freq = (1.0 / np.float32(10000.0) ** (np.arange(0, DR, 2, dtype=np.float32) / np.float32(DR))).astype(np.float32)
    freqs = np.outer(inv_freq, np.arange(T, dtype=np.float32)).astype(np.float32)
    pair_rows = np.tile(np.repeat(np.arange(DR // 2), 2), 2)
    cos = np.cos(freqs).astype(np.float32)[pair_rows]
    sin = np.sin(freqs).astype(np.float32)[pair_rows] * np.where(np.arange(P) % 2, 1, -1).astype(np.float32)[:, None]
    mask = np.where(np.arange(P)[:, None] > np.arange(P)[None, :], MASKED, 0.0).astype(np.float32)
    return {
        "x": np.ascontiguousarray(g["L0_attn_x"].reshape(N, C)), "wl": rows(wl), "wkg": rows(wkg), "a": a, "b": b,
        "e": np.ascontiguousarray(e), "sel": sel.astype(np.float32), "cos": np.ascontiguousarray(cos), "sin": np.ascontiguousarray(sin),
        "ident": np.eye(P, dtype=np.float32), "ones": np.ones((P, P), np.float32), "mask": mask,
    }


def kernel(**inputs):
    import concourse.bacc as bacc
    from concourse.bass_utils import run_bass_kernel_spmd
    nc = bacc.Bacc("TRN2", target_bir_lowering=False, num_devices=1)
    arrays = {f"in_{k}": v for k, v in laid_out(inputs).items()}
    d = {k[3:]: nc.dram_tensor(k, v.shape, mybir.dt.from_np(v.dtype), kind="ExternalInput").ap() for k, v in arrays.items()}
    d["xT"] = nc.dram_tensor("xT_scratch", [P, 2, N], F32, kind="Internal").ap()
    out = nc.dram_tensor("out_0", [N, C], F32, kind="ExternalOutput").ap()
    build(nc, d, out)
    r = run_bass_kernel_spmd(nc, [arrays], core_ids=[0])
    return r.results[0]["out_0"].reshape(B, T, C)
```

```python
import numpy as np
import concourse.bass as bass
import concourse.mybir as mybir
from contextlib import ExitStack

F32 = mybir.dt.float32
F32R = mybir.dt.float32r
BF16 = mybir.dt.bfloat16
ALU = mybir.AluOpType
ACT = mybir.ActivationFunctionType
AXX = mybir.AxisListType.X

B, T, C = 2, 1024, 256
N = B * T
H, DN, DR = 16, 128, 64
D = DN + DR
QR, KVR = 192, 64
E, I, TOPK = 32, 96, 8
P = 128
NT = N // P
CH = 512
NCH = N // CH
TPC = CH // P
PAIRS = H // 2
SCALE = 1.0 / D ** 0.5
EPS = 1e-5
MASKED = -float(2 ** 120)
IT = E * I // P
PAIRSWAP = [x ^ 1 for x in range(32)]


def ge(engine, semaphore, value):
    if not isinstance(value, int) or value > 0:
        engine.wait_ge(semaphore, value)


def tensors(nc, ctx, specs):
    return [ctx.enter_context(nc.sbuf_tensor(name, shape, dt)) for name, shape, dt in specs]


def fold_nope(nc, raw_a, out):
    qn = raw_a[:, 0:512].rearrange("p (e n) -> p e n", e=2)
    kn = raw_a[:, 512:640].rearrange("p (e n) -> p e n", e=2)
    for part in range(2):
        for at, e in ((0, 1), (64, 0)):
            mm = nc.tensor.matmul(out[:, part * P + at:part * P + at + 64], qn[:, e, part * P:(part + 1) * P],
                                  kn[:, e, :], start=True, stop=True)
    return mm


def prepare(nc, d, keep):
    ctx = ExitStack()
    with ctx:
        ident = keep["ident"]
        x, xn, wl, wkg, stats, mv, var, std, rinv, tmp = tensors(nc, ctx, [
            ("x", [P, NT, C], F32), ("xn", [P, NT, C], F32),
            ("wl", [P, 2, 3 * P], F32), ("wkg", [P, 2, KVR + E], F32),
            ("stats", [P, NT, 6], F32), ("mv", [P, NT, 2], F32), ("var", [P, NT], F32), ("std", [P, NT], F32),
            ("rinv", [P, NT], F32), ("rtmp", [P, NT], F32)])
        xT, = tensors(nc, ctx, [("xT", [P, 2, N], F32)])
        ps_t = [[ctx.enter_context(nc.psum_tensor(f"ps_t{h}{k}", [P, CH], F32)) for k in range(2)] for h in range(2)]
        ps_l = [ctx.enter_context(nc.psum_tensor(f"ps_l{k}", [P, CH], F32)) for k in range(3)]
        ps_n = ctx.enter_context(nc.psum_tensor("ps_n", [P, CH], F32))
        sem = lambda name: ctx.enter_context(nc.semaphore(name))
        x_loaded = [sem(f"x_loaded{g}") for g in range(NCH)]
        y_zeroed, ident_loaded, consts16_done, folded = sem("y_zeroed"), sem("ident_loaded"), sem("consts16_done"), sem("folded")
        weights_loaded, stats_done, aggregated, norm_step = sem("weights_loaded"), sem("stats_done"), sem("aggregated"), sem("norm_step")
        std_done, normed, transposed, xT_ready = sem("std_done"), sem("normed"), sem("transposed"), sem("xT_ready")
        latent_ready, natural_ready = sem("latent_ready"), sem("natural_ready")
        hi_copied, lo_done, ahead_loaded, xT_stored = sem("hi_copied"), sem("lo_done"), sem("ahead_loaded"), sem("xT_stored")
        block = ctx.enter_context(nc.Block())
        xv = d["x"].rearrange("(n p) c -> p n c", p=P)

        @block.sync
        def _(sp):
            for g in range(NCH):
                sp.dma_start(x[:, g * TPC:(g + 1) * TPC, :], xv[:, g * TPC:(g + 1) * TPC, :]).then_inc(x_loaded[g], 16)
                if g == 0:
                    sp.dma_start(wl[:, :, :], d["wl"]).then_inc(weights_loaded, 16)
                if g == 1:
                    sp.dma_start(wkg[:, :, :], d["wkg"]).then_inc(weights_loaded, 16)
            for name, to in (("cos", keep["cosv"]), ("sin", keep["sinv"]), ("ones", keep["ones"]), ("mask", keep["raw_mask"])):
                sp.dma_start(to[:, :], d[name]).then_inc(ahead_loaded, 16)
            sp.dma_start(keep["raw_a"][:, :], d["a"][0]).then_inc(ahead_loaded, 16)
            sp.dma_start(keep["raw_b"][:, :], d["b"][0]).then_inc(ahead_loaded, 16)
            for g in range(NCH):
                sp.wait_ge(xT_ready, 2 * (g + 1))
                sp.dma_start(d["xT"][:, :, g * CH:(g + 1) * CH], xT[:, :, g * CH:(g + 1) * CH]).then_inc(xT_stored, 16)
            sp.wait_ge(xT_stored, 16 * NCH)
            sp.wait_ge(ahead_loaded, 16 * 6)

        @block.vector
        def _(dve):
            def normalise(g):
                tiles = range(g * TPC, (g + 1) * TPC)
                q = slice(g * TPC, (g + 1) * TPC)
                dve.wait_ge(x_loaded[g], 16)
                for t in tiles:
                    nc.vector.bn_stats(stats[:, t, :], x[:, t, :]).then_inc(stats_done, 1)
                dve.wait_ge(stats_done, TPC * (g + 1))
                for t in tiles:
                    nc.vector.bn_aggr(mv[:, t, :], stats[:, t, :]).then_inc(aggregated, 1)
                dve.wait_ge(aggregated, TPC * (g + 1))
                nc.vector.tensor_scalar(var[:, q], mv[:, q, 1], EPS, None, ALU.add).then_inc(norm_step, 1)
                dve.wait_ge(std_done, g + 1)
                nc.vector.reciprocal(rinv[:, q], std[:, q]).then_inc(norm_step, 1)
                dve.wait_ge(norm_step, 6 * g + 2)
                nc.vector.tensor_tensor(tmp[:, q], rinv[:, q], rinv[:, q], ALU.mult).then_inc(norm_step, 1)
                dve.wait_ge(norm_step, 6 * g + 3)
                nc.vector.tensor_tensor(tmp[:, q], tmp[:, q], var[:, q], ALU.mult).then_inc(norm_step, 1)
                dve.wait_ge(norm_step, 6 * g + 4)
                nc.vector.tensor_scalar(tmp[:, q], tmp[:, q], -0.5, 1.5, ALU.mult, ALU.add).then_inc(norm_step, 1)
                dve.wait_ge(norm_step, 6 * g + 5)
                nc.vector.tensor_tensor(rinv[:, q], rinv[:, q], tmp[:, q], ALU.mult).then_inc(norm_step, 1)
                dve.wait_ge(norm_step, 6 * g + 6)
                for t in tiles:
                    nc.vector.tensor_scalar(xn[:, t, :], x[:, t, :], mv[:, t, 0:1], rinv[:, t:t + 1],
                                            ALU.subtract, ALU.mult).then_inc(normed, 1)

            def low_parts(g):
                s = slice(g * CH, (g + 1) * CH)
                b, c = g // 2, g % 2
                cs = slice(c * CH, (c + 1) * CH)
                for count, lo, ps, hi in (
                        (3, keep["kv"][64:P, s], ps_l[2][64:P, :], keep["kv"][64:P, s]),
                        (3, keep["klo"][b][0][64:P, cs], ps_l[2][64:P, :], keep["khi"][b][0][64:P, cs]),
                        (3, keep["klo"][b][1][0:64, cs], ps_l[2][0:64, :], keep["khi"][b][1][0:64, cs]),
                        (4, keep["q1lo"][:, s], ps_l[0][:, :], keep["q1hi"][:, s]),
                        (5, keep["q2"][64:P, s], ps_l[1][64:P, :], keep["q2"][64:P, s])):
                    dve.wait_ge(hi_copied, 7 * g + count)
                    nc.vector.tensor_tensor(lo, ps, hi.bitcast(F32), ALU.subtract).then_inc(lo_done, 1)

            def split_first_weights():
                dve.wait_ge(ahead_loaded, 16 * 6)
                raw = keep["raw_a"][:, 640:1024]
                nc.vector.tensor_copy(keep["rhi"][:, :], raw).then_inc(keep["a_split"], 1)
                dve.wait_ge(folded, 1)
                nc.vector.tensor_copy(keep["lhi"][:, :], ps_t[0][0][:, 0:256]).then_inc(keep["a_split"], 1)
                dve.wait_ge(keep["a_split"], 2)
                nc.vector.tensor_tensor(keep["rlo"][:, :], raw, keep["rhi"][:, :].bitcast(F32), ALU.subtract).then_inc(keep["a_split"], 1)
                nc.vector.tensor_tensor(keep["llo"][:, :], ps_t[0][0][:, 0:256], keep["lhi"][:, :].bitcast(F32), ALU.subtract).then_inc(keep["a_split"], 1)

            for g in range(NCH):
                normalise(g)
            for g in range(NCH):
                low_parts(g)
                if g == 2:
                    split_first_weights()

        @block.gpsimd
        def _(pool):
            nc.gpsimd.memset(keep["yacc"][:, :, :], 0.0).then_inc(y_zeroed, 1)
            pool.wait_ge(y_zeroed, 1)

        @block.scalar
        def _(act):
            act.dma_start(ident[:, :], d["ident"]).then_inc(ident_loaded, 16)
            def root(g):
                act.wait_ge(norm_step, 6 * g + 1)
                nc.scalar.activation(std[:, g * TPC:(g + 1) * TPC], var[:, g * TPC:(g + 1) * TPC], ACT.Sqrt).then_inc(std_done, 1)

            def take_xT(g):
                act.wait_ge(transposed, 2 * TPC * (g + 1))
                for k in range(2):
                    nc.scalar.activation(xT[:, k, g * CH:(g + 1) * CH], ps_t[g % 2][k][:, :], ACT.Copy).then_inc(xT_ready, 1)

            root(0)
            root(1)
            take_xT(0)
            root(2)
            for g in range(NCH):
                s = slice(g * CH, (g + 1) * CH)
                if g + 1 < NCH:
                    take_xT(g + 1)
                if g == 0:
                    root(3)
                b, c = g // 2, g % 2
                cs = slice(c * CH, (c + 1) * CH)
                act.wait_ge(latent_ready, 3 * g + 1)
                nc.scalar.activation(keep["kv"][:, s], ps_l[2][:, :], ACT.Copy).then_inc(hi_copied, 1)
                nc.scalar.activation(keep["khi"][b][0][64:P, cs], ps_l[2][64:P, :], ACT.Copy).then_inc(hi_copied, 1)
                nc.scalar.activation(keep["khi"][b][1][0:64, cs], ps_l[2][0:64, :], ACT.Copy).then_inc(hi_copied, 1)
                act.wait_ge(latent_ready, 3 * g + 2)
                nc.scalar.activation(keep["q1hi"][:, s], ps_l[0][:, :], ACT.Copy).then_inc(hi_copied, 1)
                act.wait_ge(latent_ready, 3 * g + 3)
                nc.scalar.activation(keep["q2"][:, s], ps_l[1][:, :], ACT.Copy).then_inc(hi_copied, 1)
                if g == 1:
                    act.wait_ge(ident_loaded, 16)
                    act.wait_ge(ahead_loaded, 16 * 6)
                    for to, of in (("ident16", "ident"), ("ones16", "ones"), ("mask16", "raw_mask")):
                        nc.scalar.activation(keep[to][:, :], keep[of][:, :], ACT.Copy).then_inc(consts16_done, 1)
                act.wait_ge(natural_ready, g + 1)
                nat = ps_n[:, 0:TPC * (KVR + E)].rearrange("p (t n) -> p t n", t=TPC)
                nc.scalar.activation(keep["kvn"][:, g * TPC:(g + 1) * TPC, :], nat[:, :, 0:KVR], ACT.Copy).then_inc(hi_copied, 1)
                nc.scalar.activation(keep["logits"][:, g * TPC:(g + 1) * TPC, :], nat[:, :, KVR:KVR + E], ACT.Copy).then_inc(hi_copied, 1)

        @block.tensor
        def _(pe):
            pe.wait_ge(ident_loaded, 16)

            def turn(g):
                ge(pe, xT_ready, 2 * (g - 1))
                for j in range(TPC):
                    t = g * TPC + j
                    pe.wait_ge(normed, t + 1)
                    for k in range(2):
                        nc.tensor.transpose(ps_t[g % 2][k][:, j * P:(j + 1) * P], xn[:, t, k * P:(k + 1) * P], ident[:, :]).then_inc(transposed, 1)

            turn(0)
            pe.wait_ge(weights_loaded, 32)
            for g in range(NCH):
                s = slice(g * CH, (g + 1) * CH)
                if g + 1 < NCH - 1:
                    turn(g + 1)
                pe.wait_ge(xT_ready, 2 * (g + 1))
                for m, lows in ((2, 3), (0, 4), (1, 5)):
                    ge(pe, lo_done, 5 * (g - 1) + lows if g else 0)
                    ge(pe, hi_copied, 7 * (g - 1) + lows if g else 0)
                    for k in range(2):
                        mm = nc.tensor.matmul(ps_l[m][:, :], wl[:, k, m * P:(m + 1) * P], xT[:, k, s], start=k == 0, stop=k == 1)
                    mm.then_inc(latent_ready, 1)
                ge(pe, hi_copied, 7 * g)
                for j in range(TPC):
                    for k in range(2):
                        mm = nc.tensor.matmul(ps_n[:, j * (KVR + E):(j + 1) * (KVR + E)], xT[:, k, (g * TPC + j) * P:(g * TPC + j + 1) * P],
                                              wkg[:, k, :], start=k == 0, stop=k == 1)
                mm.then_inc(natural_ready, 1)
                if g == 1:
                    turn(3)
                    pe.wait_ge(xT_ready, 6)
                    pe.wait_ge(ahead_loaded, 16 * 6)
                    fold_nope(nc, keep["raw_a"], ps_t[0][0]).then_inc(folded, 1)


ROUND = 1024
UNITS = ROUND // CH
SLOTS = 3
UP_AT, DOWN_AT, SEL_AT, TW = C, 2 * C, 3 * C, 3 * C + P


STEPS = 12
PROLOGUE = ["QR0", "KR0", "QR1", "KR1", "QL0", "QL1"]
STAGE = ["QR0", "KR0", "QR1", "KR1", "Lp", "QL0", "QL1", "L0", "Yp0", "Yp1", "B", "WA", "Y0", "Y1"]


def misc_order(first=False, last=False):
    got = []
    for b in range(B):
        for name in STAGE:
            if (name in ("B", "WA") and b) or (first and b == 0 and name in ("Lp", "Yp0", "Yp1")):
                continue
            if last and (name == "WA" or (b and name in PROLOGUE)):
                continue
            got.append((b, name))
    return got


FIRST, LATER, LAST = misc_order(first=True), misc_order(), misc_order(last=True)
AFTER_FIRST = len(PROLOGUE) + len(FIRST)
BEFORE_LAST = AFTER_FIRST + len(LATER) * (PAIRS - 2)


def misc(i, b, name):
    if b is None:
        n = PROLOGUE.index(name)
        return n, n % 2
    if isinstance(i, int) and i == 0:
        n = len(PROLOGUE) + FIRST.index((b, name))
        return n, n % 2
    if isinstance(i, int) and i == PAIRS - 1:
        n = BEFORE_LAST + LAST.index((b, name))
        return n, n % 2
    pos = LATER.index((b, name))
    if isinstance(i, int):
        n = AFTER_FIRST + len(LATER) * (i - 1) + pos
        return n, n % 2
    return i * len(LATER) + (AFTER_FIRST - len(LATER) + pos), (AFTER_FIRST + pos) % 2


def misc_predecessor(i, b, name):
    if b is None:
        at = PROLOGUE.index(name) - 2
        return (0, None, PROLOGUE[at]) if at >= 0 else None
    if isinstance(i, int) and i == 0:
        at = FIRST.index((b, name)) - 2
        return (0, *FIRST[at]) if at >= 0 else (0, None, PROLOGUE[at])
    at = (LAST if isinstance(i, int) and i == PAIRS - 1 else LATER).index((b, name)) - 2
    if at >= 0 and isinstance(i, int) and i == PAIRS - 1:
        return (i, *LAST[at])
    return (i, *LATER[at]) if at >= 0 else (i - 1, *LATER[at])


assert len(LATER) % 2 == 0


def step_of(k):
    c, j = (0, k) if k < TPC else (1, k - TPC)
    return c, j, max(0, j * P - c * CH), j * P >= c * CH


RING = 3


def ring_of(k):
    r = k - 1 if k < TPC else k - 2
    steps = [s for s in range(STEPS) if s not in (0, TPC)]
    if r >= RING:
        return r % RING, steps[r - RING]
    last = max(q for q in range(len(steps)) if q % RING == r % RING)
    return r % RING, steps[last] - STEPS


def pieces():
    got = [(e, t, 0, (t + 1) * P) for e in range(2) for t in range(TPC)]
    for t in range(TPC, 2 * TPC):
        for e in range(2):
            got += [(e, t, 0, CH), (e, t, CH, (t + 1) * P - CH)]
    return got


PIECES = pieces()
NP = len(PIECES)
PIECE_AT = dict(zip([(5, 2), (5, 3)] + [(k, n) for k in (6, 7, 8, 9) for n in range(4)] + [(k, n) for k in (10, 11) for n in range(3)],
                    range(NP)))
assert len(PIECE_AT) == NP
SIDE = {(0, 0): ["QR0"], (0, 1): ["KR0"], (1, 0): ["QR1"], (1, 1): ["KR1"], (2, 0): ["Lp"], (2, 1): ["QL0"], (3, 0): ["QL1"],
        (4, 1): ["L0"], (5, 1): ["Yp0"], (6, 1): ["Yp1"], (7, 0): ["B"], (7, 1): ["WA"], (10, 0): ["Y0"], (10, 1): ["Y1"]}
assert [x for at in sorted(SIDE) for x in SIDE[at]] == STAGE
U = 2 * STEPS
TURNS = {1: (0, 1), 4: (2, 3)}


def is_first(i):
    return isinstance(i, int) and i == 0


def is_last(i, b=None):
    return isinstance(i, int) and i == PAIRS - 1 and b in (None, B - 1)


def attend(nc, d, keep):
    ctx = ExitStack()
    with ctx:
        khi, klo, kvn = keep["khi"], keep["klo"], keep["kvn"]
        qhi, qlo = ([[ctx.enter_context(nc.sbuf_tensor(f"q{w}{b}{e}", [P, T], F32R)) for e in range(2)] for b in range(B)]
                    for w in ("hi", "lo"))
        cosv, sinv, ident, ones, raw_a, raw_b = (keep[n] for n in ("cosv", "sinv", "ident", "ones", "raw_a", "raw_b"))
        ident16, ones16, mask16, rhi, rlo, lhi, llo = (keep[n] for n in ("ident16", "ones16", "mask16", "rhi", "rlo", "lhi", "llo"))
        rest, shifted, top, total = tensors(nc, ctx, [
            ("rest", [P, NT, E], F32), ("shifted", [P, NT, E], F32), ("top", [P, NT, 8], F32), ("total", [P, NT], F32)])
        logits, w2 = keep["logits"], keep["w2"]
        bhi, blo = tensors(nc, ctx, [("bhi", [P, 256], F32R), ("blo", [P, 256], F32R)])
        wst = keep["wst"]
        sh = keep["xtf"][:, :, :].rearrange("p k (g c) -> p (k g) c", c=CH)
        t1, first, ring, shift, oe, rec, on, ohi, olo = tensors(nc, ctx, [
            ("t1", [P, 4, CH], F32), ("first", [P, 2, 2, CH], F32), ("ring", [P, RING, 2, CH], F32),
            ("shift", [P, 2, 2, CH], BF16), ("oe", [P, CH], F32), ("rec", [P, CH], F32), ("on", [P, CH], F32),
            ("ohi", [P, CH], F32R), ("olo", [P, CH], F32R)])
        nm0, nm1, nm1c = tensors(nc, ctx, [("nm0", [P, 8], F32), ("nm1", [P, 2, 8], F32), ("nm1c", [P, 8], F32)])
        yacc = keep["yacc"]
        bank = lambda name: ctx.enter_context(nc.psum_tensor(name, [P, CH], F32))
        ps_s = [bank(f"ps_s{k}") for k in range(3)]
        ps_m = [bank(f"ps_m{k}") for k in range(2)]
        ps_o = bank("ps_o")
        ps_x = [bank(f"ps_x{k}") for k in range(2)]
        sem = lambda name: ctx.enter_context(nc.semaphore(name))
        a_loaded, b_loaded = sem("a_loaded"), sem("b_loaded")
        route_step, route_exp = sem("route_step"), sem("route_exp")
        scores_ready, exp_done, pv_done = sem("scores_ready"), sem("exp_done"), sem("pv_done")
        misc_ready = sem("misc_ready")
        piece_ready, piece_max, halves_joined = sem("piece_ready"), sem("piece_max"), sem("halves_joined")
        shift0_done, shift1_done = sem("shift0_done"), sem("shift1_done")
        a_split, b_split = keep["a_split"], sem("b_split")
        w_transposed = sem("w_transposed")
        rope_in, rope_sin, rope_sum = sem("rope_in"), sem("rope_sin"), sem("rope_sum")
        hi_done, latent_lo, rope_lo = sem("hi_done"), sem("latent_lo"), sem("rope_lo")
        sum_pool, sum_dve = sem("sum_pool"), sem("sum_dve")
        o_copied, rec_done, on_done, ohi_done, olo_done, y_added = (sem("o_copied"), sem("rec_done"), sem("on_done"),
                                                                    sem("ohi_done"), sem("olo_done"), sem("y_added"))
        block = ctx.enter_context(nc.Block())

        def pairs_loop(engine, body):
            body(0)
            with engine.Fori(1, PAIRS - 1) as i:
                body(i)
            body(PAIRS - 1)

        def probs(k, e):
            c, j, off, _ = step_of(k)
            if j == 0:
                return first[:, c, e, off:]
            return ring[:, ring_of(k)[0], e, off:]

        def sums(s, c, j, e):
            return (sum_pool if e else sum_dve), s * 10 + (3 + j if c else j)

        def consumed(i, b, name):
            s = 0 if b is None else i * 2 + b
            t = 0 if b is None else s + 1
            if name in ("QR0", "KR0", "QR1", "KR1"):
                return rope_in, t * 8 + 2 * (2 * int(name[2]) + (name[0] == "K")) + 2
            if name in ("QL0", "QL1"):
                return latent_lo, t * 4 + 2 * int(name[2]) + 2
            if name == "WA":
                return a_split, (0 if b is None else i + 1) * 4 + 4
            if name == "B":
                return b_split, i * 2 + 2
            if name in ("L0", "Lp"):
                return rec_done, s * 2 + (name == "L0")
            return y_added, (s * 4 + int(name[1]) + 1 if name[1] != "p" else (s - 1) * 4 + 2 + int(name[2]) + 1)

        @block.sync
        def _(sp):
            with sp.Fori(0, PAIRS - 1) as i:
                sp.wait_ge(a_split, i * 4 + 4)
                sp.dma_start(raw_a[:, :], d["a"][i + 1]).then_inc(a_loaded, 16)
                sp.wait_ge(b_split, i * 2 + 2)
                sp.dma_start(raw_b[:, :], d["b"][i + 1]).then_inc(b_loaded, 16)
            sp.wait_ge(a_loaded, 16 * (PAIRS - 1))
            sp.wait_ge(b_loaded, 16 * (PAIRS - 1))
            sp.wait_ge(rope_sum, 4 * B * PAIRS)
            sp.dma_start(keep["xtf"][:, :, :], d["xT"][:, :, 0:ROUND]).then_inc(keep["xT_loaded"], 16)
            sp.wait_ge(a_split, 4 * PAIRS)
            sp.wait_ge(rope_in, 8 * B * PAIRS)
            for q in range(2):
                sp.dma_start(keep["raw"][q], d["e"][q]).then_inc(keep["w_loaded"][q], 16)
            sp.wait_ge(keep["xT_loaded"], 16)
            for q in range(2):
                sp.wait_ge(keep["w_loaded"][q], 16)

        @block.tensor
        def _(pe):
            def side(i, b, name, products):
                _, x = misc(i, b, name)
                last = misc_predecessor(i, b, name)
                if last is not None:
                    pe.wait_ge(*consumed(*last))
                products(ps_x[x]).then_inc(misc_ready, 1)

            def fold_a(i, b, p):
                ge(pe, a_loaded, p * 16)
                side(i, b, "WA", lambda out: fold_nope(nc, raw_a, out))

            def fold_b(i, b):
                ge(pe, b_loaded, i * 16)
                vt = raw_b[:, 0:256].rearrange("p (e h n) -> p e h n", e=2, h=2)
                wo = raw_b[:, 256:1280].rearrange("p (e h n) -> p e h n", e=2, h=2)

                def products(out):
                    for e in range(2):
                        for h in range(2):
                            mm = nc.tensor.matmul(out[64 * e:64 * e + 64, 0:C], vt[:, e, h, :], wo[:, e, h, :], start=h == 0, stop=h == 1)
                    return mm
                side(i, b, "B", products)

            def project(i, b, name, p, to_b):
                c = int(name[2])
                s = slice((2 * to_b + c) * CH, (2 * to_b + c + 1) * CH)
                q1h, q1l, q2, kv = (keep[n][:, s] for n in ("q1hi", "q1lo", "q2", "kv"))
                hi, lo = (lhi, llo) if name[:2] == "QL" else (rhi, rlo)
                if name[:2] == "KR":
                    passes = [(rhi[:, 256:384], kv), (rlo[:, 256:384], kv)]
                else:
                    passes = [(hi[:, 0:P], q1h), (hi[:, 0:P], q1l), (hi[:, P:2 * P], q2), (lo[:, P:2 * P], q2), (lo[:, 0:P], q1h)]
                ge(pe, a_split, p * 4 + 4)

                def products(out):
                    for n, (w, x) in enumerate(passes):
                        mm = nc.tensor.matmul(out[:, :], w, x, start=n == 0, stop=n == len(passes) - 1)
                    return mm
                side(i, b, name, products)

            def piece(s, n, b):
                e, t, k0, keys = PIECES[n]
                ge(pe, piece_max, s * NP + n - 1)
                if n == 0:
                    pe.wait_ge(hi_done, s * 12 + 8)
                if n == 8:
                    pe.wait_ge(hi_done, s * 12 + 12)
                out = ps_m[n % 2]
                diagonal = k0 + keys == (t + 1) * P
                mm = nc.tensor.matmul(out[:, 0:keys], qhi[b][e][:, t * P:(t + 1) * P], khi[b][e][:, k0:k0 + keys],
                                      start=True, stop=not diagonal)
                if diagonal:
                    mm = nc.tensor.matmul(out[:, keys - P:keys], mask16[:, :], ident16[:, :], start=False, stop=True)
                mm.then_inc(piece_ready, 1)

            def scores(s, b, k, e):
                c, j, off, diagonal = step_of(k)
                u = s * U + 2 * k + e
                if k == 0 and e == 0:
                    pe.wait_ge(hi_done, s * 12 + 12)
                    pe.wait_ge(latent_lo, s * 4 + 4)
                    pe.wait_ge(rope_lo, s * 8 + 8)
                if k == 0:
                    pe.wait_ge(shift0_done, s * 8 + 8)
                if k == TPC:
                    pe.wait_ge(shift1_done, s * 8 + 8)
                ge(pe, exp_done, u - 2)
                out = ps_s[(2 * k + e) % 3]
                q = slice(c * CH + off, (c + 1) * CH)
                kk = slice(j * P, (j + 1) * P)
                nc.tensor.matmul(out[:, off:], ones16[:, :], shift[:, c, e, off:], start=True, stop=False)
                if diagonal:
                    nc.tensor.matmul(out[:, off:off + P], ident16[:, :], mask16[:, :], start=False, stop=False)
                nc.tensor.matmul(out[:, off:], khi[b][e][:, kk], qhi[b][e][:, q], start=False, stop=False)
                nc.tensor.matmul(out[:, off:], khi[b][e][:, kk], qlo[b][e][:, q], start=False, stop=False)
                nc.tensor.matmul(out[:, off:], klo[b][e][:, kk], qhi[b][e][:, q], start=False, stop=True).then_inc(scores_ready, 1)

            def values(s, b, k):
                c, j, off, _ = step_of(k)
                last = k in (TPC - 1, STEPS - 1)
                if j == 0:
                    ge(pe, o_copied, s * 2 + c)
                for e in range(2):
                    pe.wait_ge(exp_done, s * U + 2 * k + e + 1)
                    nc.tensor.matmul(ps_o[64 * e:64 * e + 64, off:], kvn[:, b * 8 + j, :], probs(k, e),
                                     start=j == 0, stop=last).then_inc(pv_done, 1)

            def turn_weights(chunks):
                pe.wait_ge(route_step, 2 * NT + 6)
                pe.wait_ge(piece_max, B * PAIRS * NP)
                for g in chunks:
                    ge(pe, keep["w_lo"], g - 1)
                    for j in range(TPC):
                        mm = nc.tensor.transpose(ps_m[g % 2][0:2 * E, j * P:(j + 1) * P], w2[:, g * TPC + j, :], ident[:, :])
                    mm.then_inc(w_transposed, 1)

            def row_sums(i, b, name, s, c):
                for e in range(2):
                    pe.wait_ge(*sums(s, c, 7 if c else 3, e))

                def products(out):
                    for e in range(2):
                        mm = nc.tensor.matmul(out[64 * e:64 * e + 64, :], ones[:, 0:64], first[:, c, e, :], start=True, stop=True)
                    return mm
                side(i, b, name, products)

            def project_out(i, b, name, s, c, m):
                pe.wait_ge(b_split, i * 2 + 2 if name[1] != "p" or b else i * 2)
                pe.wait_ge(olo_done, s * 2 + c + 1)

                def products(out):
                    cols = slice(m * P, (m + 1) * P)
                    nc.tensor.matmul(out[:, :], bhi[:, cols], ohi[:, :], start=True, stop=False)
                    nc.tensor.matmul(out[:, :], bhi[:, cols], olo[:, :], start=False, stop=False)
                    return nc.tensor.matmul(out[:, :], blo[:, cols], ohi[:, :], start=False, stop=True)
                side(i, b, name, products)

            def body(i):
                for b in range(B):
                    s = i * 2 + b
                    earlier = b == 1 or not is_first(i)
                    p = i + 1 if b else i
                    for k in range(STEPS):
                        def side_work(half):
                            for name in SIDE.get((k, half), ()):
                                if is_last(i) and (name == "WA" or (b and name in PROLOGUE)):
                                    continue
                                if name in ("B", "WA"):
                                    if b == 0:
                                        fold_b(i, b) if name == "B" else fold_a(i, b, i + 1)
                                elif name == "Lp":
                                    if earlier:
                                        row_sums(i, b, name, s - 1, 1)
                                elif name == "L0":
                                    row_sums(i, b, name, s, 0)
                                elif name[:2] == "Yp":
                                    if earlier:
                                        project_out(i, b, name, s - 1, 1, int(name[2]))
                                elif name[0] == "Y":
                                    project_out(i, b, name, s, 0, int(name[1]))
                                else:
                                    project(i, b, name, p, 1 - b)

                        def maxima(slot):
                            if (k, slot) in PIECE_AT and not is_last(i, b):
                                piece(s + 1, PIECE_AT[k, slot], 1 - b)
                        scores(s, b, k, 0)
                        maxima(0)
                        side_work(0)
                        scores(s, b, k, 1)
                        maxima(1)
                        if k:
                            values(s, b, k - 1)
                        elif earlier:
                            values(s - 1, 1 - b, STEPS - 1)
                        maxima(2)
                        side_work(1)
                        maxima(3)
                        if is_last(i, b) and k in TURNS:
                            turn_weights(TURNS[k])

            for name in PROLOGUE:
                project(0, None, name, 0, 0)
            for n in range(NP):
                piece(0, n, 0)
            pairs_loop(pe, body)
            s = 2 * PAIRS - 1
            values(s, 1, STEPS - 1)
            n = BEFORE_LAST + len(LAST)
            for e in range(2):
                pe.wait_ge(*sums(s, 1, 7, e))
            pe.wait_ge(y_added, s * 4 + 2)
            for e in range(2):
                mm = nc.tensor.matmul(ps_x[n % 2][64 * e:64 * e + 64, :], ones[:, 0:64], first[:, 1, e, :], start=True, stop=True)
            mm.then_inc(misc_ready, 1)
            pe.wait_ge(olo_done, 2 * s + 2)
            for m in range(2):
                out, cols = ps_x[(n + 1 + m) % 2], slice(m * P, (m + 1) * P)
                nc.tensor.matmul(out[:, :], bhi[:, cols], ohi[:, :], start=True, stop=False)
                nc.tensor.matmul(out[:, :], bhi[:, cols], olo[:, :], start=False, stop=False)
                nc.tensor.matmul(out[:, :], blo[:, cols], ohi[:, :], start=False, stop=True).then_inc(misc_ready, 1)

        @block.scalar
        def _(act):
            def exponent(s, k, e):
                c, j, off, _ = step_of(k)
                u = s * U + 2 * k + e
                act.wait_ge(scores_ready, u + 1)
                if j:
                    _, before = ring_of(k)
                    ge(act, pv_done, s * U + 2 * before + e + 1)
                    if before >= 0:
                        cb, jb, _, _ = step_of(before)
                        sb = s
                    else:
                        cb, jb, _, _ = step_of(before + STEPS)
                        sb = s - 1
                    ge(act, *sums(sb, cb, jb, e))
                nc.scalar.activation(probs(k, e), ps_s[(2 * k + e) % 3][:, off:], ACT.Exp, scale=SCALE).then_inc(exp_done, 1)

            def first_free(i, b, c):
                if c == 0:
                    if b == 1:
                        act.wait_ge(misc_ready, misc(i, 0, "L0")[0] + 1)
                    elif not is_first(i):
                        act.wait_ge(misc_ready, misc(i, 0, "QR0")[0] - 2)
                elif b == 1 or not is_first(i):
                    act.wait_ge(misc_ready, misc(i, b, "Lp")[0] + 1)

            def latent_hi(i, b, c, to_b):
                n, x = misc(i, b, f"QL{c}")
                act.wait_ge(misc_ready, n + 1)
                cs = slice(c * CH, (c + 1) * CH)
                nc.scalar.activation(qhi[to_b][1][0:64, cs], ps_x[x][0:64, :], ACT.Copy).then_inc(hi_done, 1)
                nc.scalar.activation(qhi[to_b][0][64:P, cs], ps_x[x][64:P, :], ACT.Copy).then_inc(hi_done, 1)

            def rope_hi(s, c, to_b):
                cs = slice(c * CH, (c + 1) * CH)
                for g, to in ((2 * c, qhi), (2 * c + 1, khi)):
                    act.wait_ge(rope_sum, s * 4 + g + 1)
                    nc.scalar.activation(to[to_b][0][0:64, cs], t1[0:64, g, :], ACT.Copy).then_inc(hi_done, 1)
                    nc.scalar.activation(to[to_b][1][64:P, cs], t1[64:P, g, :], ACT.Copy).then_inc(hi_done, 1)

            def shift_matrix(s, c):
                if c == 0:
                    act.wait_ge(piece_max, s * NP + 8)
                    ge(act, scores_ready, (s - 1) * U + 8)
                else:
                    act.wait_ge(halves_joined, s + 1)
                    ge(act, scores_ready, s * U)
                for e in range(2):
                    for t in range(TPC):
                        m = (nm1c if c else nm0)[:, e * TPC + t:e * TPC + t + 1]
                        nc.scalar.activation(shift[:, c, e, t * P:(t + 1) * P], ident[:, :], ACT.Copy, scale=m).then_inc(
                            shift1_done if c else shift0_done, 1)

            def copy_out(s, c):
                act.wait_ge(pv_done, s * U + (U if c else 8))
                ge(act, on_done, s * 2 + c)
                nc.scalar.activation(oe[:, :], ps_o[:, :], ACT.Copy).then_inc(o_copied, 1)

            def out_hi(s, c, last_y):
                act.wait_ge(on_done, s * 2 + c + 1)
                if last_y is not None:
                    act.wait_ge(misc_ready, last_y + 1)
                nc.scalar.activation(ohi[:, :], on[:, :], ACT.Copy).then_inc(ohi_done, 1)

            def body(i):
                for b in range(B):
                    s = i * 2 + b
                    earlier = b == 1 or not is_first(i)
                    for k in range(STEPS):
                        if k in (0, TPC):
                            first_free(i, b, k // TPC)
                        exponent(s, k, 0)
                        if k == 3 and not is_last(i, b):
                            latent_hi(i, b, 0, 1 - b)
                        exponent(s, k, 1)
                        if k == 0 and earlier:
                            copy_out(s - 1, 1)
                        if k == 1:
                            shift_matrix(s, 1)
                        if k == 3:
                            if not is_last(i, b):
                                latent_hi(i, b, 1, 1 - b)
                                rope_hi(s + 1, 0, 1 - b)
                            if earlier:
                                last = misc(i, 0, "Y1")[0] if b else misc(i, 0, "QR0")[0] - 1
                                out_hi(s - 1, 1, last)
                        if k == 4:
                            copy_out(s, 0)
                        if k == 5 and not is_last(i, b):
                            rope_hi(s + 1, 1, 1 - b)
                        if k == 7:
                            out_hi(s, 0, misc(i, b, "Yp1")[0] if earlier else None)
                        if k == 8 and not is_last(i, b):
                            shift_matrix(s + 1, 0)
                        if is_last(i, b) and k - 1 in TURNS:
                            for g in TURNS[k - 1]:
                                act.wait_ge(w_transposed, g + 1)
                                nc.scalar.activation(wst[0:2 * E, g * CH:(g + 1) * CH], ps_m[g % 2][0:2 * E, :], ACT.Copy).then_inc(keep["w_hi"], 1)
                        if is_last(i, b) and k in (6, 7):
                            act.wait_ge(keep["xT_loaded"], 16)
                            nc.scalar.activation(keep["xhi"][k - 6][:, 0:ROUND], keep["xtf"][:, k - 6, :], ACT.Copy).then_inc(keep["x_hi"], 1)
                        if is_last(i, b) and k == 8:
                            act.wait_ge(keep["w_loaded"][0], 16)
                            nc.scalar.activation(keep["whi"][0], keep["raw"][0], ACT.Copy).then_inc(keep["expert_hi"], 1)
                        if k == 6 and b == 0 and not earlier:
                            act.wait_ge(route_step, NT + 1)
                            nc.scalar.activation(shifted[:, :, :], shifted[:, :, :], ACT.Exp).then_inc(route_exp, 1)

            for c in range(2):
                latent_hi(0, None, c, 0)
            for c in range(2):
                rope_hi(0, c, 0)
            shift_matrix(0, 0)
            pairs_loop(act, body)
            s = 2 * PAIRS - 1
            copy_out(s, 1)
            out_hi(s, 1, BEFORE_LAST + len(LAST) - 1)

        @block.vector
        def _(dve):
            def rope_products(i, b, name, g, s):
                n, x = misc(i, b, name)
                c = g // 2
                ge(dve, rope_lo, (s - 1) * 8 + 2 * g + 2)
                dve.wait_ge(misc_ready, n + 1)
                nc.vector.tensor_tensor(t1[:, g, :], ps_x[x][:, :], cosv[:, c * CH:(c + 1) * CH], ALU.mult).then_inc(rope_in, 1)
                nc.vector.stream_shuffle(sh[:, g, :], ps_x[x][:, :], PAIRSWAP).then_inc(rope_in, 1)

            def latent_low(i, b, c, s, to_b):
                _, x = misc(i, b, f"QL{c}")
                cs = slice(c * CH, (c + 1) * CH)
                dve.wait_ge(hi_done, s * 12 + 2 * c + 2)
                nc.vector.tensor_tensor(qlo[to_b][1][0:64, cs], ps_x[x][0:64, :], qhi[to_b][1][0:64, cs].bitcast(F32),
                                        ALU.subtract).then_inc(latent_lo, 1)
                nc.vector.tensor_tensor(qlo[to_b][0][64:P, cs], ps_x[x][64:P, :], qhi[to_b][0][64:P, cs].bitcast(F32),
                                        ALU.subtract).then_inc(latent_lo, 1)

            def split_a(i, b, p):
                n, x = misc(i, b, "WA")
                ge(dve, a_loaded, p * 16)
                nc.vector.tensor_copy(rhi[:, :], raw_a[:, 640:1024]).then_inc(a_split, 1)
                dve.wait_ge(misc_ready, n + 1)
                nc.vector.tensor_copy(lhi[:, :], ps_x[x][:, 0:256]).then_inc(a_split, 1)
                dve.wait_ge(a_split, p * 4 + 2)
                nc.vector.tensor_tensor(rlo[:, :], raw_a[:, 640:1024], rhi[:, :].bitcast(F32), ALU.subtract).then_inc(a_split, 1)
                nc.vector.tensor_tensor(llo[:, :], ps_x[x][:, 0:256], lhi[:, :].bitcast(F32), ALU.subtract).then_inc(a_split, 1)

            def split_b(i, b):
                n, x = misc(i, b, "B")
                dve.wait_ge(misc_ready, n + 1)
                nc.vector.tensor_copy(bhi[:, :], ps_x[x][:, 0:256]).then_inc(b_split, 1)
                dve.wait_ge(b_split, i * 2 + 1)
                nc.vector.tensor_tensor(blo[:, :], ps_x[x][:, 0:256], bhi[:, :].bitcast(F32), ALU.subtract).then_inc(b_split, 1)

            def join_halves(s):
                dve.wait_ge(piece_max, s * NP + NP)
                ge(dve, shift1_done, s * 8)
                nc.vector.tensor_tensor(nm1c[:, :], nm1[:, 0, :], nm1[:, 1, :], ALU.min).then_inc(halves_joined, 1)

            def maximum(s, n):
                e, t, k0, keys = PIECES[n]
                dve.wait_ge(piece_ready, s * NP + n + 1)
                if n == 0:
                    ge(dve, shift0_done, s * 8)
                if n == 8:
                    ge(dve, halves_joined, s)
                col = e * TPC + t % TPC
                to = nm0[:, col:col + 1] if t < TPC else nm1[:, int(k0 > 0), col:col + 1]
                nc.vector.tensor_reduce(out=to, in_=ps_m[n % 2][:, 0:keys], axis=AXX, op=ALU.max, negate=True).then_inc(piece_max, 1)

            def add_probs(s, k):
                c, j, off, _ = step_of(k)
                dve.wait_ge(exp_done, s * U + 2 * k + 1)
                if j == 1:
                    dve.wait_ge(pv_done, s * U + 2 * (k - 1) + 1)
                else:
                    dve.wait_ge(*sums(s, c, j - 1, 0))
                nc.vector.tensor_tensor(first[:, c, 0, off:], first[:, c, 0, off:], probs(k, 0), ALU.add).then_inc(sum_dve, 1)

            def normalise(n, x, s, c):
                dve.wait_ge(misc_ready, n + 1)
                ge(dve, on_done, s * 2 + c)
                nc.vector.reciprocal(rec[:, :], ps_x[x][:, :]).then_inc(rec_done, 1)
                dve.wait_ge(rec_done, s * 2 + c + 1)
                dve.wait_ge(o_copied, s * 2 + c + 1)
                ge(dve, olo_done, s * 2 + c)
                nc.vector.tensor_tensor(on[:, :], oe[:, :], rec[:, :], ALU.mult).then_inc(on_done, 1)

            def add_out(n, x, s, b, c, m):
                dve.wait_ge(misc_ready, n + 1)
                ge(dve, y_added, s * 4 + 2 * c + m - 4)
                at = slice(b * T + c * CH, b * T + (c + 1) * CH)
                nc.vector.tensor_tensor(yacc[:, m, at], yacc[:, m, at], ps_x[x][:, :], ALU.add).then_inc(y_added, 1)

            def rope(i, b, c, s):
                for g, name in ((2 * c, f"QR{c}"), (2 * c + 1, f"KR{c}")):
                    rope_products(i, b, name, g, s)

            def body(i):
                for b in range(B):
                    s = i * 2 + b
                    earlier = b == 1 or not is_first(i)
                    for k in range(STEPS):
                        if k == 0:
                            join_halves(s)
                        if k < 2 and not is_last(i, b):
                            rope(i, b, k, s + 1)
                        if k == 2 and earlier:
                            normalise(*misc(i, b, "Lp"), s - 1, 1)
                        if k in (3, 4) and not is_last(i, b):
                            latent_low(i, b, k - 3, s + 1, 1 - b)
                        if is_last(i, b) and k - 2 in TURNS:
                            for g in TURNS[k - 2]:
                                at = slice(g * CH, (g + 1) * CH)
                                dve.wait_ge(keep["w_hi"], g + 1)
                                nc.vector.tensor_tensor(wst[E:2 * E, at], ps_m[g % 2][E:2 * E, :], wst[E:2 * E, at].bitcast(F32),
                                                        ALU.subtract).then_inc(keep["w_lo"], 1)
                        if k == 7 and b == 0:
                            split_b(i, b)
                        if k == 4 and is_first(i):
                            route_weights() if b else route_choice()
                        for slot in range(4):
                            if (k, slot) in PIECE_AT and not is_last(i, b):
                                maximum(s + 1, PIECE_AT[k, slot])
                            if slot == 2:
                                if k in (5, 6) and earlier:
                                    add_out(*misc(i, b, f"Yp{k - 5}"), s - 1, 1 - b, 1, k - 5)
                                if k == 7 and b == 0 and not is_last(i):
                                    split_a(i, b, i + 1)
                            if k == 10 and slot in (0, 2):
                                add_out(*misc(i, b, f"Y{slot // 2}"), s, b, 0, slot // 2)
                        if k % TPC or k > TPC:
                            add_probs(s, k)
                        if k == 4:
                            normalise(*misc(i, b, "L0"), s, 0)

            def route_choice():
                for t in range(NT):
                    nc.vector.max(top[:, t, :], logits[:, t, :]).then_inc(route_step, 1)
                dve.wait_ge(route_step, NT)
                nc.vector.tensor_tensor(shifted[:, :, :], logits[:, :, :], top[:, :, 0:1].broadcast_to([P, NT, E]),
                                        ALU.subtract).then_inc(route_step, 1)
                for t in range(NT):
                    nc.vector.match_replace(rest[:, t, :], top[:, t, :], logits[:, t, :], MASKED * 64).then_inc(route_step, 1)

            def route_weights():
                dve.wait_ge(route_step, 2 * NT + 1)
                nc.vector.tensor_tensor(rest[:, :, :], rest[:, :, :], logits[:, :, :], ALU.not_equal).then_inc(route_step, 1)
                dve.wait_ge(route_step, 2 * NT + 2)
                dve.wait_ge(route_exp, 1)
                nc.vector.tensor_tensor(rest[:, :, :], rest[:, :, :], shifted[:, :, :], ALU.mult).then_inc(route_step, 1)
                dve.wait_ge(route_step, 2 * NT + 3)
                nc.vector.tensor_reduce(out=total[:, :], in_=rest[:, :, :], axis=AXX, op=ALU.add).then_inc(route_step, 1)
                dve.wait_ge(route_step, 2 * NT + 4)
                nc.vector.reciprocal(total[:, :], total[:, :]).then_inc(route_step, 1)
                dve.wait_ge(route_step, 2 * NT + 5)
                for half in range(2):
                    nc.vector.tensor_tensor(w2[:, :, half * E:(half + 1) * E], rest[:, :, :],
                                            total[:, :].rearrange("p (n o) -> p n o", o=1).broadcast_to([P, NT, E]),
                                            ALU.mult).then_inc(route_step, 1)

            for c in range(2):
                rope(0, None, c, 0)
            for c in range(2):
                latent_low(0, None, c, 0, 0)
            for n in range(NP):
                maximum(0, n)
            pairs_loop(dve, body)
            s = 2 * PAIRS - 1
            n = BEFORE_LAST + len(LAST)
            normalise(n, n % 2, s, 1)
            for m in range(2):
                add_out(n + 1 + m, (n + 1 + m) % 2, s, 1, 1, m)

        @block.gpsimd
        def _(pool):
            def rope_sum_of(s, g):
                c = g // 2
                pool.wait_ge(rope_in, s * 8 + 2 * g + 2)
                nc.gpsimd.tensor_tensor(sh[:, g, :], sh[:, g, :], sinv[:, c * CH:(c + 1) * CH], ALU.mult).then_inc(rope_sin, 1)
                pool.wait_ge(rope_sin, s * 4 + g + 1)
                nc.gpsimd.tensor_tensor(t1[:, g, :], t1[:, g, :], sh[:, g, :], ALU.add).then_inc(rope_sum, 1)

            def rope_low(s, g, to_b, before):
                c = g // 2
                cs = slice(c * CH, (c + 1) * CH)
                hi, lo = (khi, klo) if g % 2 else (qhi, qlo)
                pool.wait_ge(*before)
                pool.wait_ge(rope_sum, s * 4 + g + 1)
                pool.wait_ge(hi_done, s * 12 + 4 + 2 * (g + 1))
                for e, rows in ((0, slice(0, 64)), (1, slice(64, P))):
                    ge(pool, rope_lo, s * 8 + 2 * g + e)
                    nc.gpsimd.tensor_tensor(lo[to_b][e][rows, cs], t1[rows, g, :], hi[to_b][e][rows, cs].bitcast(F32),
                                            ALU.subtract).then_inc(rope_lo, 1)
                pool.wait_ge(rope_lo, s * 8 + 2 * g + 2)

            def add_probs(s, k):
                c, j, off, _ = step_of(k)
                pool.wait_ge(exp_done, s * U + 2 * k + 2)
                if j == 1:
                    pool.wait_ge(pv_done, s * U + 2 * (k - 1) + 2)
                else:
                    pool.wait_ge(*sums(s, c, j - 1, 1))
                nc.gpsimd.tensor_tensor(first[:, c, 1, off:], first[:, c, 1, off:], probs(k, 1), ALU.add).then_inc(sum_pool, 1)

            def out_low(s, c):
                pool.wait_ge(ohi_done, s * 2 + c + 1)
                nc.gpsimd.tensor_tensor(olo[:, :], on[:, :], ohi[:, :].bitcast(F32), ALU.subtract).then_inc(olo_done, 1)

            def body(i):
                for b in range(B):
                    s = i * 2 + b
                    earlier = b == 1 or not is_first(i)
                    if is_last(i, b):
                        pool.wait_ge(*sums(s - 1, 1, 7, 1))
                        nc.gpsimd.memset(wst[2 * E:P, :].bitcast(F32), 0.0).then_inc(keep["zeroed"], 1)
                        pool.wait_ge(keep["zeroed"], 1)
                    else:
                        rope_sum_of(s + 1, 0)
                        rope_sum_of(s + 1, 1)
                    for k in range(1, TPC):
                        add_probs(s, k)
                        if k < 3 and not is_last(i, b):
                            rope_sum_of(s + 1, k + 1)
                    if earlier:
                        out_low(s - 1, 1)
                    for k in range(TPC + 1, STEPS):
                        add_probs(s, k)
                        if k == 7:
                            out_low(s, 0)
                            before = (olo_done, s * 2 + 1)
                        else:
                            before = sums(s, 1, k - TPC, 1)
                        if is_last(i, b) and k in (8, 9):
                            pool.wait_ge(keep["x_hi"], k - 7)
                            nc.gpsimd.tensor_tensor(keep["xlo"][k - 8][:, 0:ROUND], keep["xtf"][:, k - 8, :],
                                                    keep["xhi"][k - 8][:, 0:ROUND].bitcast(F32), ALU.subtract).then_inc(keep["x_lo"], 1)
                        if is_last(i, b) and k == 10:
                            pool.wait_ge(keep["expert_hi"], 1)
                            nc.gpsimd.tensor_tensor(keep["wlo"][0], keep["raw"][0][:, 0:SEL_AT], keep["whi"][0][:, 0:SEL_AT].bitcast(F32),
                                                    ALU.subtract).then_inc(keep["expert_lo"], 1)
                        if k in (5, 6, 8, 9) and not is_last(i, b):
                            rope_low(s + 1, k - 5 if k < 7 else k - 6, 1 - b, before)

            for g in range(4):
                rope_sum_of(0, g)
            for g in range(4):
                rope_low(0, g, 0, (rope_sum, 4))
            pairs_loop(pool, body)
            out_low(2 * PAIRS - 1, 1)




def mix(nc, d, keep, out):
    ctx = ExitStack()
    with ctx:
        yacc, w2, ident = keep["yacc"], keep["w2"], keep["ident"]
        xtf, xhi, xlo, wst = (keep[name] for name in ("xtf", "xhi", "xlo", "wst"))
        raw, whi, wlo = (list(keep[name]) for name in ("raw", "whi", "wlo"))
        for held, name, width, dt in ((raw, "raw", TW, F32), (whi, "whi", TW, F32R), (wlo, "wlo", SEL_AT, F32R)):
            for q in range(len(held), SLOTS):
                held.append(ctx.enter_context(nc.sbuf_tensor(f"{name}{q}", [P, width], dt))[:, :])
        xres, yout = tensors(nc, ctx, [
            ("xres", [P, NT, C], F32), ("yout", [P, NT, C], F32)])
        gs, hf, hh, hl = tensors(nc, ctx, [
            ("gs", [P, 2, CH], F32), ("hf", [P, 2, CH], F32), ("hh", [P, 2, CH], F32R), ("hl", [P, 2, CH], F32R)])
        bank = lambda name: ctx.enter_context(nc.psum_tensor(name, [P, CH], F32))
        ps_y = [[bank(f"ps_y{m}{c}") for c in range(UNITS)] for m in range(2)]
        ps_g, ps_u, ps_w, ps_t = bank("ps_g"), bank("ps_u"), bank("ps_w"), bank("ps_tr")
        sem = lambda name: ctx.enter_context(nc.semaphore(name))
        x_loaded, res_loaded, w_loaded = keep["xT_loaded"], sem("res_loaded"), keep["w_loaded"]
        x_hi, x_lo, expert_hi, expert_lo, w_lo, zeroed = (keep[n] for n in ("x_hi", "x_lo", "expert_hi", "expert_lo", "w_lo", "zeroed"))
        weights_bcast, gate_ready, up_ready, silu_done, gated, h_done, h_hi, h_lo, down_done = (
            sem("weights_bcast"), sem("gate_ready"), sem("up_ready"), sem("silu_done"), sem("gated"), sem("h_done"),
            sem("h_hi"), sem("h_lo"), sem("down_done"))
        y_summed, y_transposed, y_final, stored = sem("y_summed"), sem("y_transposed"), sem("y_final"), sem("stored")
        block = ctx.enter_context(nc.Block())
        UR = IT * UNITS
        ROUNDS = N // ROUND
        TR = ROUND // P
        xv = d["x"].rearrange("(n p) c -> p n c", p=P)
        ov = out.rearrange("(n p) c -> p n c", p=P)

        def tiles_loop(engine, body):
            body(0)
            with engine.Fori(1, IT // SLOTS) as i:
                body(i)

        @block.sync
        def _(sp):
            for q in range(2, SLOTS):
                sp.dma_start(raw[q], d["e"][q]).then_inc(w_loaded[q], 16)
            for r in range(ROUNDS):
                def body(i):
                    for q in range(SLOTS):
                        sp.wait_ge(expert_lo, i * SLOTS + (r * IT + q + 1))
                        sp.dma_start(raw[q], d["e"][i * SLOTS + (q + SLOTS)]).then_inc(w_loaded[q], 16)
                    if isinstance(i, int) and r + 1 < ROUNDS:
                        sp.wait_ge(x_lo, 2 * (r + 1))
                        sp.dma_start(xtf[:, :, :], d["xT"][:, :, (r + 1) * ROUND:(r + 2) * ROUND]).then_inc(x_loaded, 16)
                        sp.dma_start(xres[:, :, :], xv).then_inc(res_loaded, 16)
                    if isinstance(i, int) and r:
                        sp.wait_ge(y_final, r * TR)
                        sp.dma_start(ov[:, (r - 1) * TR:r * TR, :], yout[:, (r - 1) * TR:r * TR, :]).then_inc(stored, 16)
                tiles_loop(sp, body)
            at = (ROUNDS - 1) * TR
            for half in range(2):
                tiles = slice(at + half * (TR // 2), at + (half + 1) * (TR // 2))
                sp.wait_ge(y_final, tiles.stop)
                sp.dma_start(ov[:, tiles, :], yout[:, tiles, :]).then_inc(stored, 16)
            sp.wait_ge(stored, 16 * (ROUNDS + 1))
            for q in range(SLOTS):
                sp.wait_ge(w_loaded[q], 16 * (1 + ROUNDS * (IT // SLOTS)))

        @block.tensor
        def _(pe):
            pe.wait_ge(w_lo, NCH)
            pe.wait_ge(zeroed, 1)

            def down(r, i, q, c, first):
                pe.wait_ge(h_lo, i * (SLOTS * UNITS) + (r * UR + q * UNITS + c + 1))
                if first:
                    ge(pe, y_summed, r * 4)
                for m in range(2):
                    cols = slice(DOWN_AT + m * P, DOWN_AT + (m + 1) * P)
                    nc.tensor.matmul(ps_y[m][c][:, :], whi[q][:, cols], hh[:, c, :], start=first, stop=False, skip_group_check=True)
                    nc.tensor.matmul(ps_y[m][c][:, :], whi[q][:, cols], hl[:, c, :], start=False, stop=False, skip_group_check=True)
                    mm = nc.tensor.matmul(ps_y[m][c][:, :], wlo[q][:, cols], hh[:, c, :], start=False, stop=True, skip_group_check=True)
                mm.then_inc(down_done, 1)

            def turn_back(r):
                for t in range(TR):
                    if t % 2 == 0:
                        pe.wait_ge(y_summed, r * 4 + 2 * (t // TPC) + 2)
                        ge(pe, y_final, r * TR + t)
                    for m in range(2):
                        mm = nc.tensor.transpose(ps_t[:, (t % 2) * C + m * P:(t % 2) * C + (m + 1) * P],
                                                 yacc[:, m, r * ROUND + t * P:r * ROUND + (t + 1) * P], ident[:, :])
                    mm.then_inc(y_transposed, 1)

            for r in range(ROUNDS):
                pe.wait_ge(x_lo, 2 * r + 2)

                def body(i):
                    for q in range(SLOTS):
                        for c in range(UNITS):
                            n = i * (SLOTS * UNITS) + (r * UR + q * UNITS + c)
                            tokens = slice((r * UNITS + c) * CH, (r * UNITS + c + 1) * CH)
                            if c == 0:
                                pe.wait_ge(expert_lo, i * SLOTS + (r * IT + q + 1))
                            ge(pe, gated, n)
                            nc.tensor.matmul(ps_w[:, :], whi[q][:, SEL_AT:TW], wst[:, tokens], start=True, stop=True).then_inc(weights_bcast, 1)
                            for out_ps, w0, done in ((ps_g, 0, gate_ready), (ps_u, UP_AT, up_ready)):
                                if done is up_ready:
                                    ge(pe, h_done, n)
                                for k in range(2):
                                    cols = slice(w0 + k * P, w0 + (k + 1) * P)
                                    nc.tensor.matmul(out_ps[:, :], whi[q][:, cols], xhi[k][:, tokens], start=k == 0, stop=False)
                                    nc.tensor.matmul(out_ps[:, :], whi[q][:, cols], xlo[k][:, tokens], start=False, stop=False)
                                    mm = nc.tensor.matmul(out_ps[:, :], wlo[q][:, cols], xhi[k][:, tokens], start=False, stop=k == 1)
                                mm.then_inc(done, 1)
                            if c:
                                down(r, i, q, c - 1, isinstance(i, int) and q == 0)
                            elif q:
                                down(r, i, q - 1, UNITS - 1, isinstance(i, int) and q == 1)
                            elif not isinstance(i, int):
                                down(r, i - 1, SLOTS - 1, UNITS - 1, False)
                    if isinstance(i, int) and r:
                        turn_back(r - 1)
                tiles_loop(pe, body)
                down(r, IT // SLOTS - 1, SLOTS - 1, UNITS - 1, False)
            turn_back(ROUNDS - 1)

        @block.scalar
        def _(act):
            def split_x(r):
                act.wait_ge(x_loaded, 16 * (r + 1))
                for k in range(2):
                    nc.scalar.activation(xhi[k][:, r * ROUND:(r + 1) * ROUND], xtf[:, k, :], ACT.Copy).then_inc(x_hi, 1)

            def split_weights(turn, q, n):
                act.wait_ge(w_loaded[q], turn * 16 + 16)
                ge(act, down_done, n * UNITS - UNITS * (SLOTS - 1))
                nc.scalar.activation(whi[q], raw[q], ACT.Copy).then_inc(expert_hi, 1)

            for r in range(ROUNDS):
                def body(i):
                    for q in range(SLOTS):
                        for c in range(UNITS):
                            n = i * (SLOTS * UNITS) + (r * UR + q * UNITS + c)
                            act.wait_ge(gate_ready, n + 1)
                            ge(act, h_done, n - 1)
                            nc.scalar.activation(gs[:, c, :], ps_g[:, :], ACT.Silu).then_inc(silu_done, 1)
                            if c == 0:
                                split_weights(i + (r * (IT // SLOTS) + (q == SLOTS - 1)), (q + 1) % SLOTS, i * SLOTS + (r * IT + q + 1))
                            act.wait_ge(h_done, n + 1)
                            nc.scalar.activation(hh[:, c, :], hf[:, c, :], ACT.Copy).then_inc(h_hi, 1)
                    if isinstance(i, int) and r + 1 < ROUNDS:
                        split_x(r + 1)
                tiles_loop(act, body)

        @block.vector
        def _(dve):
            def split_x(r):
                for k in range(2):
                    dve.wait_ge(x_hi, 2 * r + k + 1)
                    at = slice(r * ROUND, (r + 1) * ROUND)
                    nc.vector.tensor_tensor(xlo[k][:, at], xtf[:, k, :], xhi[k][:, at].bitcast(F32), ALU.subtract).then_inc(x_lo, 1)

            def split_weights(q, n):
                dve.wait_ge(expert_hi, n + 1)
                nc.vector.tensor_tensor(wlo[q], raw[q][:, 0:SEL_AT], whi[q][:, 0:SEL_AT].bitcast(F32), ALU.subtract).then_inc(expert_lo, 1)

            def add_residual(r):
                dve.wait_ge(res_loaded, 16)
                for t in range(0, TR, 2):
                    dve.wait_ge(y_transposed, r * TR + t + 2)
                    for h in range(2):
                        n = r * TR + t + h
                        nc.vector.tensor_tensor(yout[:, n, :], xres[:, n, :], ps_t[:, h * C:(h + 1) * C], ALU.add).then_inc(y_final, 1)

            for r in range(ROUNDS):
                def body(i):
                    for q in range(SLOTS):
                        for c in range(UNITS):
                            n = i * (SLOTS * UNITS) + (r * UR + q * UNITS + c)
                            dve.wait_ge(silu_done, n + 1)
                            dve.wait_ge(weights_bcast, n + 1)
                            nc.vector.tensor_tensor(gs[:, c, :], gs[:, c, :], ps_w[:, :], ALU.mult).then_inc(gated, 1)
                            dve.wait_ge(gated, n + 1)
                            dve.wait_ge(up_ready, n + 1)
                            ge(dve, h_lo, n - 1)
                            nc.vector.tensor_tensor(hf[:, c, :], gs[:, c, :], ps_u[:, :], ALU.mult).then_inc(h_done, 1)
                            if c == 0:
                                split_weights((q + 1) % SLOTS, i * SLOTS + (r * IT + q + 1))
                    if isinstance(i, int) and r + 1 < ROUNDS:
                        split_x(r + 1)
                    if isinstance(i, int) and r:
                        add_residual(r - 1)
                tiles_loop(dve, body)
                for c in range(UNITS):
                    dve.wait_ge(down_done, (r + 1) * UR - (UNITS - 1 - c))
                    for m in range(2):
                        at = slice(r * ROUND + c * CH, r * ROUND + (c + 1) * CH)
                        nc.vector.tensor_tensor(yacc[:, m, at], yacc[:, m, at], ps_y[m][c][:, :], ALU.add).then_inc(y_summed, 1)
            add_residual(ROUNDS - 1)

        @block.gpsimd
        def _(pool):
            for r in range(ROUNDS):
                def body(i):
                    for q in range(SLOTS):
                        for c in range(UNITS):
                            n = i * (SLOTS * UNITS) + (r * UR + q * UNITS + c)
                            pool.wait_ge(h_hi, n + 1)
                            ge(pool, down_done, n - 1)
                            nc.gpsimd.tensor_tensor(hl[:, c, :], hf[:, c, :], hh[:, c, :].bitcast(F32), ALU.subtract).then_inc(h_lo, 1)
                tiles_loop(pool, body)


def build(nc, d, out):
    ctx = ExitStack()
    with ctx:
        keep = {}
        for name, shape, dt in (("ident", [P, P], F32), ("w2", [P, NT, 2 * E], F32), ("yacc", [P, 2, N], F32),
                                ("q1hi", [P, N], F32R), ("q1lo", [P, N], F32R), ("q2", [P, N], F32R), ("kv", [P, N], F32R),
                                ("keys0", [P, 4, T], F32R), ("xtf", [P, 2, ROUND], F32),
                                ("cosv", [P, T], F32), ("raw_a", [P, 1024], F32)):
            keep[name] = ctx.enter_context(nc.sbuf_tensor(name, shape, dt))
        keep["xhi"], keep["xlo"] = (keep["q1hi"], keep["q1lo"]), (keep["q2"], keep["kv"])
        keep["wst"] = keep["keys0"][:, 0:2, :].rearrange("p k n -> p (k n)")
        keep["raw"] = [keep[name][:, 0:TW] for name in ("raw_a", "cosv")]
        keep["whi"], keep["wlo"] = [keep["keys0"][:, 2, 0:TW]], [keep["keys0"][:, 3, 0:SEL_AT]]
        assert T >= TW and N == 2 * T
        for name in ("xT_loaded", "x_hi", "x_lo", "expert_hi", "expert_lo", "w_hi", "w_lo", "zeroed"):
            keep[name] = ctx.enter_context(nc.semaphore(name))
        keep["w_loaded"] = [ctx.enter_context(nc.semaphore(f"w_loaded{q}")) for q in range(SLOTS)]
        with ExitStack() as inner:
            for name, shape, dt in (("kvn", [P, NT, KVR], F32), ("logits", [P, NT, E], F32), ("sinv", [P, T], F32),
                                    ("ones", [P, P], F32), ("raw_mask", [P, P], F32), ("raw_b", [96, 1280], F32),
                                    ("ident16", [P, P], BF16), ("ones16", [P, P], BF16), ("mask16", [P, P], BF16),
                                    ("rhi", [P, 384], F32R), ("rlo", [P, 384], F32R), ("lhi", [P, 256], F32R), ("llo", [P, 256], F32R)):
                keep[name] = inner.enter_context(nc.sbuf_tensor(name, shape, dt))
            for w in ("khi", "klo"):
                keep[w] = [[keep["keys0"][:, 2 * (w == "klo") + e, :] for e in range(2)]]
                keep[w] += [[inner.enter_context(nc.sbuf_tensor(f"{w}{b}{e}", [P, T], F32R)) for e in range(2)] for b in range(1, B)]
            keep["a_split"] = inner.enter_context(nc.semaphore("a_split"))
            prepare(nc, d, keep)
            attend(nc, d, keep)
        mix(nc, d, keep, out)


def laid_out(inputs):
    g = {k: np.asarray(v) for k, v in inputs.items()}
    wqd, wkvd = g["L0_attn_wq_down"], g["L0_attn_wkv_down"]
    wl = np.concatenate([wqd, wqd[:, P:], wkvd, wkvd], axis=1)
    wkg = np.concatenate([wkvd, g["L0_ffn_gate_w"].T], axis=1)
    rows = lambda w: np.ascontiguousarray(w.reshape(2, P, -1).transpose(1, 0, 2))
    wqn, wkn = g["L0_attn_wq_nope"], g["L0_attn_wk_nope"]
    wqr, wkr = g["L0_attn_wq_rope"], g["L0_attn_wk_rope"]
    wvu, wo = g["L0_attn_wv_up"], g["L0_attn_wo"]
    a = np.zeros((PAIRS, P, 1024), np.float32)
    b = np.zeros((PAIRS, 96, 1280), np.float32)
    for p in range(PAIRS):
        for e in range(2):
            h = 2 * p + e
            q = wqn[:, h * DN:(h + 1) * DN].T
            a[p, :, 256 * e:256 * e + 192] = q
            a[p, :, 256 * e + 192:256 * e + 256] = q[:, P:]
            a[p, :, 512 + 64 * e:576 + 64 * e] = wkn[:, h * DN:(h + 1) * DN].T
            for half in range(2):
                r = slice(h * D + 96 * half, h * D + 96 * half + 96)
                b[p, :, 128 * e + 64 * half:128 * e + 64 * half + 64] = wvu[:, r].T
                b[p, :, 256 + 512 * e + 256 * half:512 + 512 * e + 256 * half] = wo[r, :]
        r = slice(p * P, (p + 1) * P)
        a[p, :, 640:768] = wqr[0:P, r]
        for k in range(2):
            a[p, 64 * k:64 * k + 64, 768:896] = wqr[P:, r]
            a[p, 64 * k:64 * k + 64, 896:1024] = wkr[:, r]
    turned = lambda w: w.reshape(IT, P, 2, P).transpose(0, 3, 2, 1).reshape(IT, P, 2 * P)
    wd = g["L0_ffn_w_down_proj"].transpose(0, 2, 1).reshape(IT, P, C)
    expert = (np.arange(IT * P) // I).reshape(IT, 1, P)
    row = np.arange(P)[None, :, None]
    sel = ((row % E == expert) & (row < 2 * E)).astype(np.float32)
    e = np.concatenate([turned(g["L0_ffn_w_gate_proj"]), turned(g["L0_ffn_w_up_proj"]), wd, sel], axis=2)
    e = np.concatenate([e, e[:SLOTS]], axis=0)
    inv_freq = (1.0 / np.float32(10000.0) ** (np.arange(0, DR, 2, dtype=np.float32) / np.float32(DR))).astype(np.float32)
    freqs = np.outer(inv_freq, np.arange(T, dtype=np.float32)).astype(np.float32)
    pair_rows = np.tile(np.repeat(np.arange(DR // 2), 2), 2)
    cos = np.cos(freqs).astype(np.float32)[pair_rows]
    sin = np.sin(freqs).astype(np.float32)[pair_rows] * np.where(np.arange(P) % 2, 1, -1).astype(np.float32)[:, None]
    mask = np.where(np.arange(P)[:, None] > np.arange(P)[None, :], MASKED, 0.0).astype(np.float32)
    return {
        "x": np.ascontiguousarray(g["L0_attn_x"].reshape(N, C)), "wl": rows(wl), "wkg": rows(wkg), "a": a, "b": b,
        "e": np.ascontiguousarray(e), "cos": np.ascontiguousarray(cos), "sin": np.ascontiguousarray(sin),
        "ident": np.eye(P, dtype=np.float32), "ones": np.ones((P, P), np.float32), "mask": mask,
    }


def kernel(**inputs):
    import concourse.bacc as bacc
    from concourse.bass_utils import run_bass_kernel_spmd
    nc = bacc.Bacc("TRN2", target_bir_lowering=False, num_devices=1)
    arrays = {f"in_{k}": v for k, v in laid_out(inputs).items()}
    d = {k[3:]: nc.dram_tensor(k, v.shape, mybir.dt.from_np(v.dtype), kind="ExternalInput").ap() for k, v in arrays.items()}
    d["xT"] = nc.dram_tensor("xT_scratch", [P, 2, N], F32, kind="Internal").ap()
    out = nc.dram_tensor("out_0", [N, C], F32, kind="ExternalOutput").ap()
    build(nc, d, out)
    r = run_bass_kernel_spmd(nc, [arrays], core_ids=[0])
    return r.results[0]["out_0"].reshape(B, T, C)
```

```python
import numpy as np
import concourse.bass as bass
import concourse.mybir as mybir
from contextlib import ExitStack

F32 = mybir.dt.float32
F32R = mybir.dt.float32r
BF16 = mybir.dt.bfloat16
ALU = mybir.AluOpType
ACT = mybir.ActivationFunctionType
AXX = mybir.AxisListType.X

B, T, C = 2, 1024, 256
N = B * T
H, DN, DR = 16, 128, 64
D = DN + DR
QR, KVR = 192, 64
E, I, TOPK = 32, 96, 8
P = 128
NT = N // P
CH = 512
NCH = N // CH
TPC = CH // P
PAIRS = H // 2
SCALE = 1.0 / D ** 0.5
EPS = 1e-5
MASKED = -float(2 ** 120)
IT = E * I // P
PAIRSWAP = [x ^ 1 for x in range(32)]


def ge(engine, semaphore, value):
    if not isinstance(value, int) or value > 0:
        engine.wait_ge(semaphore, value)


def tensors(nc, ctx, specs):
    return [ctx.enter_context(nc.sbuf_tensor(name, shape, dt)) for name, shape, dt in specs]


def fold_nope(nc, raw_a, out):
    qn = raw_a[:, 0:512].rearrange("p (e n) -> p e n", e=2)
    kn = raw_a[:, 512:640].rearrange("p (e n) -> p e n", e=2)
    for part in range(2):
        for at, e in ((0, 1), (64, 0)):
            mm = nc.tensor.matmul(out[:, part * P + at:part * P + at + 64], qn[:, e, part * P:(part + 1) * P],
                                  kn[:, e, :], start=True, stop=True)
    return mm


def prepare(nc, d, keep):
    ctx = ExitStack()
    with ctx:
        ident = keep["ident"]
        x, xn, wl, wkg, stats, mv, var, std, rinv, tmp = tensors(nc, ctx, [
            ("x", [P, NT, C], F32), ("xn", [P, NT, C], F32),
            ("wl", [P, 2, 3 * P], F32), ("wkg", [P, 2, KVR + E], F32),
            ("stats", [P, NT, 6], F32), ("mv", [P, NT, 2], F32), ("var", [P, NT], F32), ("std", [P, NT], F32),
            ("rinv", [P, NT], F32), ("rtmp", [P, NT], F32)])
        xT, = tensors(nc, ctx, [("xT", [P, 2, N], F32)])
        ps_t = [[ctx.enter_context(nc.psum_tensor(f"ps_t{h}{k}", [P, CH], F32)) for k in range(2)] for h in range(2)]
        ps_l = [ctx.enter_context(nc.psum_tensor(f"ps_l{k}", [P, CH], F32)) for k in range(3)]
        ps_n = ctx.enter_context(nc.psum_tensor("ps_n", [P, CH], F32))
        sem = lambda name: ctx.enter_context(nc.semaphore(name))
        x_loaded = [sem(f"x_loaded{g}") for g in range(NCH)]
        wkg_loaded = sem("wkg_loaded")
        y_zeroed, ident_loaded, consts16_done, folded = sem("y_zeroed"), sem("ident_loaded"), sem("consts16_done"), sem("folded")
        weights_loaded, stats_done, aggregated, norm_step = sem("weights_loaded"), sem("stats_done"), sem("aggregated"), sem("norm_step")
        std_done, normed, transposed, xT_ready = sem("std_done"), sem("normed"), sem("transposed"), sem("xT_ready")
        latent_ready, natural_ready = sem("latent_ready"), sem("natural_ready")
        hi_copied, lo_done, ahead_loaded, xT_stored = sem("hi_copied"), sem("lo_done"), sem("ahead_loaded"), sem("xT_stored")
        block = ctx.enter_context(nc.Block())
        xv = d["x"].rearrange("(n p) c -> p n c", p=P)

        @block.sync
        def _(sp):
            for g in range(NCH):
                sp.dma_start(x[:, g * TPC:(g + 1) * TPC, :], xv[:, g * TPC:(g + 1) * TPC, :]).then_inc(x_loaded[g], 16)
                if g == 0:
                    sp.dma_start(wl[:, :, :], d["wl"]).then_inc(weights_loaded, 16)
                if g == 1:
                    sp.dma_start(wkg[:, :, :], d["wkg"]).then_inc(wkg_loaded, 16)
            for name, to in (("cos", keep["cosv"]), ("sin", keep["sinv"]), ("ones", keep["ones"]), ("mask", keep["raw_mask"])):
                sp.dma_start(to[:, :], d[name]).then_inc(ahead_loaded, 16)
            sp.dma_start(keep["raw_a"][:, :], d["a"][0]).then_inc(ahead_loaded, 16)
            sp.dma_start(keep["raw_b"][:, :], d["b"][0]).then_inc(ahead_loaded, 16)
            for g in range(NCH):
                sp.wait_ge(xT_ready, 2 * (g + 1))
                sp.dma_start(d["xT"][:, :, g * CH:(g + 1) * CH], xT[:, :, g * CH:(g + 1) * CH]).then_inc(xT_stored, 16)
            sp.wait_ge(xT_stored, 16 * NCH)
            sp.wait_ge(ahead_loaded, 16 * 6)

        @block.vector
        def _(dve):
            def normalise(g):
                tiles = range(g * TPC, (g + 1) * TPC)
                q = slice(g * TPC, (g + 1) * TPC)
                dve.wait_ge(x_loaded[g], 16)
                for t in tiles:
                    nc.vector.bn_stats(stats[:, t, :], x[:, t, :]).then_inc(stats_done, 1)
                dve.wait_ge(stats_done, TPC * (g + 1))
                for t in tiles:
                    nc.vector.bn_aggr(mv[:, t, :], stats[:, t, :]).then_inc(aggregated, 1)
                dve.wait_ge(aggregated, TPC * (g + 1))
                nc.vector.tensor_scalar(var[:, q], mv[:, q, 1], EPS, None, ALU.add).then_inc(norm_step, 1)
                dve.wait_ge(std_done, g + 1)
                nc.vector.reciprocal(rinv[:, q], std[:, q]).then_inc(norm_step, 1)
                dve.wait_ge(norm_step, 6 * g + 2)
                nc.vector.tensor_tensor(tmp[:, q], rinv[:, q], rinv[:, q], ALU.mult).then_inc(norm_step, 1)
                dve.wait_ge(norm_step, 6 * g + 3)
                nc.vector.tensor_tensor(tmp[:, q], tmp[:, q], var[:, q], ALU.mult).then_inc(norm_step, 1)
                dve.wait_ge(norm_step, 6 * g + 4)
                nc.vector.tensor_scalar(tmp[:, q], tmp[:, q], -0.5, 1.5, ALU.mult, ALU.add).then_inc(norm_step, 1)
                dve.wait_ge(norm_step, 6 * g + 5)
                nc.vector.tensor_tensor(rinv[:, q], rinv[:, q], tmp[:, q], ALU.mult).then_inc(norm_step, 1)
                dve.wait_ge(norm_step, 6 * g + 6)
                for t in tiles:
                    nc.vector.tensor_scalar(xn[:, t, :], x[:, t, :], mv[:, t, 0:1], rinv[:, t:t + 1],
                                            ALU.subtract, ALU.mult).then_inc(normed, 1)

            def low_parts(g):
                s = slice(g * CH, (g + 1) * CH)
                b, c = g // 2, g % 2
                cs = slice(c * CH, (c + 1) * CH)
                for count, lo, ps, hi in (
                        (3, keep["kv"][64:P, s], ps_l[2][64:P, :], keep["kv"][64:P, s]),
                        (3, keep["klo"][b][0][64:P, cs], ps_l[2][64:P, :], keep["khi"][b][0][64:P, cs]),
                        (3, keep["klo"][b][1][0:64, cs], ps_l[2][0:64, :], keep["khi"][b][1][0:64, cs]),
                        (4, keep["q1lo"][:, s], ps_l[0][:, :], keep["q1hi"][:, s]),
                        (5, keep["q2"][64:P, s], ps_l[1][64:P, :], keep["q2"][64:P, s])):
                    dve.wait_ge(hi_copied, 7 * g + count)
                    nc.vector.tensor_tensor(lo, ps, hi.bitcast(F32), ALU.subtract).then_inc(lo_done, 1)

            def split_first_weights():
                dve.wait_ge(ahead_loaded, 16 * 6)
                raw = keep["raw_a"][:, 640:1024]
                nc.vector.tensor_copy(keep["rhi"][:, :], raw).then_inc(keep["a_split"], 1)
                dve.wait_ge(folded, 1)
                nc.vector.tensor_copy(keep["lhi"][:, :], ps_t[0][0][:, 0:256]).then_inc(keep["a_split"], 1)
                dve.wait_ge(keep["a_split"], 2)
                nc.vector.tensor_tensor(keep["rlo"][:, :], raw, keep["rhi"][:, :].bitcast(F32), ALU.subtract).then_inc(keep["a_split"], 1)
                nc.vector.tensor_tensor(keep["llo"][:, :], ps_t[0][0][:, 0:256], keep["lhi"][:, :].bitcast(F32), ALU.subtract).then_inc(keep["a_split"], 1)

            for g in range(NCH):
                normalise(g)
            for g in range(NCH):
                low_parts(g)
                if g == 2:
                    split_first_weights()

        @block.gpsimd
        def _(pool):
            nc.gpsimd.memset(keep["yacc"][:, :, :], 0.0).then_inc(y_zeroed, 1)
            pool.wait_ge(y_zeroed, 1)

        @block.scalar
        def _(act):
            act.dma_start(ident[:, :], d["ident"]).then_inc(ident_loaded, 16)
            def root(g):
                act.wait_ge(norm_step, 6 * g + 1)
                nc.scalar.activation(std[:, g * TPC:(g + 1) * TPC], var[:, g * TPC:(g + 1) * TPC], ACT.Sqrt).then_inc(std_done, 1)

            def take_xT(g):
                act.wait_ge(transposed, 2 * TPC * (g + 1))
                for k in range(2):
                    nc.scalar.activation(xT[:, k, g * CH:(g + 1) * CH], ps_t[g % 2][k][:, :], ACT.Copy).then_inc(xT_ready, 1)

            root(0)
            root(1)
            take_xT(0)
            root(2)
            for g in range(NCH):
                s = slice(g * CH, (g + 1) * CH)
                if g + 1 < NCH:
                    take_xT(g + 1)
                if g == 0:
                    root(3)
                b, c = g // 2, g % 2
                cs = slice(c * CH, (c + 1) * CH)
                act.wait_ge(latent_ready, 3 * g + 1)
                nc.scalar.activation(keep["kv"][:, s], ps_l[2][:, :], ACT.Copy).then_inc(hi_copied, 1)
                nc.scalar.activation(keep["khi"][b][0][64:P, cs], ps_l[2][64:P, :], ACT.Copy).then_inc(hi_copied, 1)
                nc.scalar.activation(keep["khi"][b][1][0:64, cs], ps_l[2][0:64, :], ACT.Copy).then_inc(hi_copied, 1)
                act.wait_ge(latent_ready, 3 * g + 2)
                nc.scalar.activation(keep["q1hi"][:, s], ps_l[0][:, :], ACT.Copy).then_inc(hi_copied, 1)
                act.wait_ge(latent_ready, 3 * g + 3)
                nc.scalar.activation(keep["q2"][:, s], ps_l[1][:, :], ACT.Copy).then_inc(hi_copied, 1)
                if g == 1:
                    act.wait_ge(ident_loaded, 16)
                    act.wait_ge(ahead_loaded, 16 * 6)
                    for to, of in (("ident16", "ident"), ("ones16", "ones"), ("mask16", "raw_mask")):
                        nc.scalar.activation(keep[to][:, :], keep[of][:, :], ACT.Copy).then_inc(consts16_done, 1)
                act.wait_ge(natural_ready, g + 1)
                nat = ps_n[:, 0:TPC * (KVR + E)].rearrange("p (t n) -> p t n", t=TPC)
                nc.scalar.activation(keep["kvn"][:, g * TPC:(g + 1) * TPC, :], nat[:, :, 0:KVR], ACT.Copy).then_inc(hi_copied, 1)
                nc.scalar.activation(keep["logits"][:, g * TPC:(g + 1) * TPC, :], nat[:, :, KVR:KVR + E], ACT.Copy).then_inc(hi_copied, 1)

        @block.tensor
        def _(pe):
            pe.wait_ge(ident_loaded, 16)

            def turn(g):
                ge(pe, xT_ready, 2 * (g - 1))
                for j in range(TPC):
                    t = g * TPC + j
                    pe.wait_ge(normed, t + 1)
                    for k in range(2):
                        nc.tensor.transpose(ps_t[g % 2][k][:, j * P:(j + 1) * P], xn[:, t, k * P:(k + 1) * P], ident[:, :]).then_inc(transposed, 1)

            turn(0)
            pe.wait_ge(weights_loaded, 16)
            for g in range(NCH):
                s = slice(g * CH, (g + 1) * CH)
                if g + 1 < NCH - 1:
                    turn(g + 1)
                pe.wait_ge(xT_ready, 2 * (g + 1))
                for m, lows in ((2, 3), (0, 4), (1, 5)):
                    ge(pe, lo_done, 5 * (g - 1) + lows if g else 0)
                    ge(pe, hi_copied, 7 * (g - 1) + lows if g else 0)
                    for k in range(2):
                        mm = nc.tensor.matmul(ps_l[m][:, :], wl[:, k, m * P:(m + 1) * P], xT[:, k, s], start=k == 0, stop=k == 1)
                    mm.then_inc(latent_ready, 1)
                pe.wait_ge(wkg_loaded, 16)
                ge(pe, hi_copied, 7 * g)
                for j in range(TPC):
                    for k in range(2):
                        mm = nc.tensor.matmul(ps_n[:, j * (KVR + E):(j + 1) * (KVR + E)], xT[:, k, (g * TPC + j) * P:(g * TPC + j + 1) * P],
                                              wkg[:, k, :], start=k == 0, stop=k == 1)
                mm.then_inc(natural_ready, 1)
                if g == 1:
                    turn(3)
                    pe.wait_ge(xT_ready, 6)
                    pe.wait_ge(ahead_loaded, 16 * 6)
                    fold_nope(nc, keep["raw_a"], ps_t[0][0]).then_inc(folded, 1)


ROUND = 1024
UNITS = ROUND // CH
SLOTS = 3
UP_AT, DOWN_AT, TW = C, 2 * C, 3 * C
TURN_EXPERTS = SLOTS * P // I
assert TURN_EXPERTS * I == SLOTS * P and IT % SLOTS == 0


def load_routing(sp, d, to, slot, turn, loaded):
    for expert in range(slot * P // I, (slot * P + P - 1) // I + 1):
        first, end = max(0, expert * I - slot * P), min(P, (expert + 1) * I - slot * P)
        source = d["wT"][bass.ds(turn * TURN_EXPERTS + expert, 1), :].broadcast_to([end - first, ROUND])
        sp.dma_start(to[first:end, :], source).then_inc(loaded, 16)


ROUTED = 16 * 2


STEPS = 12
PROLOGUE = ["QR0", "KR0", "QL0", "QR1", "KR1", "QL1"]
STAGE = ["QR0", "KR0", "QR1", "KR1", "Lp", "QL0", "QL1", "L0", "Yp0", "Yp1", "B", "WA", "Y0", "Y1"]


def misc_order(first=False, last=False):
    got = []
    for b in range(B):
        for name in STAGE:
            if (name in ("B", "WA") and b) or (first and b == 0 and name in ("Lp", "Yp0", "Yp1")):
                continue
            if last and (name == "WA" or (b and name in PROLOGUE)):
                continue
            got.append((b, name))
    return got


FIRST, LATER, LAST = misc_order(first=True), misc_order(), misc_order(last=True)
AFTER_FIRST = len(PROLOGUE) + len(FIRST)
BEFORE_LAST = AFTER_FIRST + len(LATER) * (PAIRS - 2)


def misc(i, b, name):
    if b is None:
        n = PROLOGUE.index(name)
        return n, n % 2
    if isinstance(i, int) and i == 0:
        n = len(PROLOGUE) + FIRST.index((b, name))
        return n, n % 2
    if isinstance(i, int) and i == PAIRS - 1:
        n = BEFORE_LAST + LAST.index((b, name))
        return n, n % 2
    pos = LATER.index((b, name))
    if isinstance(i, int):
        n = AFTER_FIRST + len(LATER) * (i - 1) + pos
        return n, n % 2
    return i * len(LATER) + (AFTER_FIRST - len(LATER) + pos), (AFTER_FIRST + pos) % 2


def misc_predecessor(i, b, name):
    if b is None:
        at = PROLOGUE.index(name) - 2
        return (0, None, PROLOGUE[at]) if at >= 0 else None
    if isinstance(i, int) and i == 0:
        at = FIRST.index((b, name)) - 2
        return (0, *FIRST[at]) if at >= 0 else (0, None, PROLOGUE[at])
    at = (LAST if isinstance(i, int) and i == PAIRS - 1 else LATER).index((b, name)) - 2
    if at >= 0 and isinstance(i, int) and i == PAIRS - 1:
        return (i, *LAST[at])
    return (i, *LATER[at]) if at >= 0 else (i - 1, *LATER[at])


assert len(LATER) % 2 == 0


def step_of(k):
    c, j = (0, k) if k < TPC else (1, k - TPC)
    return c, j, max(0, j * P - c * CH), j * P >= c * CH


RING = 3


def ring_of(k):
    r = k - 1 if k < TPC else k - 2
    steps = [s for s in range(STEPS) if s not in (0, TPC)]
    if r >= RING:
        return r % RING, steps[r - RING]
    last = max(q for q in range(len(steps)) if q % RING == r % RING)
    return r % RING, steps[last] - STEPS


def pieces():
    got = [(e, t, 0, (t + 1) * P) for e in range(2) for t in range(TPC)]
    for t in range(TPC, 2 * TPC):
        for e in range(2):
            got += [(e, t, 0, CH), (e, t, CH, (t + 1) * P - CH)]
    return got


PIECES = pieces()
NP = len(PIECES)
PIECE_AT = dict(zip([(5, 3)] + [(k, n) for k in (6, 7, 8, 9, 10) for n in range(4)] + [(11, n) for n in range(3)],
                    range(NP)))
assert len(PIECE_AT) == NP
SIDE = {(0, 0): ["QR0"], (0, 1): ["KR0"], (1, 0): ["QR1"], (1, 1): ["KR1"], (2, 0): ["Lp"], (2, 1): ["QL0"], (3, 1): ["QL1"],
        (4, 1): ["L0"], (6, 0): ["Yp0"], (6, 1): ["Yp1"], (7, 0): ["B"], (7, 1): ["WA"], (10, 0): ["Y0"], (10, 1): ["Y1"]}
assert [x for at in sorted(SIDE) for x in SIDE[at]] == STAGE
U = 2 * STEPS
TURNS = {1: (0, 1), 4: (2, 3)}


def is_first(i):
    return isinstance(i, int) and i == 0


def is_last(i, b=None):
    return isinstance(i, int) and i == PAIRS - 1 and b in (None, B - 1)


def attend(nc, d, keep):
    ctx = ExitStack()
    with ctx:
        khi, klo, kvn = keep["khi"], keep["klo"], keep["kvn"]
        qhi, qlo = ([[ctx.enter_context(nc.sbuf_tensor(f"q{w}{b}{e}", [P, T], F32R)) for e in range(2)] for b in range(B)]
                    for w in ("hi", "lo"))
        cosv, sinv, ident, ones, raw_a, raw_b = (keep[n] for n in ("cosv", "sinv", "ident", "ones", "raw_a", "raw_b"))
        ident16, ones16, mask16, rhi, rlo, lhi, llo = (keep[n] for n in ("ident16", "ones16", "mask16", "rhi", "rlo", "lhi", "llo"))
        rest, shifted, top, total = tensors(nc, ctx, [
            ("rest", [P, NT, E], F32), ("shifted", [P, NT, E], F32), ("top", [P, NT, 8], F32), ("total", [P, NT], F32)])
        logits, w2 = keep["logits"], keep["w2"]
        bhi, blo = tensors(nc, ctx, [("bhi", [P, 256], F32R), ("blo", [P, 256], F32R)])
        sh = keep["xtf"][:, :, :].rearrange("p k (g c) -> p (k g) c", c=CH)
        t1, first, ring, shift, oe, rec, on, ohi, olo = tensors(nc, ctx, [
            ("t1", [P, 4, CH], F32), ("first", [P, 2, 2, CH], F32), ("ring", [P, RING, 2, CH], F32),
            ("shift", [P, 2, 2, CH], BF16), ("oe", [P, CH], F32), ("rec", [P, CH], F32), ("on", [P, CH], F32),
            ("ohi", [P, CH], F32R), ("olo", [P, CH], F32R)])
        wst = t1[0:E, :, :].rearrange("p g c -> p (g c)")
        nm0, nm1, nm1c = tensors(nc, ctx, [("nm0", [P, 8], F32), ("nm1", [P, 2, 8], F32), ("nm1c", [P, 8], F32)])
        yacc = keep["yacc"]
        bank = lambda name: ctx.enter_context(nc.psum_tensor(name, [P, CH], F32))
        ps_s = [bank(f"ps_s{k}") for k in range(3)]
        ps_m = [bank(f"ps_m{k}") for k in range(2)]
        ps_m5 = ps_m + ps_s
        ps_o = bank("ps_o")
        ps_x = [bank(f"ps_x{k}") for k in range(2)]
        sem = lambda name: ctx.enter_context(nc.semaphore(name))
        a_loaded, b_loaded = sem("a_loaded"), sem("b_loaded")
        route_step, route_exp = sem("route_step"), sem("route_exp")
        scores_ready, exp_done, pv_done = sem("scores_ready"), sem("exp_done"), sem("pv_done")
        misc_ready = sem("misc_ready")
        piece_ready, piece_max, halves_joined = sem("piece_ready"), sem("piece_max"), sem("halves_joined")
        shift0_done, shift1_done = sem("shift0_done"), sem("shift1_done")
        a_split, b_split = keep["a_split"], sem("b_split")
        w_transposed, w_rows, w_stored = sem("w_transposed"), sem("w_rows"), sem("w_stored")
        rope_in, rope_sin, rope_sum = sem("rope_in"), sem("rope_sin"), sem("rope_sum")
        hi_done, latent_lo, rope_lo = sem("hi_done"), sem("latent_lo"), sem("rope_lo")
        sum_pool, sum_dve = sem("sum_pool"), sem("sum_dve")
        o_copied, rec_done, on_done, ohi_done, olo_done, y_added = (sem("o_copied"), sem("rec_done"), sem("on_done"),
                                                                    sem("ohi_done"), sem("olo_done"), sem("y_added"))
        block = ctx.enter_context(nc.Block())

        def pairs_loop(engine, body):
            body(0)
            with engine.Fori(1, PAIRS - 1) as i:
                body(i)
            body(PAIRS - 1)

        def probs(k, e):
            c, j, off, _ = step_of(k)
            if j == 0:
                return first[:, c, e, off:]
            return ring[:, ring_of(k)[0], e, off:]

        def sums(s, c, j, e):
            return (sum_pool if e else sum_dve), s * 10 + (3 + j if c else j)

        def consumed(i, b, name):
            s = 0 if b is None else i * 2 + b
            t = 0 if b is None else s + 1
            if name in ("QR0", "KR0", "QR1", "KR1"):
                return rope_in, t * 8 + 2 * (2 * int(name[2]) + (name[0] == "K")) + 2
            if name in ("QL0", "QL1"):
                return latent_lo, t * 4 + 2 * int(name[2]) + 2
            if name == "WA":
                return a_split, (0 if b is None else i + 1) * 4 + 4
            if name == "B":
                return b_split, i * 2 + 2
            if name in ("L0", "Lp"):
                return rec_done, s * 2 + (name == "L0")
            return y_added, (s * 4 + int(name[1]) + 1 if name[1] != "p" else (s - 1) * 4 + 2 + int(name[2]) + 1)

        @block.sync
        def _(sp):
            with sp.Fori(0, PAIRS - 1) as i:
                sp.wait_ge(a_split, i * 4 + 4)
                sp.dma_start(raw_a[:, :], d["a"][i + 1]).then_inc(a_loaded, 16)
                sp.wait_ge(b_split, i * 2 + 2)
                sp.dma_start(raw_b[:, :], d["b"][i + 1]).then_inc(b_loaded, 16)
            sp.wait_ge(a_loaded, 16 * (PAIRS - 1))
            sp.wait_ge(b_loaded, 16 * (PAIRS - 1))
            sp.wait_ge(rope_sum, 4 * B * PAIRS)
            sp.dma_start(keep["xtf"][:, :, :], d["xT"][:, :, 0:ROUND]).then_inc(keep["xT_loaded"], 16)
            sp.wait_ge(a_split, 4 * PAIRS)
            sp.wait_ge(rope_in, 8 * B * PAIRS)
            for q in range(2):
                sp.dma_start(keep["raw"][q], d["e"][q]).then_inc(keep["w_loaded"][q], 16)
            sp.wait_ge(w_rows, NCH)
            for r in range(N // ROUND):
                sp.dma_start(d["wT"][r * E:(r + 1) * E, :], wst[:, r * ROUND:(r + 1) * ROUND]).then_inc(w_stored, 16)
            sp.dma_start(d["wT"][N // ROUND * E:, :], wst[0:TURN_EXPERTS, 0:ROUND]).then_inc(w_stored, 16)
            sp.wait_ge(w_stored, 16 * (N // ROUND + 1))
            load_routing(sp, d, keep["routing"][0], 0, 0, keep["routing_loaded"][0])
            sp.wait_ge(keep["xT_loaded"], 16)
            for q in range(2):
                sp.wait_ge(keep["w_loaded"][q], 16)
            sp.wait_ge(keep["routing_loaded"][0], ROUTED)

        @block.tensor
        def _(pe):
            def side(i, b, name, products):
                _, x = misc(i, b, name)
                last = misc_predecessor(i, b, name)
                if last is not None:
                    pe.wait_ge(*consumed(*last))
                products(ps_x[x]).then_inc(misc_ready, 1)

            def fold_a(i, b, p):
                ge(pe, a_loaded, p * 16)
                side(i, b, "WA", lambda out: fold_nope(nc, raw_a, out))

            def fold_b(i, b):
                ge(pe, b_loaded, i * 16)
                vt = raw_b[:, 0:256].rearrange("p (e h n) -> p e h n", e=2, h=2)
                wo = raw_b[:, 256:1280].rearrange("p (e h n) -> p e h n", e=2, h=2)

                def products(out):
                    for e in range(2):
                        for h in range(2):
                            mm = nc.tensor.matmul(out[64 * e:64 * e + 64, 0:C], vt[:, e, h, :], wo[:, e, h, :], start=h == 0, stop=h == 1)
                    return mm
                side(i, b, "B", products)

            def project(i, b, name, p, to_b):
                c = int(name[2])
                s = slice((2 * to_b + c) * CH, (2 * to_b + c + 1) * CH)
                q1h, q1l, q2, kv = (keep[n][:, s] for n in ("q1hi", "q1lo", "q2", "kv"))
                hi, lo = (lhi, llo) if name[:2] == "QL" else (rhi, rlo)
                if name[:2] == "KR":
                    passes = [(rhi[:, 256:384], kv), (rlo[:, 256:384], kv)]
                else:
                    passes = [(hi[:, 0:P], q1h), (hi[:, 0:P], q1l), (hi[:, P:2 * P], q2), (lo[:, P:2 * P], q2), (lo[:, 0:P], q1h)]
                if name == "QR0" and b != 0:
                    pe.wait_ge(a_split, p * 4 + 4)

                def products(out):
                    for n, (w, x) in enumerate(passes):
                        mm = nc.tensor.matmul(out[:, :], w, x, start=n == 0, stop=n == len(passes) - 1)
                    return mm
                side(i, b, name, products)

            def piece(s, n, b):
                e, t, k0, keys = PIECES[n]
                prologue = isinstance(s, int) and s == 0
                ge(pe, piece_max, n - len(ps_m5) + 1 if prologue else s * NP + n - 1)
                if n == 0:
                    pe.wait_ge(hi_done, s * 12 + 8 if not isinstance(s, int) or s else 6)
                if n == 8:
                    pe.wait_ge(hi_done, s * 12 + 12)
                out = ps_m5[n % len(ps_m5)] if prologue else ps_m[n % 2]
                diagonal = k0 + keys == (t + 1) * P
                mm = nc.tensor.matmul(out[:, 0:keys], qhi[b][e][:, t * P:(t + 1) * P], khi[b][e][:, k0:k0 + keys],
                                      start=True, stop=not diagonal)
                if diagonal:
                    mm = nc.tensor.matmul(out[:, keys - P:keys], mask16[:, :], ident16[:, :], start=False, stop=True)
                mm.then_inc(piece_ready, 1)

            def scores(s, b, k, e):
                c, j, off, diagonal = step_of(k)
                u = s * U + 2 * k + e
                started = not isinstance(s, int) or s > 0
                if k == 0 and e == 0 and not started:
                    pe.wait_ge(hi_done, 6)
                    pe.wait_ge(latent_lo, 2)
                    pe.wait_ge(rope_lo, 4)
                    pe.wait_ge(piece_max, NP)
                if k == (0 if started else TPC) and e == 0:
                    pe.wait_ge(rope_lo, s * 8 + 8)
                if k == 0:
                    pe.wait_ge(shift0_done, s * 8 + 8)
                if k == TPC:
                    pe.wait_ge(shift1_done, s * 8 + 8)
                ge(pe, exp_done, u - 2)
                out = ps_s[(2 * k + e) % 3]
                q = slice(c * CH + off, (c + 1) * CH)
                kk = slice(j * P, (j + 1) * P)
                nc.tensor.matmul(out[:, off:], ones16[:, :], shift[:, c, e, off:], start=True, stop=False)
                if diagonal:
                    nc.tensor.matmul(out[:, off:off + P], ident16[:, :], mask16[:, :], start=False, stop=False)
                nc.tensor.matmul(out[:, off:], khi[b][e][:, kk], qhi[b][e][:, q], start=False, stop=False)
                nc.tensor.matmul(out[:, off:], khi[b][e][:, kk], qlo[b][e][:, q], start=False, stop=False)
                nc.tensor.matmul(out[:, off:], klo[b][e][:, kk], qhi[b][e][:, q], start=False, stop=True).then_inc(scores_ready, 1)

            def values(s, b, k, alone=False):
                c, j, off, _ = step_of(k)
                last = k in (TPC - 1, STEPS - 1)
                if j == 0:
                    ge(pe, o_copied, s * 2 + c)
                for e in range(2):
                    if e or alone:
                        pe.wait_ge(exp_done, s * U + 2 * k + e + 1)
                    nc.tensor.matmul(ps_o[64 * e:64 * e + 64, off:], kvn[:, b * 8 + j, :], probs(k, e),
                                     start=j == 0, stop=last).then_inc(pv_done, 1)

            def turn_weights(chunks):
                pe.wait_ge(route_step, 2 * NT + 6)
                pe.wait_ge(piece_max, B * PAIRS * NP)
                for g in chunks:
                    ge(pe, w_rows, g - 1)
                    for j in range(TPC):
                        mm = nc.tensor.transpose(ps_m[g % 2][0:E, j * P:(j + 1) * P], w2[:, g * TPC + j, :], ident[:, :])
                    mm.then_inc(w_transposed, 1)

            def row_sums(i, b, name, s, c):
                for e in range(2):
                    pe.wait_ge(*sums(s, c, 7 if c else 3, e))

                def products(out):
                    for e in range(2):
                        mm = nc.tensor.matmul(out[64 * e:64 * e + 64, :], ones[:, 0:64], first[:, c, e, :], start=True, stop=True)
                    return mm
                side(i, b, name, products)

            def project_out(i, b, name, s, c, m):
                pe.wait_ge(b_split, i * 2 + 2 if name[1] != "p" or b else i * 2)
                pe.wait_ge(olo_done, s * 2 + c + 1)

                def products(out):
                    cols = slice(m * P, (m + 1) * P)
                    nc.tensor.matmul(out[:, :], bhi[:, cols], ohi[:, :], start=True, stop=False)
                    nc.tensor.matmul(out[:, :], bhi[:, cols], olo[:, :], start=False, stop=False)
                    return nc.tensor.matmul(out[:, :], blo[:, cols], ohi[:, :], start=False, stop=True)
                side(i, b, name, products)

            def body(i):
                for b in range(B):
                    s = i * 2 + b
                    earlier = b == 1 or not is_first(i)
                    p = i + 1 if b else i
                    for k in range(STEPS):
                        def side_work(half):
                            for name in SIDE.get((k, half), ()):
                                if is_last(i) and (name == "WA" or (b and name in PROLOGUE)):
                                    continue
                                if name in ("B", "WA"):
                                    if b == 0:
                                        fold_b(i, b) if name == "B" else fold_a(i, b, i + 1)
                                elif name == "Lp":
                                    if earlier:
                                        row_sums(i, b, name, s - 1, 1)
                                elif name == "L0":
                                    row_sums(i, b, name, s, 0)
                                elif name[:2] == "Yp":
                                    if earlier:
                                        project_out(i, b, name, s - 1, 1, int(name[2]))
                                elif name[0] == "Y":
                                    project_out(i, b, name, s, 0, int(name[1]))
                                else:
                                    project(i, b, name, p, 1 - b)

                        def maxima(slot):
                            if (k, slot) in PIECE_AT and not is_last(i, b):
                                piece(s + 1, PIECE_AT[k, slot], 1 - b)
                        scores(s, b, k, 0)
                        maxima(0)
                        side_work(0)
                        scores(s, b, k, 1)
                        maxima(1)
                        if k:
                            values(s, b, k - 1)
                        elif earlier:
                            values(s - 1, 1 - b, STEPS - 1)
                        maxima(2)
                        side_work(1)
                        maxima(3)
                        if is_last(i, b) and k in TURNS:
                            turn_weights(TURNS[k])

            for name in PROLOGUE:
                project(0, None, name, 0, 0)
            for n in range(NP):
                piece(0, n, 0)
            pairs_loop(pe, body)
            s = 2 * PAIRS - 1
            values(s, 1, STEPS - 1, alone=True)
            n = BEFORE_LAST + len(LAST)
            for e in range(2):
                pe.wait_ge(*sums(s, 1, 7, e))
            pe.wait_ge(y_added, s * 4 + 2)
            for e in range(2):
                mm = nc.tensor.matmul(ps_x[n % 2][64 * e:64 * e + 64, :], ones[:, 0:64], first[:, 1, e, :], start=True, stop=True)
            mm.then_inc(misc_ready, 1)
            pe.wait_ge(olo_done, 2 * s + 2)
            for m in range(2):
                out, cols = ps_x[(n + 1 + m) % 2], slice(m * P, (m + 1) * P)
                nc.tensor.matmul(out[:, :], bhi[:, cols], ohi[:, :], start=True, stop=False)
                nc.tensor.matmul(out[:, :], bhi[:, cols], olo[:, :], start=False, stop=False)
                nc.tensor.matmul(out[:, :], blo[:, cols], ohi[:, :], start=False, stop=True).then_inc(misc_ready, 1)

        @block.scalar
        def _(act):
            def exponent(s, k, e):
                c, j, off, _ = step_of(k)
                u = s * U + 2 * k + e
                act.wait_ge(scores_ready, u + 1)
                if j:
                    _, before = ring_of(k)
                    ge(act, pv_done, s * U + 2 * before + e + 1)
                    if before >= 0:
                        cb, jb, _, _ = step_of(before)
                        sb = s
                    else:
                        cb, jb, _, _ = step_of(before + STEPS)
                        sb = s - 1
                    ge(act, *sums(sb, cb, jb, e))
                nc.scalar.activation(probs(k, e), ps_s[(2 * k + e) % 3][:, off:], ACT.Exp, scale=SCALE).then_inc(exp_done, 1)

            def first_free(i, b, c):
                if c == 0:
                    if b == 1:
                        act.wait_ge(misc_ready, misc(i, 0, "L0")[0] + 1)
                    elif not is_first(i):
                        act.wait_ge(misc_ready, misc(i, 0, "QR0")[0] - 2)
                elif b == 1 or not is_first(i):
                    act.wait_ge(misc_ready, misc(i, b, "Lp")[0] + 1)

            def latent_hi(i, b, c, to_b):
                n, x = misc(i, b, f"QL{c}")
                act.wait_ge(misc_ready, n + 1)
                cs = slice(c * CH, (c + 1) * CH)
                nc.scalar.activation(qhi[to_b][1][0:64, cs], ps_x[x][0:64, :], ACT.Copy).then_inc(hi_done, 1)
                nc.scalar.activation(qhi[to_b][0][64:P, cs], ps_x[x][64:P, :], ACT.Copy).then_inc(hi_done, 1)

            def rope_hi(s, c, to_b):
                cs = slice(c * CH, (c + 1) * CH)
                for g, to in ((2 * c, qhi), (2 * c + 1, khi)):
                    act.wait_ge(rope_sum, s * 4 + g + 1)
                    nc.scalar.activation(to[to_b][0][0:64, cs], t1[0:64, g, :], ACT.Copy).then_inc(hi_done, 1)
                    nc.scalar.activation(to[to_b][1][64:P, cs], t1[64:P, g, :], ACT.Copy).then_inc(hi_done, 1)

            def shift_matrix(s, c, e):
                if c == 0:
                    act.wait_ge(piece_max, s * NP + 8)
                    ge(act, scores_ready, (s - 1) * U + 8)
                else:
                    act.wait_ge(halves_joined, s + 1)
                    ge(act, scores_ready, s * U)
                for t in range(TPC):
                    m = (nm1c if c else nm0)[:, e * TPC + t:e * TPC + t + 1]
                    nc.scalar.activation(shift[:, c, e, t * P:(t + 1) * P], ident[:, :], ACT.Copy, scale=m).then_inc(
                        shift1_done if c else shift0_done, 1)

            def copy_out(s, c):
                act.wait_ge(pv_done, s * U + (U if c else 8))
                ge(act, on_done, s * 2 + c)
                nc.scalar.activation(oe[:, :], ps_o[:, :], ACT.Copy).then_inc(o_copied, 1)

            def out_hi(s, c, last_y):
                act.wait_ge(on_done, s * 2 + c + 1)
                if last_y is not None:
                    act.wait_ge(misc_ready, last_y + 1)
                nc.scalar.activation(ohi[:, :], on[:, :], ACT.Copy).then_inc(ohi_done, 1)

            def body(i):
                for b in range(B):
                    s = i * 2 + b
                    earlier = b == 1 or not is_first(i)
                    for k in range(STEPS):
                        if k in (0, TPC):
                            first_free(i, b, k // TPC)
                        exponent(s, k, 0)
                        if k == 3 and not is_last(i, b):
                            latent_hi(i, b, 0, 1 - b)
                        exponent(s, k, 1)
                        if k == 0 and earlier:
                            copy_out(s - 1, 1)
                        if k in (1, 2):
                            shift_matrix(s, 1, k - 1)
                        if k == 3:
                            if not is_last(i, b):
                                latent_hi(i, b, 1, 1 - b)
                                rope_hi(s + 1, 0, 1 - b)
                        if k == 4:
                            copy_out(s, 0)
                            if earlier:
                                last = misc(i, 0, "Y1")[0] if b else misc(i, 0, "QR0")[0] - 1
                                out_hi(s - 1, 1, last)
                        if k == 5 and not is_last(i, b):
                            rope_hi(s + 1, 1, 1 - b)
                        if k == 7:
                            out_hi(s, 0, misc(i, b, "Yp1")[0] if earlier else None)
                        if k in (8, 9) and not is_last(i, b):
                            shift_matrix(s + 1, 0, k - 8)
                        if is_last(i, b) and k - 1 in TURNS:
                            for g in TURNS[k - 1]:
                                act.wait_ge(rope_lo, 8 * B * PAIRS)
                                act.wait_ge(w_transposed, g + 1)
                                nc.scalar.activation(wst[:, g * CH:(g + 1) * CH], ps_m[g % 2][0:E, :], ACT.Copy).then_inc(w_rows, 1)
                        if is_last(i, b) and k in (6, 7):
                            act.wait_ge(keep["xT_loaded"], 16)
                            nc.scalar.activation(keep["xhi"][k - 6][:, 0:ROUND], keep["xtf"][:, k - 6, :], ACT.Copy).then_inc(keep["x_hi"], 1)
                        if is_last(i, b) and k == 8:
                            act.wait_ge(keep["w_loaded"][0], 16)
                            nc.scalar.activation(keep["whi"][0], keep["raw"][0], ACT.Copy).then_inc(keep["expert_hi"], 1)
                        if k == 9 and b == 0 and not earlier:
                            act.wait_ge(route_step, NT + 1)
                            nc.scalar.activation(shifted[:, :, :], shifted[:, :, :], ACT.Exp).then_inc(route_exp, 1)

            for c in range(2):
                latent_hi(0, None, c, 0)
                rope_hi(0, c, 0)
            for e in range(2):
                shift_matrix(0, 0, e)
            pairs_loop(act, body)
            s = 2 * PAIRS - 1
            copy_out(s, 1)
            out_hi(s, 1, BEFORE_LAST + len(LAST) - 1)

        @block.vector
        def _(dve):
            def rope_products(i, b, name, g, s):
                n, x = misc(i, b, name)
                c = g // 2
                ge(dve, rope_lo, (s - 1) * 8 + 2 * g + 2)
                dve.wait_ge(misc_ready, n + 1)
                nc.vector.tensor_tensor(t1[:, g, :], ps_x[x][:, :], cosv[:, c * CH:(c + 1) * CH], ALU.mult).then_inc(rope_in, 1)
                nc.vector.stream_shuffle(sh[:, g, :], ps_x[x][:, :], PAIRSWAP).then_inc(rope_in, 1)

            def latent_low(i, b, c, s, to_b):
                _, x = misc(i, b, f"QL{c}")
                cs = slice(c * CH, (c + 1) * CH)
                dve.wait_ge(hi_done, s * 12 + (6 if b is None else 2) * c + 2)
                nc.vector.tensor_tensor(qlo[to_b][1][0:64, cs], ps_x[x][0:64, :], qhi[to_b][1][0:64, cs].bitcast(F32),
                                        ALU.subtract).then_inc(latent_lo, 1)
                nc.vector.tensor_tensor(qlo[to_b][0][64:P, cs], ps_x[x][64:P, :], qhi[to_b][0][64:P, cs].bitcast(F32),
                                        ALU.subtract).then_inc(latent_lo, 1)

            def split_a(i, b, p):
                n, x = misc(i, b, "WA")
                ge(dve, a_loaded, p * 16)
                nc.vector.tensor_copy(rhi[:, :], raw_a[:, 640:1024]).then_inc(a_split, 1)
                dve.wait_ge(misc_ready, n + 1)
                nc.vector.tensor_copy(lhi[:, :], ps_x[x][:, 0:256]).then_inc(a_split, 1)
                dve.wait_ge(a_split, p * 4 + 2)
                nc.vector.tensor_tensor(rlo[:, :], raw_a[:, 640:1024], rhi[:, :].bitcast(F32), ALU.subtract).then_inc(a_split, 1)
                nc.vector.tensor_tensor(llo[:, :], ps_x[x][:, 0:256], lhi[:, :].bitcast(F32), ALU.subtract).then_inc(a_split, 1)

            def split_b(i, b):
                n, x = misc(i, b, "B")
                dve.wait_ge(misc_ready, n + 1)
                nc.vector.tensor_copy(bhi[:, :], ps_x[x][:, 0:256]).then_inc(b_split, 1)
                dve.wait_ge(b_split, i * 2 + 1)
                nc.vector.tensor_tensor(blo[:, :], ps_x[x][:, 0:256], bhi[:, :].bitcast(F32), ALU.subtract).then_inc(b_split, 1)

            def join_halves(s):
                dve.wait_ge(piece_max, s * NP + NP)
                ge(dve, shift1_done, s * 8)
                nc.vector.tensor_tensor(nm1c[:, :], nm1[:, 0, :], nm1[:, 1, :], ALU.min).then_inc(halves_joined, 1)

            def maximum(s, n):
                e, t, k0, keys = PIECES[n]
                dve.wait_ge(piece_ready, s * NP + n + 1)
                if n == 0:
                    ge(dve, shift0_done, s * 8)
                if n == 8:
                    ge(dve, halves_joined, s)
                col = e * TPC + t % TPC
                to = nm0[:, col:col + 1] if t < TPC else nm1[:, int(k0 > 0), col:col + 1]
                bank = ps_m5[n % len(ps_m5)] if isinstance(s, int) and s == 0 else ps_m[n % 2]
                nc.vector.tensor_reduce(out=to, in_=bank[:, 0:keys], axis=AXX, op=ALU.max, negate=True).then_inc(piece_max, 1)

            def add_probs(s, k):
                c, j, off, _ = step_of(k)
                dve.wait_ge(exp_done, s * U + 2 * k + 1)
                if j == 1:
                    dve.wait_ge(pv_done, s * U + 2 * (k - 1) + 1)
                else:
                    dve.wait_ge(*sums(s, c, j - 1, 0))
                nc.vector.tensor_tensor(first[:, c, 0, off:], first[:, c, 0, off:], probs(k, 0), ALU.add).then_inc(sum_dve, 1)

            def normalise(n, x, s, c):
                dve.wait_ge(misc_ready, n + 1)
                ge(dve, on_done, s * 2 + c)
                nc.vector.reciprocal(rec[:, :], ps_x[x][:, :]).then_inc(rec_done, 1)
                dve.wait_ge(rec_done, s * 2 + c + 1)
                dve.wait_ge(o_copied, s * 2 + c + 1)
                ge(dve, olo_done, s * 2 + c)
                nc.vector.tensor_tensor(on[:, :], oe[:, :], rec[:, :], ALU.mult).then_inc(on_done, 1)

            def add_out(n, x, s, b, c, m):
                dve.wait_ge(misc_ready, n + 1)
                ge(dve, y_added, s * 4 + 2 * c + m - 4)
                at = slice(b * T + c * CH, b * T + (c + 1) * CH)
                nc.vector.tensor_tensor(yacc[:, m, at], yacc[:, m, at], ps_x[x][:, :], ALU.add).then_inc(y_added, 1)

            def rope(i, b, c, s):
                for g, name in ((2 * c, f"QR{c}"), (2 * c + 1, f"KR{c}")):
                    rope_products(i, b, name, g, s)

            def rotate_first():
                for g in range(2):
                    dve.wait_ge(rope_in, 2 * g + 2)
                    nc.vector.tensor_tensor(sh[:, g, :], sh[:, g, :], sinv[:, 0:CH], ALU.mult).then_inc(rope_sin, 1)
                for g in range(2):
                    dve.wait_ge(rope_sin, g + 1)
                    nc.vector.tensor_tensor(t1[:, g, :], t1[:, g, :], sh[:, g, :], ALU.add).then_inc(rope_sum, 1)

            def body(i):
                for b in range(B):
                    s = i * 2 + b
                    earlier = b == 1 or not is_first(i)
                    for k in range(STEPS):
                        if k == 0:
                            join_halves(s)
                        if k < 2 and not is_last(i, b):
                            rope(i, b, k, s + 1)
                        if k == 2 and earlier:
                            normalise(*misc(i, b, "Lp"), s - 1, 1)
                        if k in (3, 4) and not is_last(i, b):
                            latent_low(i, b, k - 3, s + 1, 1 - b)
                        if k == 7 and earlier:
                            add_out(*misc(i, b, "Yp1"), s - 1, 1 - b, 1, 1)
                        if k == 7 and b == 0:
                            split_b(i, b)
                        if k == 4 and b and is_first(i):
                            route_weights()
                        for slot in range(4):
                            if (k, slot) in PIECE_AT and not is_last(i, b):
                                maximum(s + 1, PIECE_AT[k, slot])
                            if slot == 2:
                                if k == 6 and earlier:
                                    add_out(*misc(i, b, "Yp0"), s - 1, 1 - b, 1, 0)
                                if k == 7 and b == 0 and not is_last(i):
                                    split_a(i, b, i + 1)
                            if k == 10 and slot in (0, 2):
                                add_out(*misc(i, b, f"Y{slot // 2}"), s, b, 0, slot // 2)
                        if k % TPC or k > TPC:
                            add_probs(s, k)
                        if k == 4:
                            normalise(*misc(i, b, "L0"), s, 0)
                        if k in (6, 7, 8) and b == 0 and is_first(i):
                            route_choice(k - 6)

            def route_choice(part):
                if part == 0:
                    for t in range(NT):
                        nc.vector.max(top[:, t, :], logits[:, t, :]).then_inc(route_step, 1)
                elif part == 1:
                    dve.wait_ge(route_step, NT)
                    nc.vector.tensor_tensor(shifted[:, :, :], logits[:, :, :], top[:, :, 0:1].broadcast_to([P, NT, E]),
                                            ALU.subtract).then_inc(route_step, 1)
                else:
                    for t in range(NT):
                        nc.vector.match_replace(rest[:, t, :], top[:, t, :], logits[:, t, :], MASKED * 64).then_inc(route_step, 1)

            def route_weights():
                dve.wait_ge(route_step, 2 * NT + 1)
                nc.vector.tensor_tensor(rest[:, :, :], rest[:, :, :], logits[:, :, :], ALU.not_equal).then_inc(route_step, 1)
                dve.wait_ge(route_step, 2 * NT + 2)
                dve.wait_ge(route_exp, 1)
                nc.vector.tensor_tensor(rest[:, :, :], rest[:, :, :], shifted[:, :, :], ALU.mult).then_inc(route_step, 1)
                dve.wait_ge(route_step, 2 * NT + 3)
                nc.vector.tensor_reduce(out=total[:, :], in_=rest[:, :, :], axis=AXX, op=ALU.add).then_inc(route_step, 1)
                dve.wait_ge(route_step, 2 * NT + 4)
                nc.vector.reciprocal(total[:, :], total[:, :]).then_inc(route_step, 1)
                dve.wait_ge(route_step, 2 * NT + 5)
                nc.vector.tensor_tensor(w2[:, :, :], rest[:, :, :], total[:, :].rearrange("p (n o) -> p n o", o=1).broadcast_to([P, NT, E]),
                                        ALU.mult).then_inc(route_step, 1)

            rope(0, None, 0, 0)
            rotate_first()
            latent_low(0, None, 0, 0, 0)
            rope(0, None, 1, 0)
            latent_low(0, None, 1, 0, 0)
            for n in range(NP):
                maximum(0, n)
            pairs_loop(dve, body)
            s = 2 * PAIRS - 1
            n = BEFORE_LAST + len(LAST)
            dve.wait_ge(keep["expert_hi"], 1)
            nc.vector.tensor_tensor(keep["wlo"][0], keep["raw"][0], keep["whi"][0].bitcast(F32), ALU.subtract).then_inc(keep["expert_lo"], 1)
            normalise(n, n % 2, s, 1)
            dve.wait_ge(ohi_done, s * 2 + 2)
            nc.vector.tensor_tensor(olo[:, :], on[:, :], ohi[:, :].bitcast(F32), ALU.subtract).then_inc(olo_done, 1)
            for m in range(2):
                add_out(n + 1 + m, (n + 1 + m) % 2, s, 1, 1, m)

        @block.gpsimd
        def _(pool):
            def rope_sum_of(s, g):
                c = g // 2
                pool.wait_ge(rope_in, s * 8 + 2 * g + 2)
                nc.gpsimd.tensor_tensor(sh[:, g, :], sh[:, g, :], sinv[:, c * CH:(c + 1) * CH], ALU.mult).then_inc(rope_sin, 1)
                pool.wait_ge(rope_sin, s * 4 + g + 1)
                nc.gpsimd.tensor_tensor(t1[:, g, :], t1[:, g, :], sh[:, g, :], ALU.add).then_inc(rope_sum, 1)

            def rope_low(s, g, to_b, before):
                c = g // 2
                cs = slice(c * CH, (c + 1) * CH)
                hi, lo = (khi, klo) if g % 2 else (qhi, qlo)
                pool.wait_ge(*before)
                pool.wait_ge(rope_sum, s * 4 + g + 1)
                if isinstance(s, int) and s == 0:
                    pool.wait_ge(hi_done, 2 * (c + 1) + 2 * (g + 1))
                else:
                    pool.wait_ge(hi_done, s * 12 + 4 + 2 * (g + 1))
                for e, rows in ((0, slice(0, 64)), (1, slice(64, P))):
                    ge(pool, rope_lo, s * 8 + 2 * g + e)
                    nc.gpsimd.tensor_tensor(lo[to_b][e][rows, cs], t1[rows, g, :], hi[to_b][e][rows, cs].bitcast(F32),
                                            ALU.subtract).then_inc(rope_lo, 1)
                pool.wait_ge(rope_lo, s * 8 + 2 * g + 2)

            def add_probs(s, k):
                c, j, off, _ = step_of(k)
                pool.wait_ge(exp_done, s * U + 2 * k + 2)
                if j == 1:
                    pool.wait_ge(pv_done, s * U + 2 * (k - 1) + 2)
                else:
                    pool.wait_ge(*sums(s, c, j - 1, 1))
                nc.gpsimd.tensor_tensor(first[:, c, 1, off:], first[:, c, 1, off:], probs(k, 1), ALU.add).then_inc(sum_pool, 1)

            def out_low(s, c):
                pool.wait_ge(ohi_done, s * 2 + c + 1)
                nc.gpsimd.tensor_tensor(olo[:, :], on[:, :], ohi[:, :].bitcast(F32), ALU.subtract).then_inc(olo_done, 1)

            def body(i):
                for b in range(B):
                    s = i * 2 + b
                    earlier = b == 1 or not is_first(i)
                    if not is_last(i, b):
                        rope_sum_of(s + 1, 0)
                        rope_sum_of(s + 1, 1)
                    for k in range(1, TPC):
                        add_probs(s, k)
                        if k < 3 and not is_last(i, b):
                            rope_sum_of(s + 1, k + 1)
                    if earlier:
                        out_low(s - 1, 1)
                    for k in range(TPC + 1, STEPS):
                        add_probs(s, k)
                        if k == 7:
                            out_low(s, 0)
                            before = (olo_done, s * 2 + 1)
                        else:
                            before = sums(s, 1, k - TPC, 1)
                        if is_last(i, b) and k in (8, 9):
                            pool.wait_ge(keep["x_hi"], k - 7)
                            nc.gpsimd.tensor_tensor(keep["xlo"][k - 8][:, 0:ROUND], keep["xtf"][:, k - 8, :],
                                                    keep["xhi"][k - 8][:, 0:ROUND].bitcast(F32), ALU.subtract).then_inc(keep["x_lo"], 1)
                        if k in (5, 6, 8, 9) and not is_last(i, b):
                            rope_low(s + 1, k - 5 if k < 7 else k - 6, 1 - b, before)

            for g in (2, 3):
                rope_sum_of(0, g)
            for g in range(4):
                rope_low(0, g, 0, (rope_sum, 4))
            pairs_loop(pool, body)




def mix(nc, d, keep, out):
    ctx = ExitStack()
    with ctx:
        yacc, w2, ident = keep["yacc"], keep["w2"], keep["ident"]
        xtf, xhi, xlo = (keep[name] for name in ("xtf", "xhi", "xlo"))
        raw, whi, wlo, routing = (list(keep[name]) for name in ("raw", "whi", "wlo", "routing"))
        for held, name, width, dt in ((raw, "raw", TW, F32), (whi, "whi", TW, F32R), (wlo, "wlo", TW, F32R),
                                      (routing, "routing", ROUND, F32)):
            for q in range(len(held), SLOTS):
                held.append(ctx.enter_context(nc.sbuf_tensor(f"{name}{q}", [P, width], dt))[:, :])
        xres, yout = tensors(nc, ctx, [
            ("xres", [P, NT, C], F32), ("yout", [P, NT, C], F32)])
        gs, hf, hh, hl = tensors(nc, ctx, [
            ("gs", [P, 2, CH], F32), ("hf", [P, 2, CH], F32), ("hh", [P, 2, CH], F32R), ("hl", [P, 2, CH], F32R)])
        bank = lambda name: ctx.enter_context(nc.psum_tensor(name, [P, CH], F32))
        ps_y = [[bank(f"ps_y{m}{c}") for c in range(UNITS)] for m in range(2)]
        ps_g, ps_u, ps_t = bank("ps_g"), bank("ps_u"), [bank(f"ps_tr{k}") for k in range(2)]
        sem = lambda name: ctx.enter_context(nc.semaphore(name))
        x_loaded, res_loaded, w_loaded = keep["xT_loaded"], sem("res_loaded"), keep["w_loaded"]
        routing_loaded = keep["routing_loaded"]
        x_hi, x_lo, expert_hi, expert_lo = (keep[n] for n in ("x_hi", "x_lo", "expert_hi", "expert_lo"))
        gate_ready, up_ready, silu_done, gated, h_done, h_hi, h_lo, down_done = (
            sem("gate_ready"), sem("up_ready"), sem("silu_done"), sem("gated"), sem("h_done"),
            sem("h_hi"), sem("h_lo"), sem("down_done"))
        y_summed, y_transposed, y_final, stored = sem("y_summed"), sem("y_transposed"), sem("y_final"), sem("stored")
        block = ctx.enter_context(nc.Block())
        UR = IT * UNITS
        ROUNDS = N // ROUND
        TR = ROUND // P
        xv = d["x"].rearrange("(n p) c -> p n c", p=P)
        ov = out.rearrange("(n p) c -> p n c", p=P)

        def tiles_loop(engine, body):
            body(0)
            with engine.Fori(1, IT // SLOTS) as i:
                body(i)

        @block.sync
        def _(sp):
            for q in range(2, SLOTS):
                sp.dma_start(raw[q], d["e"][q]).then_inc(w_loaded[q], 16)
            for q in range(1, SLOTS):
                load_routing(sp, d, routing[q], q, 0, routing_loaded[q])
            for r in range(ROUNDS):
                def body(i):
                    for q in range(SLOTS):
                        sp.wait_ge(expert_lo, i * SLOTS + (r * IT + q + 1))
                        sp.dma_start(raw[q], d["e"][i * SLOTS + (q + SLOTS)]).then_inc(w_loaded[q], 16)
                        if not isinstance(i, int) or r or q:
                            before = (q - 1) % SLOTS
                            sp.wait_ge(gated, i * (SLOTS * UNITS) + (r * UR + q * UNITS))
                            load_routing(sp, d, routing[before], before, i + (r * (IT // SLOTS) + (q > 0)), routing_loaded[before])
                    if isinstance(i, int) and r + 1 < ROUNDS:
                        sp.wait_ge(x_lo, 2 * (r + 1))
                        sp.dma_start(xtf[:, :, :], d["xT"][:, :, (r + 1) * ROUND:(r + 2) * ROUND]).then_inc(x_loaded, 16)
                        sp.dma_start(xres[:, :, :], xv).then_inc(res_loaded, 16)
                    if isinstance(i, int) and r:
                        sp.wait_ge(y_final, r * TR)
                        sp.dma_start(ov[:, (r - 1) * TR:r * TR, :], yout[:, (r - 1) * TR:r * TR, :]).then_inc(stored, 16)
                tiles_loop(sp, body)
            at = (ROUNDS - 1) * TR
            for half in range(2):
                tiles = slice(at + half * (TR // 2), at + (half + 1) * (TR // 2))
                sp.wait_ge(y_final, tiles.stop)
                sp.dma_start(ov[:, tiles, :], yout[:, tiles, :]).then_inc(stored, 16)
            sp.wait_ge(stored, 16 * (ROUNDS + 1))
            for q in range(SLOTS):
                sp.wait_ge(w_loaded[q], 16 * (1 + ROUNDS * (IT // SLOTS)))
                sp.wait_ge(routing_loaded[q], ROUTED * ((q < SLOTS - 1) + ROUNDS * (IT // SLOTS)))

        @block.tensor
        def _(pe):
            def down(r, i, q, c, first):
                pe.wait_ge(h_lo, i * (SLOTS * UNITS) + (r * UR + q * UNITS + c + 1))
                if first:
                    ge(pe, y_summed, (r - 1) * 4 + 2 * c + 2 if r else 0)
                for m in range(2):
                    cols = slice(DOWN_AT + m * P, DOWN_AT + (m + 1) * P)
                    nc.tensor.matmul(ps_y[m][c][:, :], whi[q][:, cols], hh[:, c, :], start=first, stop=False, skip_group_check=True)
                    nc.tensor.matmul(ps_y[m][c][:, :], whi[q][:, cols], hl[:, c, :], start=False, stop=False, skip_group_check=True)
                    mm = nc.tensor.matmul(ps_y[m][c][:, :], wlo[q][:, cols], hh[:, c, :], start=False, stop=True, skip_group_check=True)
                mm.then_inc(down_done, 1)

            def turn_back(r, c):
                pe.wait_ge(y_summed, r * 4 + 2 * c + 2)
                for t in range(c * TPC, (c + 1) * TPC):
                    ge(pe, y_final, r * TR + t - t % 2 - 2)
                    for m in range(2):
                        mm = nc.tensor.transpose(ps_t[t // 2 % 2][:, (t % 2) * C + m * P:(t % 2) * C + (m + 1) * P],
                                                 yacc[:, m, r * ROUND + t * P:r * ROUND + (t + 1) * P], ident[:, :])
                    mm.then_inc(y_transposed, 1)

            for r in range(ROUNDS):
                pe.wait_ge(x_lo, 2 * r + 2)

                def body(i):
                    for q in range(SLOTS):
                        for c in range(UNITS):
                            n = i * (SLOTS * UNITS) + (r * UR + q * UNITS + c)
                            tokens = slice((r * UNITS + c) * CH, (r * UNITS + c + 1) * CH)
                            if c == 0:
                                pe.wait_ge(expert_lo, i * SLOTS + (r * IT + q + 1))
                            ge(pe, silu_done, n)
                            for out_ps, w0, done in ((ps_g, 0, gate_ready), (ps_u, UP_AT, up_ready)):
                                if done is up_ready:
                                    ge(pe, h_done, n)
                                for k in range(2):
                                    cols = slice(w0 + k * P, w0 + (k + 1) * P)
                                    nc.tensor.matmul(out_ps[:, :], whi[q][:, cols], xhi[k][:, tokens], start=k == 0, stop=False)
                                    nc.tensor.matmul(out_ps[:, :], whi[q][:, cols], xlo[k][:, tokens], start=False, stop=False)
                                    mm = nc.tensor.matmul(out_ps[:, :], wlo[q][:, cols], xhi[k][:, tokens], start=False, stop=k == 1)
                                mm.then_inc(done, 1)
                            if c:
                                down(r, i, q, c - 1, isinstance(i, int) and q == 0)
                            elif q:
                                down(r, i, q - 1, UNITS - 1, isinstance(i, int) and q == 1)
                            elif not isinstance(i, int):
                                down(r, i - 1, SLOTS - 1, UNITS - 1, False)
                            elif r:
                                down(r - 1, IT // SLOTS - 1, SLOTS - 1, UNITS - 1, False)
                    if isinstance(i, int) and r:
                        for c in range(UNITS):
                            turn_back(r - 1, c)
                tiles_loop(pe, body)
            turn_back(ROUNDS - 1, 0)
            down(ROUNDS - 1, IT // SLOTS - 1, SLOTS - 1, UNITS - 1, False)
            turn_back(ROUNDS - 1, 1)

        @block.scalar
        def _(act):
            def split_x(r):
                act.wait_ge(x_loaded, 16 * (r + 1))
                for k in range(2):
                    nc.scalar.activation(xhi[k][:, r * ROUND:(r + 1) * ROUND], xtf[:, k, :], ACT.Copy).then_inc(x_hi, 1)

            def split_weights(turn, q, n):
                act.wait_ge(w_loaded[q], turn * 16 + 16)
                ge(act, down_done, n * UNITS - UNITS * (SLOTS - 1))
                nc.scalar.activation(whi[q], raw[q], ACT.Copy).then_inc(expert_hi, 1)

            for r in range(ROUNDS):
                def body(i):
                    for q in range(SLOTS):
                        for c in range(UNITS):
                            n = i * (SLOTS * UNITS) + (r * UR + q * UNITS + c)
                            act.wait_ge(gate_ready, n + 1)
                            ge(act, h_done, n - 1)
                            nc.scalar.activation(gs[:, c, :], ps_g[:, :], ACT.Silu).then_inc(silu_done, 1)
                            if c == 0:
                                split_weights(i + (r * (IT // SLOTS) + (q == SLOTS - 1)), (q + 1) % SLOTS, i * SLOTS + (r * IT + q + 1))
                            act.wait_ge(h_done, n + 1)
                            nc.scalar.activation(hh[:, c, :], hf[:, c, :], ACT.Copy).then_inc(h_hi, 1)
                    if isinstance(i, int) and r + 1 < ROUNDS:
                        split_x(r + 1)
                tiles_loop(act, body)

        @block.vector
        def _(dve):
            def split_x(r):
                for k in range(2):
                    dve.wait_ge(x_hi, 2 * r + k + 1)
                    at = slice(r * ROUND, (r + 1) * ROUND)
                    nc.vector.tensor_tensor(xlo[k][:, at], xtf[:, k, :], xhi[k][:, at].bitcast(F32), ALU.subtract).then_inc(x_lo, 1)

            def split_weights(q, n):
                dve.wait_ge(expert_hi, n + 1)
                nc.vector.tensor_tensor(wlo[q], raw[q], whi[q].bitcast(F32), ALU.subtract).then_inc(expert_lo, 1)

            def add_residual(r, c):
                dve.wait_ge(res_loaded, 16)
                for t in range(c * TPC, (c + 1) * TPC, 2):
                    dve.wait_ge(y_transposed, r * TR + t + 2)
                    for h in range(2):
                        n = r * TR + t + h
                        nc.vector.tensor_tensor(yout[:, n, :], xres[:, n, :], ps_t[t // 2 % 2][:, h * C:(h + 1) * C], ALU.add).then_inc(y_final, 1)

            for r in range(ROUNDS):
                def body(i):
                    for q in range(SLOTS):
                        for c in range(UNITS):
                            n = i * (SLOTS * UNITS) + (r * UR + q * UNITS + c)
                            dve.wait_ge(silu_done, n + 1)
                            dve.wait_ge(routing_loaded[q], i * ROUTED + (r * (IT // SLOTS) + 1) * ROUTED)
                            nc.vector.tensor_tensor(gs[:, c, :], gs[:, c, :], routing[q][:, c * CH:(c + 1) * CH], ALU.mult).then_inc(gated, 1)
                            dve.wait_ge(gated, n + 1)
                            dve.wait_ge(up_ready, n + 1)
                            ge(dve, h_lo, n - 1)
                            nc.vector.tensor_tensor(hf[:, c, :], gs[:, c, :], ps_u[:, :], ALU.mult).then_inc(h_done, 1)
                            if c == 0:
                                split_weights((q + 1) % SLOTS, i * SLOTS + (r * IT + q + 1))
                    if isinstance(i, int) and r + 1 < ROUNDS:
                        split_x(r + 1)
                    if isinstance(i, int) and r:
                        for c in range(UNITS):
                            add_residual(r - 1, c)
                tiles_loop(dve, body)
                for c in range(UNITS):
                    dve.wait_ge(down_done, (r + 1) * UR - (UNITS - 1 - c))
                    for m in range(2):
                        at = slice(r * ROUND + c * CH, r * ROUND + (c + 1) * CH)
                        nc.vector.tensor_tensor(yacc[:, m, at], yacc[:, m, at], ps_y[m][c][:, :], ALU.add).then_inc(y_summed, 1)
                    if r == ROUNDS - 1:
                        add_residual(r, c)

        @block.gpsimd
        def _(pool):
            for r in range(ROUNDS):
                def body(i):
                    for q in range(SLOTS):
                        for c in range(UNITS):
                            n = i * (SLOTS * UNITS) + (r * UR + q * UNITS + c)
                            pool.wait_ge(h_hi, n + 1)
                            ge(pool, down_done, n - 1)
                            nc.gpsimd.tensor_tensor(hl[:, c, :], hf[:, c, :], hh[:, c, :].bitcast(F32), ALU.subtract).then_inc(h_lo, 1)
                tiles_loop(pool, body)


def build(nc, d, out):
    ctx = ExitStack()
    with ctx:
        keep = {}
        for name, shape, dt in (("ident", [P, P], F32), ("w2", [P, NT, E], F32), ("yacc", [P, 2, N], F32),
                                ("q1hi", [P, N], F32R), ("q1lo", [P, N], F32R), ("q2", [P, N], F32R), ("kv", [P, N], F32R),
                                ("keys0", [P, 4, T], F32R), ("xtf", [P, 2, ROUND], F32),
                                ("cosv", [P, T], F32), ("sinv", [P, T], F32), ("raw_a", [P, 1024], F32)):
            keep[name] = ctx.enter_context(nc.sbuf_tensor(name, shape, dt))
        keep["xhi"], keep["xlo"] = (keep["q1hi"], keep["q1lo"]), (keep["q2"], keep["kv"])
        keep["routing"] = [keep["sinv"][:, 0:ROUND]]
        keep["raw"] = [keep[name][:, 0:TW] for name in ("raw_a", "cosv")]
        keep["whi"], keep["wlo"] = [keep["keys0"][:, 2, 0:TW]], [keep["keys0"][:, 3, 0:TW]]
        assert T >= TW and T >= ROUND
        for name in ("xT_loaded", "x_hi", "x_lo", "expert_hi", "expert_lo"):
            keep[name] = ctx.enter_context(nc.semaphore(name))
        keep["routing_loaded"] = [ctx.enter_context(nc.semaphore(f"routing_loaded{q}")) for q in range(SLOTS)]
        keep["w_loaded"] = [ctx.enter_context(nc.semaphore(f"w_loaded{q}")) for q in range(SLOTS)]
        with ExitStack() as inner:
            for name, shape, dt in (("kvn", [P, NT, KVR], F32), ("logits", [P, NT, E], F32),
                                    ("ones", [P, P], F32), ("raw_mask", [P, P], F32), ("raw_b", [96, 1280], F32),
                                    ("ident16", [P, P], BF16), ("ones16", [P, P], BF16), ("mask16", [P, P], BF16),
                                    ("rhi", [P, 384], F32R), ("rlo", [P, 384], F32R), ("lhi", [P, 256], F32R), ("llo", [P, 256], F32R)):
                keep[name] = inner.enter_context(nc.sbuf_tensor(name, shape, dt))
            for w in ("khi", "klo"):
                keep[w] = [[keep["keys0"][:, 2 * (w == "klo") + e, :] for e in range(2)]]
                keep[w] += [[inner.enter_context(nc.sbuf_tensor(f"{w}{b}{e}", [P, T], F32R)) for e in range(2)] for b in range(1, B)]
            keep["a_split"] = inner.enter_context(nc.semaphore("a_split"))
            prepare(nc, d, keep)
            attend(nc, d, keep)
        mix(nc, d, keep, out)


def laid_out(inputs):
    g = {k: np.asarray(v) for k, v in inputs.items()}
    wqd, wkvd = g["L0_attn_wq_down"], g["L0_attn_wkv_down"]
    wl = np.concatenate([wqd, wqd[:, P:], wkvd, wkvd], axis=1)
    wkg = np.concatenate([wkvd, g["L0_ffn_gate_w"].T], axis=1)
    rows = lambda w: np.ascontiguousarray(w.reshape(2, P, -1).transpose(1, 0, 2))
    wqn, wkn = g["L0_attn_wq_nope"], g["L0_attn_wk_nope"]
    wqr, wkr = g["L0_attn_wq_rope"], g["L0_attn_wk_rope"]
    wvu, wo = g["L0_attn_wv_up"], g["L0_attn_wo"]
    a = np.zeros((PAIRS, P, 1024), np.float32)
    b = np.zeros((PAIRS, 96, 1280), np.float32)
    for p in range(PAIRS):
        for e in range(2):
            h = 2 * p + e
            q = wqn[:, h * DN:(h + 1) * DN].T
            a[p, :, 256 * e:256 * e + 192] = q
            a[p, :, 256 * e + 192:256 * e + 256] = q[:, P:]
            a[p, :, 512 + 64 * e:576 + 64 * e] = wkn[:, h * DN:(h + 1) * DN].T
            for half in range(2):
                r = slice(h * D + 96 * half, h * D + 96 * half + 96)
                b[p, :, 128 * e + 64 * half:128 * e + 64 * half + 64] = wvu[:, r].T
                b[p, :, 256 + 512 * e + 256 * half:512 + 512 * e + 256 * half] = wo[r, :]
        r = slice(p * P, (p + 1) * P)
        a[p, :, 640:768] = wqr[0:P, r]
        for k in range(2):
            a[p, 64 * k:64 * k + 64, 768:896] = wqr[P:, r]
            a[p, 64 * k:64 * k + 64, 896:1024] = wkr[:, r]
    turned = lambda w: w.reshape(IT, P, 2, P).transpose(0, 3, 2, 1).reshape(IT, P, 2 * P)
    wd = g["L0_ffn_w_down_proj"].transpose(0, 2, 1).reshape(IT, P, C)
    e = np.concatenate([turned(g["L0_ffn_w_gate_proj"]), turned(g["L0_ffn_w_up_proj"]), wd], axis=2)
    e = np.concatenate([e, e[:SLOTS]], axis=0)
    inv_freq = (1.0 / np.float32(10000.0) ** (np.arange(0, DR, 2, dtype=np.float32) / np.float32(DR))).astype(np.float32)
    freqs = np.outer(inv_freq, np.arange(T, dtype=np.float32)).astype(np.float32)
    pair_rows = np.tile(np.repeat(np.arange(DR // 2), 2), 2)
    cos = np.cos(freqs).astype(np.float32)[pair_rows]
    sin = np.sin(freqs).astype(np.float32)[pair_rows] * np.where(np.arange(P) % 2, 1, -1).astype(np.float32)[:, None]
    mask = np.where(np.arange(P)[:, None] > np.arange(P)[None, :], MASKED, 0.0).astype(np.float32)
    return {
        "x": np.ascontiguousarray(g["L0_attn_x"].reshape(N, C)), "wl": rows(wl), "wkg": rows(wkg), "a": a, "b": b,
        "e": np.ascontiguousarray(e), "cos": np.ascontiguousarray(cos), "sin": np.ascontiguousarray(sin),
        "ident": np.eye(P, dtype=np.float32), "ones": np.ones((P, P), np.float32), "mask": mask,
    }


def kernel(**inputs):
    import concourse.bacc as bacc
    from concourse.bass_utils import run_bass_kernel_spmd
    nc = bacc.Bacc("TRN2", target_bir_lowering=False, num_devices=1)
    arrays = {f"in_{k}": v for k, v in laid_out(inputs).items()}
    d = {k[3:]: nc.dram_tensor(k, v.shape, mybir.dt.from_np(v.dtype), kind="ExternalInput").ap() for k, v in arrays.items()}
    d["xT"] = nc.dram_tensor("xT_scratch", [P, 2, N], F32, kind="Internal").ap()
    d["wT"] = nc.dram_tensor("wT_scratch", [N // ROUND * E + TURN_EXPERTS, ROUND], F32, kind="Internal").ap()
    out = nc.dram_tensor("out_0", [N, C], F32, kind="ExternalOutput").ap()
    build(nc, d, out)
    r = run_bass_kernel_spmd(nc, [arrays], core_ids=[0])
    return r.results[0]["out_0"].reshape(B, T, C)
```
